# Optimizing a Trainium2 kernel written in Bass

```python
import numpy as np
import jax
import jax.numpy as jnp

def _softmax(x, axis=-1):
    return jax.nn.softmax(x, axis=axis)

def _gelu(x):
    return jax.nn.gelu(x, approximate=True)

def _silu(x):
    return jax.nn.silu(x)

def _sigmoid(x):
    return jax.nn.sigmoid(x)

def _layernorm(x, axis=-1, eps=1e-05):
    m = jnp.mean(x, axis=axis, keepdims=True)
    v = jnp.var(x, axis=axis, keepdims=True)
    return (x - m) / jnp.sqrt(v + eps)

def _scatter_add(tgt, idx, src, axis=0):
    return tgt.at[idx].add(src)

def _segment_sum(src, seg, n):
    return jax.ops.segment_sum(src, seg, n)
kernel_name = 'mk_adaln_d2_jaxref_r8_de5c29'

def setup_inputs(seed: int=0):
    np.random.seed(seed)
    _w = jnp.asarray

    def _L0_attn_setup():
        import jax, jax.numpy as jnp
        import numpy as np
        D_MODEL = 128
        N_HEADS = 16
        HEAD_DIM = D_MODEL // N_HEADS
        ROPE_BASE = 10000.0

        def _rope(q, k):
            S, Dh = (q.shape[1], q.shape[-1])
            inv_freq = 1.0 / ROPE_BASE ** (jnp.arange(0, Dh, 2, dtype=jnp.float32) / Dh)
            t = jnp.arange(S, dtype=jnp.float32)
            freqs = jnp.outer(t, inv_freq)
            emb = jnp.concatenate([freqs, freqs], axis=-1)
            cos = jnp.cos(emb)[None, :, None, :]
            sin = jnp.sin(emb)[None, :, None, :]

            def rotate_half(v):
                v1, v2 = (v[..., :Dh // 2], v[..., Dh // 2:])
                return jnp.concatenate([-v2, v1], axis=-1)
            return (q * cos + rotate_half(q) * sin, k * cos + rotate_half(k) * sin)
        key = jax.random.key(seed)
        ks = jax.random.split(key, 5)
        B, S = (1, 512)
        scale = 1.0 / np.sqrt(D_MODEL)
        x = jax.random.normal(ks[0], (B, S, D_MODEL), dtype=jnp.float32)
        Wq = jax.random.normal(ks[1], (D_MODEL, D_MODEL), dtype=jnp.float32) * scale
        Wk = jax.random.normal(ks[2], (D_MODEL, D_MODEL), dtype=jnp.float32) * scale
        Wv = jax.random.normal(ks[3], (D_MODEL, D_MODEL), dtype=jnp.float32) * scale
        Wo = jax.random.normal(ks[4], (D_MODEL, D_MODEL), dtype=jnp.float32) * scale
        return {'x': x, 'Wq': Wq, 'Wk': Wk, 'Wv': Wv, 'Wo': Wo}
    _L0_attn_in = _L0_attn_setup()

    def _L0_ffn_setup():
        import jax, jax.numpy as jnp
        import numpy as np
        D = 128
        H = 16
        HD = D // H
        L = 64
        E = 8
        B, T = (4, 256)
        EPS = 1e-06

        def _glorot(k, shape):
            fan_in, fan_out = (shape[-2], shape[-1])
            lim = np.sqrt(6.0 / (fan_in + fan_out)).astype(np.float32)
            return jax.random.uniform(k, shape, jnp.float32, -lim, lim)

        def _rmsnorm(x, gamma):
            return gamma * x * jax.lax.rsqrt(jnp.mean(x * x, axis=-1, keepdims=True) + EPS)
        key = jax.random.key(seed)
        ks = jax.random.split(key, 8)
        return {'x': jax.random.normal(ks[0], (B, T, D), jnp.float32), 'gamma1': jnp.ones((D,), jnp.float32), 'Wq': _glorot(ks[1], (D, D)), 'bq': jnp.zeros((D,), jnp.float32), 'Wdown': _glorot(ks[2], (D, L)), 'bdown': jnp.zeros((L,), jnp.float32), 'Wup': _glorot(ks[3], (L, 2 * D)), 'bup': jnp.zeros((2 * D,), jnp.float32), 'Wo': _glorot(ks[4], (D, D)), 'bo': jnp.zeros((D,), jnp.float32), 'gamma2': jnp.ones((D,), jnp.float32), 'Wg': _glorot(ks[5], (D, E)), 'bg': jnp.zeros((E,), jnp.float32), 'We': _glorot(ks[6], (E, D, D))}
    _L0_ffn_in = _L0_ffn_setup()
    _L0_c = _w((lambda *s: np.random.randn(*s).astype(np.float32) * 0.05)(2, 128))
    _L0_wmod = _w((lambda *s: np.random.randn(*s).astype(np.float32) * 0.05)(128, 6 * 128) * 128 ** (-0.5))

    def _L1_attn_setup():
        import jax, jax.numpy as jnp
        import numpy as np
        B, T, D, H = (2, 256, 128, 16)
        HD = D // H
        key = jax.random.key(seed)
        ks = jax.random.split(key, 9)
        w = lambda k, shp: jax.random.normal(k, shp, jnp.float32) * 0.02
        return {'x': jax.random.normal(ks[0], (B, T, D), jnp.float32), 'Wq': w(ks[1], (D, D)), 'bq': jnp.zeros((D,), jnp.float32), 'Wk': w(ks[2], (D, D)), 'bk': jnp.zeros((D,), jnp.float32), 'Wv': w(ks[3], (D, D)), 'bv': jnp.zeros((D,), jnp.float32), 'Wo': w(ks[4], (D, D)), 'bo': jnp.zeros((D,), jnp.float32), 'Wqs': w(ks[5], (3, HD)), 'bqs': jnp.zeros((3,), jnp.float32), 'Wks': w(ks[6], (3, HD)), 'bks': jnp.zeros((3,), jnp.float32), 'Wvs': w(ks[7], (3, HD)), 'bvs': jnp.zeros((3,), jnp.float32), 'temp': jnp.float32(1.0)}
    _L1_attn_in = _L1_attn_setup()

    def _L1_ffn_setup():
        import jax, jax.numpy as jnp
        import numpy as np
        B, S, H, F, E, R, TOPK = (4, 256, 128, 512, 4, 4, 2)

        def _more_forward(x, Wg, bg, W1, b1, W2, b2):
            b, s, h = x.shape
            cur = x
            for r in range(R):
                flat = cur.reshape(-1, h)
                logits = flat @ Wg[r] + bg[r]
                vals, idx = jax.lax.top_k(logits, TOPK)
                w = jax.nn.softmax(vals, axis=-1)
                cw = jnp.sum(jax.nn.one_hot(idx, E, dtype=flat.dtype) * w[..., None], axis=1)
                hmid = jax.nn.gelu(jnp.einsum('nh,ehf->enf', flat, W1) + b1[:, None, :])
                y = jnp.einsum('enf,efh->enh', hmid, W2) + b2[:, None, :]
                out = jnp.einsum('ne,enh->nh', cw, y)
                cur = cur + out.reshape(b, s, h)
            return cur
        key = jax.random.key(seed)
        ks = jax.random.split(key, 8)
        scale = 0.02
        return {'x': jax.random.normal(ks[0], (B, S, H), dtype=jnp.float32), 'Wg': jax.random.normal(ks[1], (R, H, E), dtype=jnp.float32) * scale, 'bg': jnp.zeros((R, E), dtype=jnp.float32), 'W1': jax.random.normal(ks[2], (E, H, F), dtype=jnp.float32) * scale, 'b1': jnp.zeros((E, F), dtype=jnp.float32), 'W2': jax.random.normal(ks[3], (E, F, H), dtype=jnp.float32) * scale, 'b2': jnp.zeros((E, H), dtype=jnp.float32)}
    _L1_ffn_in = _L1_ffn_setup()
    _L1_c = _w((lambda *s: np.random.randn(*s).astype(np.float32) * 0.05)(2, 128))
    _L1_wmod = _w((lambda *s: np.random.randn(*s).astype(np.float32) * 0.05)(128, 6 * 128) * 128 ** (-0.5))
    _d = {'L0_attn_x': _L0_attn_in['x'], 'L0_attn_Wq': _L0_attn_in['Wq'], 'L0_attn_Wk': _L0_attn_in['Wk'], 'L0_attn_Wv': _L0_attn_in['Wv'], 'L0_attn_Wo': _L0_attn_in['Wo'], 'L0_ffn_gamma1': _L0_ffn_in['gamma1'], 'L0_ffn_Wq': _L0_ffn_in['Wq'], 'L0_ffn_bq': _L0_ffn_in['bq'], 'L0_ffn_Wdown': _L0_ffn_in['Wdown'], 'L0_ffn_bdown': _L0_ffn_in['bdown'], 'L0_ffn_Wup': _L0_ffn_in['Wup'], 'L0_ffn_bup': _L0_ffn_in['bup'], 'L0_ffn_Wo': _L0_ffn_in['Wo'], 'L0_ffn_bo': _L0_ffn_in['bo'], 'L0_ffn_gamma2': _L0_ffn_in['gamma2'], 'L0_ffn_Wg': _L0_ffn_in['Wg'], 'L0_ffn_bg': _L0_ffn_in['bg'], 'L0_ffn_We': _L0_ffn_in['We'], 'L0_c': _L0_c, 'L0_wmod': _L0_wmod, 'L1_attn_Wq': _L1_attn_in['Wq'], 'L1_attn_bq': _L1_attn_in['bq'], 'L1_attn_Wk': _L1_attn_in['Wk'], 'L1_attn_bk': _L1_attn_in['bk'], 'L1_attn_Wv': _L1_attn_in['Wv'], 'L1_attn_bv': _L1_attn_in['bv'], 'L1_attn_Wo': _L1_attn_in['Wo'], 'L1_attn_bo': _L1_attn_in['bo'], 'L1_attn_Wqs': _L1_attn_in['Wqs'], 'L1_attn_bqs': _L1_attn_in['bqs'], 'L1_attn_Wks': _L1_attn_in['Wks'], 'L1_attn_bks': _L1_attn_in['bks'], 'L1_attn_Wvs': _L1_attn_in['Wvs'], 'L1_attn_bvs': _L1_attn_in['bvs'], 'L1_attn_temp': _L1_attn_in['temp'], 'L1_ffn_Wg': _L1_ffn_in['Wg'], 'L1_ffn_bg': _L1_ffn_in['bg'], 'L1_ffn_W1': _L1_ffn_in['W1'], 'L1_ffn_b1': _L1_ffn_in['b1'], 'L1_ffn_W2': _L1_ffn_in['W2'], 'L1_ffn_b2': _L1_ffn_in['b2'], 'L1_c': _L1_c, 'L1_wmod': _L1_wmod}
    _x0 = _d['L0_attn_x']
    _d['L0_attn_x'] = jax.random.normal(jax.random.fold_in(jax.random.key(seed), 1), (2, 1024, 128), dtype=_x0.dtype)
    del _x0
    return _d

def reference(L0_attn_x, L0_attn_Wq, L0_attn_Wk, L0_attn_Wv, L0_attn_Wo, L0_ffn_gamma1, L0_ffn_Wq, L0_ffn_bq, L0_ffn_Wdown, L0_ffn_bdown, L0_ffn_Wup, L0_ffn_bup, L0_ffn_Wo, L0_ffn_bo, L0_ffn_gamma2, L0_ffn_Wg, L0_ffn_bg, L0_ffn_We, L0_c, L0_wmod, L1_attn_Wq, L1_attn_bq, L1_attn_Wk, L1_attn_bk, L1_attn_Wv, L1_attn_bv, L1_attn_Wo, L1_attn_bo, L1_attn_Wqs, L1_attn_bqs, L1_attn_Wks, L1_attn_bks, L1_attn_Wvs, L1_attn_bvs, L1_attn_temp, L1_ffn_Wg, L1_ffn_bg, L1_ffn_W1, L1_ffn_b1, L1_ffn_W2, L1_ffn_b2, L1_c, L1_wmod):

    def _L0_attn_ref(x, Wq, Wk, Wv, Wo):
        import jax, jax.numpy as jnp
        import numpy as np
        D_MODEL = 128
        N_HEADS = 16
        HEAD_DIM = D_MODEL // N_HEADS
        ROPE_BASE = 10000.0

        def _rope(q, k):
            S, Dh = (q.shape[1], q.shape[-1])
            inv_freq = 1.0 / ROPE_BASE ** (jnp.arange(0, Dh, 2, dtype=jnp.float32) / Dh)
            t = jnp.arange(S, dtype=jnp.float32)
            freqs = jnp.outer(t, inv_freq)
            emb = jnp.concatenate([freqs, freqs], axis=-1)
            cos = jnp.cos(emb)[None, :, None, :]
            sin = jnp.sin(emb)[None, :, None, :]

            def rotate_half(v):
                v1, v2 = (v[..., :Dh // 2], v[..., Dh // 2:])
                return jnp.concatenate([-v2, v1], axis=-1)
            return (q * cos + rotate_half(q) * sin, k * cos + rotate_half(k) * sin)
        B, S, _ = x.shape
        H, Dh = (N_HEADS, HEAD_DIM)
        q = (x @ Wq.T).reshape(B, S, H, Dh)
        k = (x @ Wk.T).reshape(B, S, H, Dh)
        v = (x @ Wv.T).reshape(B, S, H, Dh)
        q, k = _rope(q, k)
        scale = 1.0 / np.sqrt(Dh)
        scores = jnp.einsum('bqhd,bkhd->bhqk', q, k) * scale
        causal = jnp.triu(jnp.ones((S, S), dtype=bool), k=1)
        scores = jnp.where(causal, -jnp.inf, scores)
        attn = jax.nn.softmax(scores, axis=-1)
        out = jnp.einsum('bhqk,bkhd->bqhd', attn, v).reshape(B, S, H * Dh)
        return out @ Wo.T

    def _L0_ffn_ref(x, gamma1, Wq, bq, Wdown, bdown, Wup, bup, Wo, bo, gamma2, Wg, bg, We):
        import jax, jax.numpy as jnp
        import numpy as np
        D = 128
        H = 16
        HD = D // H
        L = 64
        E = 8
        B, T = (4, 256)
        EPS = 1e-06

        def _glorot(k, shape):
            fan_in, fan_out = (shape[-2], shape[-1])
            lim = np.sqrt(6.0 / (fan_in + fan_out)).astype(np.float32)
            return jax.random.uniform(k, shape, jnp.float32, -lim, lim)

        def _rmsnorm(x, gamma):
            return gamma * x * jax.lax.rsqrt(jnp.mean(x * x, axis=-1, keepdims=True) + EPS)
        b, t = (x.shape[0], x.shape[1])
        h = _rmsnorm(x, gamma1)
        q = (h @ Wq + bq).reshape(b, t, H, HD)
        kv = ((h @ Wdown + bdown) @ Wup + bup).reshape(b, t, H, 2 * HD)
        k, v = jnp.split(kv, 2, axis=-1)
        att = jnp.einsum('bthd,btgd->bthg', q, k) / np.sqrt(HD).astype(np.float32)
        att = jax.nn.softmax(att, axis=-1)
        out = jnp.einsum('bthg,btgd->bthd', att, v).reshape(b, t, D)
        x = x + (out @ Wo + bo)
        h2 = _rmsnorm(x, gamma2)
        gate = jax.nn.softmax(h2 @ Wg + bg, axis=-1)
        combined = jnp.einsum('btd,edf,bte->btf', h2, We, gate)
        return x + combined

    def _L1_attn_ref(x, Wq, bq, Wk, bk, Wv, bv, Wo, bo, Wqs, bqs, Wks, bks, Wvs, bvs, temp):
        import jax, jax.numpy as jnp
        import numpy as np
        B, T, D, H = (2, 256, 128, 16)
        HD = D // H
        Bx, Tx, Dx = x.shape
        split = lambda y: y.reshape(Bx, Tx, H, HD).transpose(0, 2, 1, 3)
        q = split(x @ Wq.T + bq)
        k = split(x @ Wk.T + bk)
        v = split(x @ Wv.T + bv)
        q_stp = q @ Wqs.T + bqs
        k3 = k @ Wks.T + bks
        v3 = v @ Wvs.T + bvs
        cross_kv = jnp.cross(k3, v3, axis=-1)
        scores = (jnp.einsum('bhqd,bhkd->bhqk', q, k) + jnp.einsum('bhqc,bhkc->bhqk', q_stp, cross_kv)) * temp
        attn = jax.nn.softmax(scores, axis=-1)
        out = jnp.einsum('bhqk,bhkd->bhqd', attn, v)
        out = out.transpose(0, 2, 1, 3).reshape(Bx, Tx, Dx)
        return out @ Wo.T + bo

    def _L1_ffn_ref(x, Wg, bg, W1, b1, W2, b2):
        import jax, jax.numpy as jnp
        import numpy as np
        B, S, H, F, E, R, TOPK = (4, 256, 128, 512, 4, 4, 2)

        def _more_forward(x, Wg, bg, W1, b1, W2, b2):
            b, s, h = x.shape
            cur = x
            for r in range(R):
                flat = cur.reshape(-1, h)
                logits = flat @ Wg[r] + bg[r]
                vals, idx = jax.lax.top_k(logits, TOPK)
                w = jax.nn.softmax(vals, axis=-1)
                cw = jnp.sum(jax.nn.one_hot(idx, E, dtype=flat.dtype) * w[..., None], axis=1)
                hmid = jax.nn.gelu(jnp.einsum('nh,ehf->enf', flat, W1) + b1[:, None, :])
                y = jnp.einsum('enf,efh->enh', hmid, W2) + b2[:, None, :]
                out = jnp.einsum('ne,enh->nh', cw, y)
                cur = cur + out.reshape(b, s, h)
            return cur
        return _more_forward(x, Wg, bg, W1, b1, W2, b2)
    x = L0_attn_x
    mod = (_silu(L0_c) @ L0_wmod).reshape(L0_c.shape[0], 6, 1, -1)
    sa, ca, ga, sb, cb, gb = (mod[:, 0], mod[:, 1], mod[:, 2], mod[:, 3], mod[:, 4], mod[:, 5])
    ga = (2 * (ga >= 0) - 1) * jnp.maximum(jnp.abs(ga), 0.25)
    gb = (2 * (gb >= 0) - 1) * jnp.maximum(jnp.abs(gb), 0.25)
    h = _layernorm(x, axis=-1) * (1 + ca) + sa
    x = x + ga * _L0_attn_ref(h, L0_attn_Wq, L0_attn_Wk, L0_attn_Wv, L0_attn_Wo)
    h = _layernorm(x, axis=-1) * (1 + cb) + sb
    x = x + gb * _L0_ffn_ref(h, L0_ffn_gamma1, L0_ffn_Wq, L0_ffn_bq, L0_ffn_Wdown, L0_ffn_bdown, L0_ffn_Wup, L0_ffn_bup, L0_ffn_Wo, L0_ffn_bo, L0_ffn_gamma2, L0_ffn_Wg, L0_ffn_bg, L0_ffn_We)
    mod = (_silu(L1_c) @ L1_wmod).reshape(L1_c.shape[0], 6, 1, -1)
    sa, ca, ga, sb, cb, gb = (mod[:, 0], mod[:, 1], mod[:, 2], mod[:, 3], mod[:, 4], mod[:, 5])
    ga = (2 * (ga >= 0) - 1) * jnp.maximum(jnp.abs(ga), 0.25)
    gb = (2 * (gb >= 0) - 1) * jnp.maximum(jnp.abs(gb), 0.25)
    h = _layernorm(x, axis=-1) * (1 + ca) + sa
    x = x + ga * _L1_attn_ref(h, L1_attn_Wq, L1_attn_bq, L1_attn_Wk, L1_attn_bk, L1_attn_Wv, L1_attn_bv, L1_attn_Wo, L1_attn_bo, L1_attn_Wqs, L1_attn_bqs, L1_attn_Wks, L1_attn_bks, L1_attn_Wvs, L1_attn_bvs, L1_attn_temp)
    h = _layernorm(x, axis=-1) * (1 + cb) + sb
    x = x + gb * _L1_ffn_ref(h, L1_ffn_Wg, L1_ffn_bg, L1_ffn_W1, L1_ffn_b1, L1_ffn_W2, L1_ffn_b2)
    return x

_drawn_inputs = setup_inputs


def setup_inputs(seed=0):
    import zlib

    import numpy as np

    out = dict(_drawn_inputs(seed))
    spreads = {'L0_ffn_gamma1': (1.0, 0.6),
     'L0_ffn_bq': (0.0, 0.8),
     'L0_ffn_bdown': (0.0, 0.8),
     'L0_ffn_bup': (0.0, 0.579),
     'L0_ffn_bo': (0.0, 0.1),
     'L0_ffn_gamma2': (1.0, 0.2),
     'L0_ffn_bg': (0.0, 0.8),
     'L1_attn_bq': (0.0, 0.8),
     'L1_attn_bk': (0.0, 0.8),
     'L1_attn_bv': (0.0, 0.8),
     'L1_attn_bo': (0.0, 0.345),
     'L1_attn_bqs': (0.0, 0.8),
     'L1_attn_bks': (0.0, 0.8),
     'L1_attn_bvs': (0.0, 0.8),
     'L1_ffn_bg': (0.0, 0.336),
     'L1_ffn_b1': (0.0, 0.564),
     'L1_ffn_b2': (0.0, 0.1)}
    factors = {'L1_attn_Wq': 8.0,
     'L1_attn_Wk': 8.0,
     'L1_attn_Wv': 8.0,
     'L1_attn_Wo': 8.0,
     'L1_attn_Wqs': 8.0,
     'L1_attn_Wks': 8.0,
     'L1_attn_Wvs': 8.0}
    for name, (base, spread) in spreads.items():
        noise = np.random.default_rng([zlib.crc32(name.encode()), seed]).standard_normal(out[name].shape)
        drawn = base * np.exp(spread * noise) if base else spread * noise
        out[name] = jnp.asarray(drawn.astype(out[name].dtype))
    for name, factor in factors.items():
        out[name] = (out[name] * factor).astype(out[name].dtype)
    return out
```

```python
from contextlib import ExitStack

import numpy as np

import concourse.bass as bass
from concourse import mybir

P = 128
B, S, D = 2, 1024, 128
H, HD = 16, 8
TB = S // P
T = B * TB
PAIRS = H // 2
U = B * PAIRS
LEAD = 3
RING = 4
L = 64
E0 = 8
E1, F1, R1 = 4, 512, 4
FC = F1 // P
G = 4
GT = T // G
BIG = 1e30
ROWS = 51
ROWSM = 54
KEYW = 2 * HD + 2

ALU = mybir.AluOpType
ACT = mybir.ActivationFunctionType
AX = mybir.AxisListType
F32 = mybir.dt.float32
BF16 = mybir.dt.bfloat16

C_ID, C_MQ, C_MS, C_HM, C_SEL, C_REP, C_TIE, C_COS, C_SIN = 0, 128, 256, 512, 528, 546, 674, 690, 818
C_EPS = 946
C_END = 948


def schedule(causal):
    granules, chunks = [], []
    for half in range(2):
        for j in range(4 * (half + 1) if causal else TB):
            q0 = max(0, P * j - 512 * half) if causal else 0
            granules.append((half, j, q0))
    for i in range(TB):
        for a in range(2):
            keys = P * (i + 1) if causal else S
            for c in range((keys + 511) // 512):
                chunks.append((i, a, c, min(512, keys - 512 * c)))
    return granules, chunks


def build(nc, io, out):
    ctx = ExitStack()
    with ctx:
        def sb(name, shape, dt=F32):
            return ctx.enter_context(nc.sbuf_tensor(name, shape, dt))

        def sem(name):
            return ctx.enter_context(nc.semaphore(name))

        PS = ctx.enter_context(nc.psum_tensor("PS", [P, 8, 512], F32))

        X = sb("X", [P, T, D])
        HX = sb("HX", [P, T, D])
        XH = sb("XH", [P, T, D])
        hT = sb("hT", [P, T * P])
        QU = sb("QU", [P, U + LEAD, 3, TB * 2 * HD])
        QF = QU[:, 0:U, :, :].rearrange("p u s x -> p (u s x)").rearrange("p (t c) -> p t c", t=T)
        CR = sb("CR", [P, U + LEAD, TB * 2, 3])
        SV = sb("SV", [P, U + LEAD, TB * 2])
        ATT = sb("ATT", [P, U + 1, TB, 2 * HD])
        CST = sb("CST", [P, C_END])
        IDB = sb("IDB", [P, P], BF16)
        MQB = sb("MQB", [P, P], BF16)
        MSB = sb("MSB", [P, 2 * P], BF16)
        ONES = sb("ONES", [1, P])
        STAT = sb("STAT", [P, T, 6])
        ST1, ST2, ST3, ST4 = (sb(f"ST{n}", [P, T]) for n in range(1, 5))
        IDF = CST[:, C_ID:C_ID + P]

        WN = hT[:, 0:8 * P].rearrange("p (n c) -> p n c", n=8)
        WT = sb("WT", [P, 8, P])
        W3 = sb("W3", [P, 160])
        WS5 = sb("WS5", [HD, 10])
        BD = sb("BD", [P, 2, H, 5])
        BCOL = sb("BCOL", [P, 2])
        BS5 = sb("BS5", [1, 10])
        BR = sb("BR", [1, 384 + 160])
        BO1 = sb("BO1", [1, P])
        WQS = sb("WQS", [P, 3, HD])
        BQS = sb("BQS", [P, 3])
        TEMP = sb("TEMP", [P, 1])
        CT = sb("CT", [P, 2, B])
        SC = sb("SC", [P, 2, B])
        SC2 = sb("SC2", [P, 2, B])
        HXF = HX[:, :, :].rearrange("p t d -> p (t d)")
        SCB = HXF[:, 0:4 * P].rearrange("p (l b n) -> p l b n", l=2, b=B)
        WMOD = XH[:, :, :].rearrange("p t d -> p (t d)")[:, 0:12 * D].rearrange("p (l n) -> p l n", l=2)
        MODC = sb("MODC", [P, 2, 2, B])
        MODR = sb("MODR", [P, 2, B, 4, D])
        SGN = HXF[:, 4 * P:8 * P].rearrange("p (l b n) -> p l b n", l=2, b=B)
        FW = sb("FW", [P, 3, P])
        WUP = sb("WUP", [L + 1, 2 * D])
        LT = sb("LT", [L + 1, T * P])
        FB = sb("FB", [1, 2, P])
        FCOL = sb("FCOL", [P, 3])
        WG0 = sb("WG0", [P, E0])
        BG0 = sb("BG0", [P, E0])
        WE = sb("WE", [P, E0, D])
        WG1 = sb("WG1", [P, R1, E1])
        WGC = sb("WGC", [P, E1])
        BG1 = sb("BG1", [P, R1, E1])
        W1 = sb("W1", [P, E1, F1])
        W2 = sb("W2", [P, E1, FC, D])
        B1 = sb("B1", [P, E1, FC])
        B2F = sb("B2F", [E1, D])
        GW = sb("GW", [P, T, E0])
        GW2 = sb("GW2", [P, T])
        GW3 = sb("GW3", [P, T])

        QA = sb("QA", [P, RING, TB * 2, 64], BF16)
        KA = sb("KA", [P, RING, TB * 2, 64], BF16)
        VA = sb("VA", [P, RING, TB * 2, 32])
        QKT = sb("QKT", [P, RING * S])
        KB = sb("KB", [P, RING, S], BF16)
        QT = QKT[:, 0:RING * S // 2].bitcast(BF16).rearrange("p (r n) -> p r n", r=RING)
        KT = QKT[:, RING * S // 2:RING * S].bitcast(BF16).rearrange("p (r n) -> p r n", r=RING)
        PB = sb("PB", [P, 4, 2, 512])
        OT = sb("OT", [P, 2, 512])
        NMA = sb("NMA", [P, RING, TB * 2])
        NMB = sb("NMB", [P, RING, TB * 2])
        NM = sb("NM", [P, RING, TB * 2])
        RQ = sb("RQ", [P, TB * 2, HD])
        RM = sb("RM", [P, TB * 2])
        RD = sb("RD", [P, TB, 2])

        HMID = QU[:, 0:16, :, :].rearrange("p u s x -> p (u s x)").rearrange("p (r f n) -> p r f n", r=3, f=FC)
        PBF = PB[:, :, :, :].rearrange("p a b c -> p (a b c)")
        PRD = PBF.rearrange("p (a h g d) -> p a h g d", a=2, h=H, g=H)
        PRP = hT[:, :].rearrange("p (h g d) -> p h g d", h=H, g=H)
        C5 = PBF[:, 0:U * 2 * TB * 2 * 5].rearrange("p (u s x) -> p u s x", u=U, s=2)
        SCR = QKT[:, :].rearrange("p (t h g) -> p t h g", t=T, h=H)
        SCM = sb("SCM", [P, T * H])
        SCL = sb("SCL", [P, T * H])

        names = """small_loaded x_loaded experts_loaded const_cast weights_transposed weights_copied
            rep_ready bd_ready w3_ready w3_copied silu_exp silu_ready mod_ready mod_copied mod_rows_copied
            mod_final dve_step pool_passed pool_init act_init out_done""".split()
        s = {n: sem(n) for n in names}
        for l in range(2):
            for n in """stats_var stats_std xhat_ready hT_psum hT_copied proj_psum proj_copied operands_ready
                k_built qv_built mparts_built kT_psum qT_psum qmT_psum sel_psum kT_ready qT_ready qmT_ready
                att_ready st_full exp_done pv_done o_copied mx_full mx_reduced nm_ready pool_step aT_psum
                aT_copied o_psum o_added x_done init_done""".split():
                s[f"{n}{l}"] = sem(f"{n}{l}")
        for n in """f_stats f_std f_h f_hT_psum f_hT_copied f_lat f_lat_copied f_qkv f_qkv_copied f_prod f_prod_used f_sc
            f_scmax f_exp f_prod2 f_prod2_used f_out f_oT f_oT_copied f_o f_x2 f_std2 f_h2 f_h2T f_h2T_copied f_gate f_gexp_in
            f_gexp f_y f_y_used f_done g_stats g_std g_h g_wg g_T g_T_copied g_lg g_tanh_in g_tanh g_cw g_cwT g_cwT_copied g_up
            g_gelu g_y g_y_used g_cur g_fin g_step f_step f_pool""".split():
            s[n] = sem(n)

        NSMALL = 0

        def to3(ap, n):
            return ap.unsqueeze(2).broadcast_to([ap.shape[0], ap.shape[1], n])

        sched = [schedule(True), schedule(False)]
        block = ctx.enter_context(nc.Block())

        small_dmas = []

        def small(dst, src):
            small_dmas.append((dst, src))

        for n, w in enumerate(["L0_attn_Wq", "L0_attn_Wk", "L0_attn_Wv", "L0_attn_Wo",
                               "L1_attn_Wq", "L1_attn_Wk", "L1_attn_Wv", "L1_attn_Wo"]):
            small(WN[:, n, :], io[w])
        for l in range(2):
            small(CT[:, l, :], io[f"L{l}_c"].rearrange("b k -> k b"))
            small(WMOD[:, l, :], io[f"L{l}_wmod"])
        for n, w in enumerate(["L1_attn_Wks", "L1_attn_Wvs"]):
            small(WS5[:, 5 * n:5 * n + 3], io[w].rearrange("c d -> d c"))
            small(WS5[:, 5 * n + 3:5 * n + 5], io[w][0:2, :].rearrange("c d -> d c"))

        def row(ap):
            return ap.rearrange("(a n) -> a n", a=1)

        def col(ap):
            return ap.rearrange("(n a) -> n a", a=1)

        for n, w in enumerate(["L1_attn_bks", "L1_attn_bvs"]):
            small(BS5[0:1, 5 * n:5 * n + 3], row(io[w]))
            small(BS5[0:1, 5 * n + 3:5 * n + 5], row(io[w][0:2]))
        for n, w in enumerate(["L1_attn_bq", "L1_attn_bk", "L1_attn_bv"]):
            small(BR[0:1, P * n:P * n + P], row(io[w]))
        small(BCOL[:, 0:1], col(io["L1_attn_bk"]))
        small(BCOL[:, 1:2], col(io["L1_attn_bv"]))
        small(BO1[0:1, :], row(io["L1_attn_bo"]))
        small(WQS[:, :, :].rearrange("p c d -> p (c d)"),
              io["L1_attn_Wqs"].rearrange("c d -> (c d)").partition_broadcast(P))
        small(BQS[:, :], io["L1_attn_bqs"].partition_broadcast(P))
        small(TEMP[:, :], io["L1_attn_temp"].partition_broadcast(P))
        small(FW[:, 0, :], io["L0_ffn_Wq"])
        small(FW[:, 1, 0:L], io["L0_ffn_Wdown"])
        small(FW[:, 2, :], io["L0_ffn_Wo"])
        small(WUP[0:L, :], io["L0_ffn_Wup"])
        small(WUP[L:L + 1, :], row(io["L0_ffn_bup"]))
        small(FB[0:1, 0, :], row(io["L0_ffn_bq"]))
        small(FB[0:1, 1, :], row(io["L0_ffn_bo"]))
        small(FCOL[:, 0:1], col(io["L0_ffn_gamma1"]))
        small(FCOL[:, 1:2], col(io["L0_ffn_gamma2"]))
        small(FCOL[0:L, 2:3], col(io["L0_ffn_bdown"]))
        small(WG0[:, :], io["L0_ffn_Wg"])
        small(BG0[:, :], io["L0_ffn_bg"].partition_broadcast(P))
        small(WG1[:, :, :], io["L1_ffn_Wg"].rearrange("r h e -> h r e"))
        small(BG1[:, :, :].rearrange("p r e -> p (r e)"), io["L1_ffn_bg"].rearrange("r e -> (r e)").partition_broadcast(P))
        small(B1[:, :, :].rearrange("p e c -> p (e c)"), io["L1_ffn_b1"].rearrange("e (c p) -> p (e c)", p=P))
        small(B2F[:, :], io["L1_ffn_b2"])
        small(CST[:, :], io["consts"])
        NSMALL = 16 * len(small_dmas)

        @block.sync
        def _(sp):
            for dst, src in small_dmas:
                sp.dma_start(dst, src, allow_slow_non_contiguous=True).then_inc(s["small_loaded"], 16)
            sp.dma_start(X[:, :, :], io["L0_attn_x"].rearrange("b (t p) d -> p (b t) d", p=P)).then_inc(s["x_loaded"], 16)
            sp.dma_start(WE[:, :, :], io["L0_ffn_We"].rearrange("e d f -> d e f")).then_inc(s["experts_loaded"], 16)
            sp.dma_start(W1[:, :, :], io["L1_ffn_W1"].rearrange("e h f -> h e f")).then_inc(s["experts_loaded"], 16)
            for e in range(E1):
                sp.dma_start(W2[:, e, :, :], io["L1_ffn_W2"][e].rearrange("(c p) h -> p c h", p=P)).then_inc(s["experts_loaded"], 16)
            sp.wait_ge(s["g_fin"], 1)
            sp.dma_start(out.rearrange("b (t p) d -> p (b t) d", p=P), X[:, :, :]).then_inc(s["out_done"], 16)
            sp.wait_ge(s["out_done"], 16)

        @block.tensor
        def _(pe):
            mm = nc.tensor.matmul
            tr = nc.tensor.transpose
            pe.wait_ge(s["small_loaded"], NSMALL)
            for n in range(8):
                last = tr(PS[:, n // 4, P * (n % 4):P * (n % 4) + P], WN[:, n, :], IDF)
            last.then_inc(s["weights_transposed"], 1)
            mm(PS[:, 2, 0:10], CST[0:HD, C_REP:C_REP + P], WS5[:, :], start=True, stop=True).then_inc(s["rep_ready"], 1)
            pe.wait_ge(s["bd_ready"], 1)
            for n in range(2):
                mm(PS[:, 2, 16 + 80 * n:96 + 80 * n], WN[:, 5 + n, :], BD[:, n, :, :].rearrange("p h c -> p (h c)"), start=True, stop=True)
                last = mm(PS[0:1, 3, 80 * n:80 * n + 80], BCOL[:, n:n + 1], BD[:, n, :, :].rearrange("p h c -> p (h c)"), start=True, stop=True)
            last.then_inc(s["w3_ready"], 1)
            pe.wait_ge(s["silu_ready"], 1)
            pe.wait_ge(s["w3_copied"], 1)
            for l in range(2):
                for n in range(2):
                    mm(PS[:, 3, 256 + 4 * l + 2 * n:258 + 4 * l + 2 * n], WMOD[:, l, P * n:P * n + P], SC2[:, l, :], start=True, stop=True)
                for b in range(B):
                    last = mm(PS[:, 4 + 2 * l + b, :], SCB[:, l, b, :], WMOD[:, l, 2 * P:6 * P], start=True, stop=True)
            last.then_inc(s["mod_ready"], 1)
            pe.wait_ge(s["mod_final"], 1)

            def transpose_tokens(src, full, copied, after):
                pe.wait_ge(*after)
                for g in range(G):
                    if g >= 2:
                        pe.wait_ge(copied, g - 1)
                    for t in range(GT):
                        last = tr(PS[:, g % 2, P * t:P * t + P], src(GT * g + t), IDF)
                    last.then_inc(full, 1)

            def attention(l):
                granules, chunks = sched[l]
                K = len(granules) // 2
                K0 = sum(1 for h, _, _ in granules if h == 0) // 2
                nch, ng = len(chunks), len(granules)
                TRB = PS[:, 7, :].bitcast(BF16)

                def transposes(src, full):
                    for t in range(TB):
                        last = tr(TRB[:, P * t:P * t + P], src[:, 2 * t:2 * t + 2, :].rearrange("p a c -> p (a c)"), IDB[:, :])
                    last.then_inc(full, 1)

                def max_chunk(u, r, n):
                    i, a, c, w = chunks[n]
                    pe_wait(s[f"mx_reduced{l}"], u * nch + n - 1, n >= 2, u)
                    diag = l == 0 and 512 * c + w == P * (i + 1)
                    ms = mm(PS[:, 4 + n % 2, 0:w], QT[:, r, P * i:P * i + P],
                            (KT, KB)[a][:, r, 512 * c:512 * c + w], start=True, stop=not diag)
                    if diag:
                        ms = mm(PS[:, 4 + n % 2, w - P:w], IDB[:, :], MQB[:, :], start=False, stop=True)
                    ms.then_inc(s[f"mx_full{l}"], 1)

                def pe_wait(sm, value, sure, u):
                    if sure or not isinstance(u, int) or u > 0:
                        pe.wait_ge(sm, value)

                def scores(u, r, g):
                    half, j, q0 = granules[g]
                    pe.wait_ge(s[f"exp_done{l}"], u * ng + g + 1)
                    first = l == 0 and half == 0 and j == 1
                    if first:
                        q0 = 0
                    for a in range(2):
                        o = PS[:, 2 * (g % 2) + a, q0:512]
                        diag = l == 0 and j >= 4 * half
                        last = mm(o, (KT, KB)[a][:, r, P * j:P * j + P],
                                  QT[:, r, 512 * half + q0:512 * half + 512], start=True, stop=not diag)
                        if diag:
                            w, m = (2 * P, MSB[:, :]) if first else (P, MSB[:, P:2 * P])
                            last = mm(PS[:, 2 * (g % 2) + a, q0:q0 + w], IDB[:, :], m, start=False, stop=True)
                    last.then_inc(s[f"st_full{l}"], 1)

                def values(u, r, k, extra=None):
                    start = k in (0, K0) if extra is None else True
                    for e in range(2):
                        half, j, q0 = granules[2 * k + e]
                        if l == 0 and half == 0 and j == 1 or extra:
                            q0 = 0
                        for a in range(2):
                            c0 = 32 * (2 * a + e)
                            last = mm(PS[c0:c0 + 32, 6, q0:512], VA[:, r, 2 * j + a, :],
                                      PB[:, (2 * k + e) % 4, a, q0:512], start=start,
                                      stop=(k in (K0 - 1, K - 1)) and extra is None)
                    return last

                def select(r):
                    o = PS[:, 7, 0:TB * KEYW]
                    for i in range(TB):
                        last = mm(o[:, KEYW * i:KEYW * i + KEYW], OT[:, i // 4, P * (i % 4):P * (i % 4) + P],
                                  CST[:, C_SEL:C_SEL + KEYW], start=True, stop=True)
                    last.then_inc(s[f"sel_psum{l}"], 1)

                for v in range(LEAD):
                    pe.wait_ge(s[f"k_built{l}"], v + 1)
                    if v:
                        pe.wait_ge(s[f"qT_ready{l}"], v)
                    transposes(KA[:, v, :, :], s[f"kT_psum{l}"])
                    pe.wait_ge(s[f"kT_ready{l}"], v + 1)
                    pe.wait_ge(s[f"qv_built{l}"], v + 1)
                    transposes(QA[:, v, :, :], s[f"qT_psum{l}"])
                pe.wait_ge(s[f"qT_ready{l}"], LEAD)
                for v in range(2):
                    for n in range(nch):
                        max_chunk(v, v, n)
                pe.wait_ge(s[f"mparts_built{l}"], 1)
                transposes(QA[:, 0, :, :], s[f"qmT_psum{l}"])
                values(None, RING - 1, K - 1, extra=True)

                ev = {2: "sel", K // 2: "qm", K // 2 + 1: "tk", K - 1: "tq"}

                def step(u, r):
                    nxt = (r + 1) % RING
                    n0 = 0
                    for k in range(K):
                        n1 = nch * (k + 1) // K
                        if k == 0:
                            pe.wait_ge(s[f"qT_ready{l}"], u + LEAD)
                        for n in range(n0, n0 + 2):
                            max_chunk(u + 2, (r + 2) % RING, n)
                        e = ev.get(k)
                        if e == "sel":
                            pe.wait_ge(s[f"o_copied{l}"], 2 * u + 1)
                            select(r)
                        elif e == "qm":
                            pe.wait_ge(s[f"att_ready{l}"], u + 1)
                            pe.wait_ge(s[f"mparts_built{l}"], u + 2)
                            transposes(QA[:, nxt, :, :], s[f"qmT_psum{l}"])
                        elif e == "tk":
                            pe.wait_ge(s[f"qmT_ready{l}"], u + 2)
                            pe.wait_ge(s[f"k_built{l}"], u + LEAD + 1)
                            transposes(KA[:, (r + LEAD) % RING, :, :], s[f"kT_psum{l}"])
                        elif e == "tq":
                            pe.wait_ge(s[f"kT_ready{l}"], u + LEAD + 1)
                            pe.wait_ge(s[f"qv_built{l}"], u + LEAD + 1)
                            transposes(QA[:, (r + LEAD) % RING, :, :], s[f"qT_psum{l}"])
                        if k == 0:
                            pe.wait_ge(s[f"qmT_ready{l}"], u + 1)
                        scores(u, r, 2 * k)
                        scores(u, r, 2 * k + 1)
                        for n in range(n0 + 2, n1):
                            max_chunk(u + 2, (r + 2) % RING, n)
                        n0 = n1
                        if k == 0:
                            last = values(u, (r + RING - 1) % RING, K - 1)
                        else:
                            if k - 1 in (0, K0):
                                pe.wait_ge(s[f"o_copied{l}"], 2 * u + (1 if k == 1 else 2))
                            last = values(u, r, k - 1)
                        last.then_inc(s[f"pv_done{l}"], 1)

                with pe.Fori(0, U // RING) as it:
                    for r in range(RING):
                        step(it * RING + r, r)
                pe.wait_ge(s[f"exp_done{l}"], U * ng + 2)
                values(None, RING - 1, K - 1).then_inc(s[f"pv_done{l}"], 1)
                pe.wait_ge(s[f"o_copied{l}"], 2 * U + 1)
                select(0)

            for l in range(2):
                transpose_tokens(lambda t: XH[:, t, :], s[f"hT_psum{l}"], s[f"hT_copied{l}"], (s[f"xhat_ready{l}"], 1))
                for t in range(T):
                    pe.wait_ge(s[f"hT_copied{l}"], t // GT + 1)
                    if t >= 3:
                        pe.wait_ge(s[f"proj_copied{l}"], t - 2)
                    bank = 2 + 2 * (t % 3)
                    lh = hT[:, P * t:P * t + P]
                    last = mm(PS[:, bank, 0:384], lh, WT[:, 4 * l:4 * l + 3, :].rearrange("p s n -> p (s n)"), start=True, stop=l == 0)
                    if l == 1:
                        mm(PS[:, bank, 0:384], ONES[0:1, :], BR[0:1, 0:384], start=False, stop=True)
                        mm(PS[:, bank + 1, 0:160], lh, W3[:, :], start=True, stop=False)
                        last = mm(PS[:, bank + 1, 0:160], ONES[0:1, :], BR[0:1, 384:544], start=False, stop=True)
                    last.then_inc(s[f"proj_psum{l}"], 1)
                pe.wait_ge(s[f"proj_copied{l}"], T)
                attention(l)
                transpose_tokens(lambda t: XH[:, t, :], s[f"aT_psum{l}"], s[f"aT_copied{l}"], (s[f"att_ready{l}"], U + 2))
                for t in range(T):
                    pe.wait_ge(s[f"aT_copied{l}"], t // GT + 1)
                    g = t // GT
                    if t % GT == 0 and g >= 2:
                        pe.wait_ge(s[f"o_added{l}"], g - 1)
                    o = PS[:, 2 + g % 2, P * (t % GT):P * (t % GT) + P]
                    last = mm(o, hT[:, P * t:P * t + P], WT[:, 4 * l + 3, :], start=True, stop=l == 0)
                    if l == 1:
                        last = mm(o, ONES[0:1, :], BO1[0:1, :], start=False, stop=True)
                    if t % GT == GT - 1:
                        last.then_inc(s[f"o_psum{l}"], 1)

                if l == 0:
                    pe.wait_ge(s["o_added0"], G)
                    transpose_tokens(lambda t: XH[:, t, :], s["f_hT_psum"], s["f_hT_copied"], (s["f_h"], 1))
                    for g in range(G):
                        pe.wait_ge(s["f_hT_copied"], g + 1)
                        if g >= 2:
                            pe.wait_ge(s["f_lat_copied"], g - 1)
                        mm(PS[0:L, 2 + g % 2, :], FW[:, 1, 0:L], hT[:, 512 * g:512 * g + 512], start=True, stop=True)\
                            .then_inc(s["f_lat"], 1)
                    for t in range(T):
                        pe.wait_ge(s["f_lat_copied"], t // GT + 1)
                        if t >= 4:
                            pe.wait_ge(s["f_qkv_copied"], t - 3)
                        bank = 4 + t % 4
                        mm(PS[:, bank, 0:P], hT[:, P * t:P * t + P], FW[:, 0, :], start=True, stop=False)
                        mm(PS[:, bank, 0:P], ONES[0:1, :], FB[0:1, 0, :], start=False, stop=True)
                        mm(PS[:, bank, P:3 * P], LT[:, P * t:P * t + P], WUP[:, :], start=True, stop=True)\
                            .then_inc(s["f_qkv"], 1)
                    transpose_tokens(lambda t: XH[:, t, :], s["f_oT"], s["f_oT_copied"], (s["f_out"], 1))
                    for t in range(T):
                        g = t // GT
                        pe.wait_ge(s["f_oT_copied"], g + 1)
                        if t % GT == 0 and g >= 2:
                            pe.wait_ge(s["f_x2"], g - 1)
                        o = PS[:, 2 + g % 2, P * (t % GT):P * (t % GT) + P]
                        mm(o, hT[:, P * t:P * t + P], FW[:, 2, :], start=True, stop=False)
                        last = mm(o, ONES[0:1, :], FB[0:1, 1, :], start=False, stop=True)
                        if t % GT == GT - 1:
                            last.then_inc(s["f_o"], 1)
                    transpose_tokens(lambda t: XH[:, t, :], s["f_h2T"], s["f_h2T_copied"], (s["f_h2"], 1))
                    pe.wait_ge(s["f_h2T_copied"], G)
                    for t in range(T):
                        last = mm(PS[:, 0, E0 * t:E0 * t + E0], hT[:, P * t:P * t + P], WG0[:, :], start=True, stop=True)
                    last.then_inc(s["f_gate"], 1)
                    pe.wait_ge(s["experts_loaded"], 96)
                    for t in range(T):
                        if t >= 3:
                            pe.wait_ge(s["f_y_used"], t - 2)
                        for hf in range(2):
                            last = mm(PS[:, 2 + 2 * (t % 3) + hf, :], hT[:, P * t:P * t + P],
                                      WE[:, 4 * hf:4 * hf + 4, :].rearrange("p e f -> p (e f)"), start=True, stop=True)
                        last.then_inc(s["f_y"], 1)
                    pe.wait_ge(s["f_y_used"], T)

            pe.wait_ge(s["o_added1"], G)
            with pe.Fori(0, R1) as r:
                for g in range(G):
                    pe.wait_ge(s["g_cur"], r * G + g + 1)
                    pe.wait_ge(s["g_wg"], r + 1)
                    for t in range(GT):
                        last = tr(PS[:, 0, P * t:P * t + P], HX[:, GT * g + t, :], IDF)
                    last.then_inc(s["g_T"], 1)
                    pe.wait_ge(s["g_T_copied"], r * G + g + 1)
                    pe.wait_ge(s["g_y_used"], (r * G + g) * 5 + 2)
                    for t in range(GT):
                        last = mm(PS[:, 1, E1 * t:E1 * t + E1], hT[:, 512 * (g % 2) + P * t:512 * (g % 2) + P * t + P], WGC[:, :], start=True, stop=True)
                    last.then_inc(s["g_lg"], 1)

                    def up(e):
                        for f in range(FC):
                            n = FC * e + f
                            pe.wait_ge(s["g_gelu"], (r * G + g) * 16 + n + 1)
                            mm(PS[:, 2 + f, :], W1[:, e, P * f:P * f + P], hT[:, 512 * (g % 2):512 * (g % 2) + 512],
                               start=True, stop=True).then_inc(s["g_up"], 1)

                    def down(e):
                        pe.wait_ge(s["g_y_used"], (r * G + g) * 5 + e + 1)
                        pe.wait_ge(s["g_gelu"], (r * G + g) * 16 + 4 * e + 8)
                        for t in range(GT):
                            for f in range(FC):
                                last = mm(PS[:, 6 + e % 2, P * t:P * t + P], HMID[:, e % 3, f, P * t:P * t + P], W2[:, e, f, :],
                                          start=f == 0, stop=f == FC - 1)
                        last.then_inc(s["g_y"], 1)
                    up(0)
                    up(1)
                    down(0)
                    up(2)
                    down(1)
                    up(3)
                    pe.wait_ge(s["g_cw"], r * G + g + 1)
                    for t in range(GT):
                        last = tr(PS[0:E1, 1, P * t:P * t + P], GW[:, GT * g + t, 0:E1], IDF)
                    last.then_inc(s["g_cwT"], 1)
                    down(2)
                    down(3)
                    pe.wait_ge(s["g_cwT_copied"], r * G + g + 1)
                    for t in range(GT):
                        last = mm(PS[:, 1, P * t:P * t + P], LT[0:E1, P * t:P * t + P], B2F[:, :], start=True, stop=True)
                    last.then_inc(s["g_y"], 1)

        @block.scalar
        def _(act):
            A = nc.scalar.activation
            act.wait_ge(s["small_loaded"], NSMALL)
            A(SC[:, :, :], CT[:, :, :], ACT.Exp, scale=-1.0).then_inc(s["silu_exp"], 1)
            act.wait_ge(s["weights_transposed"], 1)
            A(WT[:, :, :].rearrange("p (a n) c -> p a (n c)", a=2), PS[:, 0:2, :], ACT.Copy).then_inc(s["weights_copied"], 1)
            act.wait_ge(s["mod_ready"], 1)
            A(MODR[:, :, :, :, :].rearrange("p l b k d -> p (l b) (k d)"), PS[:, 4:8, :], ACT.Copy).then_inc(s["mod_rows_copied"], 1)

            def attention(l):
                granules, chunks = sched[l]
                K = len(granules) // 2
                K0 = sum(1 for h, _, _ in granules if h == 0) // 2
                ng = len(granules)
                TRB = PS[:, 7, :].bitcast(BF16)
                scale = float(HD) ** -0.5 if l == 0 else 1.0

                def copy_t(dst, full, count, ready):
                    act.wait_ge(full, count)
                    A(dst, TRB, ACT.Copy).then_inc(ready, 1)

                def copy_k(r, count):
                    act.wait_ge(s[f"kT_psum{l}"], count)
                    A(KT[0:64, r, :], TRB[0:64, :], ACT.Copy)
                    A(KB[64:P, r, :], TRB[64:P, :], ACT.Copy).then_inc(s[f"kT_ready{l}"], 1)

                act.wait_ge(s[f"init_done{l}"], 1)
                for v in range(LEAD):
                    copy_k(v, v + 1)
                    copy_t(QT[:, v, :], s[f"qT_psum{l}"], v + 1, s[f"qT_ready{l}"])
                copy_t(QT[:, 0, :], s[f"qmT_psum{l}"], 1, s[f"qmT_ready{l}"])
                act.sem_inc(s[f"exp_done{l}"], 2)

                ev = {2: "sel", K // 2: "qm", K // 2 + 1: "tk", K - 1: "tq"}

                def exp(u, r, g):
                    half, j, q0 = granules[g]
                    if l == 0 and half == 0 and j == 1:
                        q0 = 0
                    act.wait_ge(s[f"st_full{l}"], u * ng + g + 1)
                    act.wait_ge(s[f"pv_done{l}"], u * K + g // 2 - 1 + 2)
                    A(PB[:, g % 4, :, q0:512], PS[:, 2 * (g % 2):2 * (g % 2) + 2, q0:512], ACT.Exp, scale=scale)\
                        .then_inc(s[f"exp_done{l}"], 1)

                def copy_sums(half, groups, count):
                    act.wait_ge(s[f"pv_done{l}"], groups + 1)
                    act.wait_ge(s[f"sel_psum{l}"], count)
                    A(OT[:, half, :], PS[:, 6, :], ACT.Copy).then_inc(s[f"o_copied{l}"], 1)

                def step(u, r):
                    for k in range(K):
                        exp(u, r, 2 * k)
                        e = ev.get(k)
                        if e == "qm":
                            copy_t(QT[:, (r + 1) % RING, :], s[f"qmT_psum{l}"], u + 2, s[f"qmT_ready{l}"])
                        elif e == "tk":
                            copy_k((r + LEAD) % RING, u + LEAD + 1)
                        elif e == "tq":
                            copy_t(QT[:, (r + LEAD) % RING, :], s[f"qT_psum{l}"], u + LEAD + 1, s[f"qT_ready{l}"])
                        exp(u, r, 2 * k + 1)
                        if k == 0:
                            act.wait_ge(s[f"pv_done{l}"], u * K + 2)
                            A(OT[:, 1, :], PS[:, 6, :], ACT.Copy).then_inc(s[f"o_copied{l}"], 1)
                        elif k == K0:
                            act.wait_ge(s[f"pv_done{l}"], u * K + K0 + 2)
                            act.wait_ge(s[f"sel_psum{l}"], u + 1)
                            A(OT[:, 0, :], PS[:, 6, :], ACT.Copy).then_inc(s[f"o_copied{l}"], 1)
                act.sem_inc(s[f"pv_done{l}"], 1)
                with act.Fori(0, U // RING) as it:
                    for r in range(RING):
                        step(it * RING + r, r)
                act.wait_ge(s[f"pv_done{l}"], U * K + 2)
                A(OT[:, 1, :], PS[:, 6, :], ACT.Copy).then_inc(s[f"o_copied{l}"], 1)

            def copy_hT(full, copied, scale=None, bias=None):
                for g in range(G):
                    act.wait_ge(full, g + 1)
                    if scale is None:
                        A(hT[:, 512 * g:512 * g + 512], PS[:, g % 2, :], ACT.Copy).then_inc(copied, 1)
                    elif bias is None:
                        A(hT[:, 512 * g:512 * g + 512], PS[:, g % 2, :], ACT.Copy, scale=scale(g)).then_inc(copied, 1)
                    else:
                        A(hT[:, 512 * g:512 * g + 512], PS[:, g % 2, :], ACT.Identity, scale=scale(g), bias=bias(g))\
                            .then_inc(copied, 1)

            EPS5 = CST[:, C_EPS:C_EPS + 1]
            EPS6 = CST[:, C_EPS + 1:C_EPS + 2]
            for l in range(2):
                act.wait_ge(s[f"stats_var{l}"], 1)
                A(ST3[:, :], ST2[:, :], ACT.Sqrt, scale=1.0 / D, bias=EPS5).then_inc(s[f"stats_std{l}"], 1)
                act.wait_ge(s["mod_final"], 1)
                copy_hT(s[f"hT_psum{l}"], s[f"hT_copied{l}"],
                        scale=lambda g: MODC[:, l, 1, 2 * g // G:2 * g // G + 1], bias=lambda g: MODC[:, l, 0, 2 * g // G:2 * g // G + 1])
                for t in range(T):
                    act.wait_ge(s[f"proj_psum{l}"], t + 1)
                    bank = 2 + 2 * (t % 3)
                    b0 = PAIRS * (t // TB)
                    tt = 16 * (t % TB)
                    src = PS[:, bank, 0:384].rearrange("p (s r c) -> p r s c", s=3, r=PAIRS)
                    dst = QU[:, b0:b0 + PAIRS, :, tt:tt + 16]
                    if l == 0:
                        A(dst, src, ACT.Copy).then_inc(s["proj_copied0"], 1)
                    else:
                        A(dst[:, :, 0, :], src[:, :, 0, :], ACT.Copy, scale=TEMP[:, :])
                        A(dst[:, :, 1:3, :], src[:, :, 1:3, :], ACT.Copy)
                        A(C5[:, b0:b0 + PAIRS, :, 10 * (t % TB):10 * (t % TB) + 10],
                          PS[:, bank + 1, 0:160].rearrange("p (s r c) -> p r s c", s=2, r=PAIRS), ACT.Copy)\
                            .then_inc(s["proj_copied1"], 1)
                attention(l)
                copy_hT(s[f"aT_psum{l}"], s[f"aT_copied{l}"])
                if l == 0:
                    act.wait_ge(s["f_stats"], 1)
                    A(ST3[:, :], ST2[:, :], ACT.Sqrt, scale=1.0 / D, bias=EPS5).then_inc(s["f_std"], 1)
                    act.wait_ge(s["f_stats"], 2)
                    A(ST3[:, :], ST2[:, :], ACT.Sqrt, scale=1.0 / D, bias=EPS6).then_inc(s["f_std"], 1)
                    copy_hT(s["f_hT_psum"], s["f_hT_copied"], scale=lambda g: FCOL[:, 0:1])
                    for g in range(G):
                        act.wait_ge(s["f_lat"], g + 1)
                        A(LT[0:L, 512 * g:512 * g + 512], PS[0:L, 2 + g % 2, :], ACT.Identity, bias=FCOL[0:L, 2:3])\
                            .then_inc(s["f_lat_copied"], 1)
                    for t in range(T):
                        act.wait_ge(s["f_qkv"], t + 1)
                        A(QF[:, t, :], PS[:, 4 + t % 4, 0:384], ACT.Copy).then_inc(s["f_qkv_copied"], 1)
                    for c in range(2):
                        act.wait_ge(s["f_scmax"], c + 1)
                        half = SCR[:, TB * c:TB * c + TB, :, :].rearrange("p t h g -> p (t h g)")
                        A(half, half, ACT.Exp, scale=float(HD) ** -0.5).then_inc(s["f_exp"], 1)
                    copy_hT(s["f_oT"], s["f_oT_copied"])
                    act.wait_ge(s["f_stats"], 3)
                    A(ST3[:, :], ST2[:, :], ACT.Sqrt, scale=1.0 / D, bias=EPS6).then_inc(s["f_std"], 1)
                    copy_hT(s["f_h2T"], s["f_h2T_copied"], scale=lambda g: FCOL[:, 1:2])
                    act.wait_ge(s["f_gexp_in"], 1)
                    A(GW[:, :, :], GW[:, :, :], ACT.Exp).then_inc(s["f_gexp"], 1)
            act.wait_ge(s["g_stats"], 1)
            A(ST3[:, :], ST2[:, :], ACT.Sqrt, scale=1.0 / D, bias=EPS5).then_inc(s["g_std"], 1)
            act.sem_inc(s["g_gelu"], 4)
            with act.Fori(0, R1) as r:
                for g in range(G):
                    act.wait_ge(s["g_T"], r * G + g + 1)
                    A(hT[:, 512 * (g % 2):512 * (g % 2) + 512], PS[:, 0, :], ACT.Copy).then_inc(s["g_T_copied"], 1)

                    def gelu(e):
                        for f in range(FC):
                            act.wait_ge(s["g_up"], (r * G + g) * 16 + FC * e + f + 1)
                            if f == 0 and e >= 3:
                                act.wait_ge(s["g_y"], (r * G + g) * 5 + e - 2)
                            A(HMID[:, e % 3, f, :], PS[:, 2 + f, :], ACT.Gelu_apprx_tanh, bias=B1[:, e, f:f + 1])\
                                .then_inc(s["g_gelu"], 1)
                    gelu(0)
                    act.wait_ge(s["g_tanh_in"], r * G + g + 1)
                    A(GW[:, GT * g:GT * g + GT, E1:2 * E1], GW[:, GT * g:GT * g + GT, E1:2 * E1], ACT.Tanh).then_inc(s["g_tanh"], 1)
                    gelu(1)
                    gelu(2)
                    gelu(3)
                    act.wait_ge(s["g_cwT"], r * G + g + 1)
                    A(LT[0:E1, 0:512], PS[0:E1, 1, :], ACT.Copy).then_inc(s["g_cwT_copied"], 1)

        @block.vector
        def _(dve):
            V = nc.vector
            step_n = [0]

            def link(ins):
                step_n[0] += 1
                ins.then_inc(s["dve_step"], 1)
                dve.wait_ge(s["dve_step"], step_n[0])

            V.memset(ONES[:, :], 1.0)
            V.memset(QU[:, U:U + LEAD, :, :].rearrange("p u s x -> p (u s x)"), 0.0)
            V.memset(SV[:, U:U + LEAD, :].rearrange("p u x -> p (u x)"), 0.0)
            V.memset(PBF, 1.0)
            V.memset(VA[:, :, :, :].rearrange("p r x c -> p (r x) c"), 0.0)
            V.memset(OT[:, :, :].rearrange("p a n -> p (a n)"), 1.0)
            V.memset(LT[L:L + 1, :], 1.0)
            link(V.memset(ST1[:, :], 0.0))
            link(V.memset(VA[:, :, :, HD:HD + 1].rearrange("p r x c -> p (r x) c"), 1.0))
            dve.wait_ge(s["small_loaded"], NSMALL)
            V.tensor_copy(IDB[:, :], CST[:, C_ID:C_ID + P])
            V.tensor_copy(MQB[:, :], CST[:, C_MQ:C_MQ + P])
            link(V.tensor_copy(MSB[:, :], CST[:, C_MS:C_MS + 2 * P]))
            dve.wait_ge(s["silu_exp"], 1)
            link(V.tensor_scalar_add(SC2[:, :, :], SC[:, :, :], 1.0))
            link(V.reciprocal(SC[:, :, :], SC2[:, :, :]))
            link(V.tensor_tensor(SC2[:, :, :], CT[:, :, :], SC[:, :, :], ALU.mult))
            V.tensor_copy(SCB[:, :, :, :].rearrange("p l b n -> p (l b) n"),
                          to3(SC2[:, :, :].rearrange("p l b -> p (l b)"), P)).then_inc(s["silu_ready"], 1)
            dve.wait_ge(s["rep_ready"], 1)
            for n in range(2):
                last = V.tensor_tensor(BD[:, n, :, :], to3(CST[:, C_HM:C_HM + H], 5),
                                       PS[:, 2, 5 * n:5 * n + 5].unsqueeze(1).broadcast_to([P, H, 5]), ALU.mult)
            last.then_inc(s["bd_ready"], 1)
            dve.wait_ge(s["w3_ready"], 1)
            V.tensor_copy(W3[:, :], PS[:, 2, 16:176])
            for n in range(2):
                last = V.tensor_tensor(BR[0:1, 384 + 80 * n:464 + 80 * n].rearrange("p (h c) -> p h c", h=H),
                                       PS[0:1, 3, 80 * n:80 * n + 80].rearrange("p (h c) -> p h c", h=H),
                                       BS5[0:1, 5 * n:5 * n + 5].unsqueeze(1).broadcast_to([1, H, 5]), ALU.add)
            last.then_inc(s["w3_copied"], 1)
            dve.wait_ge(s["mod_ready"], 1)
            link(V.tensor_copy(MODC[:, :, :, :].rearrange("p l n b -> p (l n b)"), PS[:, 3, 256:264]))
            for l in range(2):
                V.tensor_scalar_add(MODC[:, l, 1, :], MODC[:, l, 1, :], 1.0)
            dve.wait_ge(s["mod_rows_copied"], 1)
            MR = MODR[:, :, :, :, :].rearrange("p l b k d -> p (l b) k d")
            SG = SGN[:, :, :, :].rearrange("p l b d -> p (l b) d")
            for k in (0, 3):
                link(V.tensor_scalar(SG, MR[:, :, k, :], 0.0, 2.0, ALU.is_ge, ALU.mult))
                link(V.tensor_scalar(SG, SG, -1.0, None, ALU.add))
                link(V.tensor_tensor(MR[:, :, k, :], MR[:, :, k, :], SG, ALU.mult))
                link(V.tensor_scalar(MR[:, :, k, :], MR[:, :, k, :], 0.25, None, ALU.max))
                link(V.tensor_tensor(MR[:, :, k, :], MR[:, :, k, :], SG, ALU.mult))
            link(V.tensor_scalar(MR[:, :, 2, :], MR[:, :, 2, :], 1.0, None, ALU.add))
            dve.sem_inc(s["mod_final"], 1)

            def batch_row(l, b, k):
                return MODR[:, l, b, k, :].unsqueeze(1).broadcast_to([P, TB, D])

            def layernorm(var, std, ready):
                for t in range(T):
                    last = V.bn_stats(STAT[:, t, :], X[:, t, :])
                link(last)
                V.tensor_tensor(ST1[:, :], STAT[:, :, 1], STAT[:, :, 4], ALU.subtract)
                V.tensor_tensor(ST2[:, :], STAT[:, :, 2], STAT[:, :, 5], ALU.add)
                link(V.tensor_tensor(ST4[:, :], STAT[:, :, 1], STAT[:, :, 4], ALU.add))
                V.tensor_scalar(ST4[:, :], ST4[:, :], 0.5, None, ALU.mult)
                link(V.tensor_tensor(ST1[:, :], ST1[:, :], ST1[:, :], ALU.mult))
                link(V.scalar_tensor_tensor(ST2[:, :], ST1[:, :], D / 4.0, ST2[:, :], ALU.mult, ALU.add))
                dve.sem_inc(var, 1)
                link(V.tensor_tensor(XH[:, :, :], X[:, :, :], to3(ST4[:, :], D), ALU.subtract))
                dve.wait_ge(*std)
                link(V.reciprocal(ST1[:, :], ST3[:, :]))
                link(V.tensor_tensor(XH[:, :, :], XH[:, :, :], to3(ST1[:, :], D), ALU.mult))
                if ready is not None:
                    dve.sem_inc(ready, 1)

            def rmsnorm(var, std, ready):
                link(V.tensor_tensor(XH[:, :, :], HX[:, :, :], HX[:, :, :], ALU.mult))
                link(V.tensor_reduce(ST2[:, :], XH[:, :, :], AX.X, ALU.add))
                dve.sem_inc(var, 1)
                dve.wait_ge(*std)
                link(V.reciprocal(ST1[:, :], ST3[:, :]))
                link(V.tensor_tensor(XH[:, :, :], HX[:, :, :], to3(ST1[:, :], D), ALU.mult))
                dve.sem_inc(ready, 1)

            def modulate(l):
                for b in range(B):
                    t = slice(TB * b, TB * b + TB)
                    V.tensor_tensor(HX[:, t, :], XH[:, t, :], batch_row(l, b, 2), ALU.mult)
                link(V.memset(ST1[:, :], 0.0))
                for b in range(B):
                    t = slice(TB * b, TB * b + TB)
                    last = V.tensor_tensor(HX[:, t, :], HX[:, t, :], batch_row(l, b, 1), ALU.add)
                link(last)

            def attention(l):
                granules, chunks = sched[l]
                K = len(granules) // 2
                nch = len(chunks)

                def reduce(u, r, n):
                    i, a, c, w = chunks[n]
                    dve.wait_ge(s[f"mx_full{l}"], u * nch + n + 1)
                    V.tensor_reduce((NMA, NMB)[c][:, r, 2 * i + a:2 * i + a + 1], PS[:, 4 + n % 2, 0:w], AX.X, ALU.max, negate=True)\
                        .then_inc(s[f"mx_reduced{l}"], 1)

                def combine(u, r):
                    dve.wait_ge(s[f"mx_reduced{l}"], u * nch + nch)
                    if l == 0:
                        V.tensor_copy(NM[:, r, 0:TB], NMA[:, r, 0:TB])
                    lo = TB if l == 0 else 0
                    V.tensor_tensor(NM[:, r, lo:2 * TB], NMA[:, r, lo:2 * TB], NMB[:, r, lo:2 * TB], ALU.min)\
                        .then_inc(s[f"nm_ready{l}"], 1)

                def normalise(u, count):
                    o = PS[:, 7, 0:TB * KEYW].rearrange("p (t c) -> p t c", c=KEYW)
                    dve.wait_ge(s[f"sel_psum{l}"], count)
                    V.reciprocal(RD[:, :, :], o[:, :, 2 * HD:KEYW]).then_inc(s[f"init_done{l}"], 1)
                    dve.wait_ge(s[f"init_done{l}"], count + 1)
                    V.tensor_tensor(ATT[:, u, :, :].rearrange("p t (a d) -> p t a d", a=2),
                                    o[:, :, 0:2 * HD].rearrange("p t (a d) -> p t a d", a=2),
                                    RD[:, :, :].unsqueeze(3).broadcast_to([P, TB, 2, HD]), ALU.mult)\
                        .then_inc(s[f"att_ready{l}"], 1)

                for v in range(2):
                    for n in range(nch):
                        reduce(v, v, n)
                    combine(v, v)

                def step(u, r):
                    for k in range(K):
                        n0, n1 = nch * k // K, nch * (k + 1) // K
                        for n in range(n0, n1):
                            reduce(u + 2, (r + 2) % RING, n)
                            if k == 2 and n == n0 + 1:
                                normalise(u, u + 1)
                    combine(u + 2, (r + 2) % RING)

                with dve.Fori(0, U // RING) as it:
                    for r in range(RING):
                        step(it * RING + r, r)
                normalise(U, U + 1)
                dve.wait_ge(s[f"att_ready{l}"], U + 1)
                for b in range(B):
                    last = V.tensor_copy(XH[:, TB * b:TB * b + TB, :].rearrange("p t (u c) -> p u t c", u=PAIRS),
                                         ATT[:, 1 + PAIRS * b:1 + PAIRS * b + PAIRS, :, :])
                last.then_inc(s[f"att_ready{l}"], 1)

            def residual(l, full, added, k):
                for g in range(G):
                    dve.wait_ge(full, g + 1)
                    t = slice(GT * g, GT * g + GT)
                    b = GT * g // TB
                    link(V.tensor_tensor(XH[:, t, :], PS[:, 2 + g % 2, :].rearrange("p (t d) -> p t d", t=GT),
                                         MODR[:, l, b, k, :].unsqueeze(1).broadcast_to([P, GT, D]), ALU.mult))
                    dve.sem_inc(added, 1)
                    link(V.tensor_tensor(X[:, t, :], X[:, t, :], XH[:, t, :], ALU.add))

            for l in range(2):
                if l == 0:
                    dve.wait_ge(s["x_loaded"], 16)
                layernorm(s[f"stats_var{l}"], (s[f"stats_std{l}"], 1), s[f"xhat_ready{l}"])
                if l == 0:
                    dve.wait_ge(s["proj_copied0"], T)
                    w = QU[:, 0:U, 0:2, :].rearrange("p u s x -> p u (s x)").rearrange("p u (x e) -> p u x e", e=HD)
                    lo, hi = w[:, :, :, 0:4], w[:, :, :, 4:8]
                    cos = CST[:, C_COS:C_COS + P].rearrange("p (x e) -> p x e", e=4).unsqueeze(1).broadcast_to([P, U, 32, 4])
                    sin = CST[:, C_SIN:C_SIN + P].rearrange("p (x e) -> p x e", e=4).unsqueeze(1).broadcast_to([P, U, 32, 4])
                    t1 = XH[:, :, :].rearrange("p t (x e) -> p t x e", e=4)
                    t2 = HX[:, :, :].rearrange("p t (x e) -> p t x e", e=4)
                    V.tensor_tensor(t1, lo, sin, ALU.mult)
                    link(V.tensor_tensor(t2, hi, sin, ALU.mult))
                    V.tensor_tensor(lo, lo, cos, ALU.mult)
                    link(V.tensor_tensor(hi, hi, cos, ALU.mult))
                    V.tensor_tensor(lo, lo, t2, ALU.subtract)
                    link(V.tensor_tensor(hi, hi, t1, ALU.add))
                    dve.sem_inc(s["operands_ready0"], 1)
                else:
                    dve.wait_ge(s["proj_copied1"], T)
                    a5 = C5[:, :, 0, :].rearrange("p u (x c) -> p u x c", c=5)
                    b5 = C5[:, :, 1, :].rearrange("p u (x c) -> p u x c", c=5)
                    t1 = XH[:, :, :].rearrange("p t d -> p (t d)")[:, 0:U * 48].rearrange("p (u x c) -> p u x c", u=U, c=3)
                    t2 = HX[:, :, :].rearrange("p t (x e) -> p t x e", e=HD)
                    cr = CR[:, 0:U, :, :]
                    V.tensor_tensor(t1, a5[:, :, :, 2:5], b5[:, :, :, 1:4], ALU.mult)
                    link(V.tensor_tensor(cr, a5[:, :, :, 1:4], b5[:, :, :, 2:5], ALU.mult))
                    link(V.tensor_tensor(cr, cr, t1, ALU.subtract))
                    kk = QU[:, 0:U, 1, :].rearrange("p u (x e) -> p u x e", e=HD)
                    for c in range(3):
                        link(V.tensor_tensor(t2, cr[:, :, :, c].unsqueeze(3).broadcast_to([P, U, 16, HD]),
                                             WQS[:, c, :].unsqueeze(1).unsqueeze(1).broadcast_to([P, U, 16, HD]), ALU.mult))
                        link(V.tensor_tensor(kk, kk, t2, ALU.add))
                    link(V.tensor_tensor(cr, cr, BQS[:, :].unsqueeze(1).unsqueeze(1).broadcast_to([P, U, 16, 3]), ALU.mult))
                    link(V.tensor_reduce(SV[:, 0:U, :], cr, AX.X, ALU.add))
                    link(V.tensor_scalar(SV[:, 0:U, :], SV[:, 0:U, :], TEMP[:, 0:1], None, ALU.mult))
                    V.memset(PBF, 1.0)
                    V.memset(VA[:, :, :, :].rearrange("p r x c -> p (r x) c"), 0.0)
                    link(V.memset(ST1[:, :], 0.0))
                    link(V.memset(VA[:, :, :, HD:HD + 1].rearrange("p r x c -> p (r x) c"), 1.0))
                    V.memset(QU[:, U:U + LEAD, :, :].rearrange("p u s x -> p (u s x)"), 0.0)
                    link(V.memset(ST1[:, :], 0.0))
                    dve.sem_inc(s["operands_ready1"], 1)
                V.memset(KT[64:P, :, :].rearrange("p r n -> p (r n)"), 0.0)
                link(V.memset(KB[0:64, :, :].rearrange("p r n -> p (r n)"), 0.0))
                dve.sem_inc(s[f"init_done{l}"], 1)
                attention(l)
                residual(l, s[f"o_psum{l}"], s[f"o_added{l}"], 0)

                if l == 0:
                    layernorm(s["f_stats"], (s["f_std"], 1), None)
                    modulate(0)
                    rmsnorm(s["f_stats"], (s["f_std"], 2), s["f_h"])
                    dve.wait_ge(s["f_qkv_copied"], T)

                    def pair_products(dst, t):
                        q = QF[:, t, 0:P].rearrange("p (h d) -> p h d", h=H).unsqueeze(2).broadcast_to([P, H, H, HD])
                        kk = QF[:, t, P:3 * P].rearrange("p (g e) -> p g e", g=H)[:, :, 0:HD].unsqueeze(1).broadcast_to([P, H, H, HD])
                        return V.tensor_tensor(dst, q, kk, ALU.mult)

                    def value_products(dst, t):
                        pr = SCR[:, t, :, :].unsqueeze(2).broadcast_to([P, H, HD, H])
                        vv = QF[:, t, P:3 * P].rearrange("p (g e) -> p e g", g=H)[:, HD:2 * HD, :].unsqueeze(1).broadcast_to([P, H, HD, H])
                        return V.tensor_tensor(dst.rearrange("p h g d -> p (h g d)").rearrange("p (h d g) -> p h d g", h=H, d=HD), pr, vv, ALU.mult)

                    for t in range(0, T, 2):
                        link(pair_products(PRD[:, 0, :, :, :], t))
                        link(V.tensor_reduce(SCR[:, t, :, :], PRD[:, 0, :, :, :], AX.X, ALU.add))
                        dve.wait_ge(s["f_prod"], t // 2 + 1)
                        pb = (PRD[:, 1], PRP)[t // 2 % 2]
                        V.tensor_reduce(SCR[:, t + 1, :, :], pb, AX.X, ALU.add).then_inc(s["f_prod_used"], 1)
                    link(V.memset(ST1[:, :], 0.0))
                    scr = SCR[:, :, :, :].rearrange("p t h g -> p (t h) g")
                    for c in range(2):
                        hf = slice(TB * H * c, TB * H * c + TB * H)
                        link(V.tensor_reduce(SCM[:, hf], scr[:, hf, :], AX.X, ALU.max))
                        link(V.tensor_tensor(scr[:, hf, :], scr[:, hf, :], to3(SCM[:, hf], H), ALU.subtract))
                        dve.sem_inc(s["f_scmax"], 1)
                    for c in range(2):
                        hf = slice(TB * H * c, TB * H * c + TB * H)
                        dve.wait_ge(s["f_exp"], c + 1)
                        link(V.tensor_reduce(SCL[:, hf], scr[:, hf, :], AX.X, ALU.add))
                    link(V.reciprocal(SCM[:, :], SCL[:, :]))
                    for t in range(0, T, 2):
                        link(value_products(PRD[:, 0, :, :, :], t))
                        dd = PRD[:, 0].rearrange("p h g d -> p (h g d)").rearrange("p (x g) -> p x g", g=H)
                        link(V.tensor_reduce(XH[:, t, :], dd, AX.X, ALU.add))
                        dve.wait_ge(s["f_prod"], TB + t // 2 + 1)
                        pb = (PRD[:, 1], PRP)[t // 2 % 2].rearrange("p h g d -> p (h g d)").rearrange("p (x g) -> p x g", g=H)
                        V.tensor_reduce(XH[:, t + 1, :], pb, AX.X, ALU.add).then_inc(s["f_prod_used"], 1)
                    link(V.memset(ST1[:, :], 0.0))
                    xo = XH[:, :, :].rearrange("p t (h d) -> p (t h) d", h=H)
                    link(V.tensor_tensor(xo, xo, to3(SCM[:, :], HD), ALU.mult))
                    dve.sem_inc(s["f_out"], 1)
                    for g in range(G):
                        dve.wait_ge(s["f_o"], g + 1)
                        t = slice(GT * g, GT * g + GT)
                        link(V.tensor_tensor(HX[:, t, :], HX[:, t, :], PS[:, 2 + g % 2, :].rearrange("p (t d) -> p t d", t=GT), ALU.add))
                        dve.sem_inc(s["f_x2"], 1)
                    rmsnorm(s["f_stats"], (s["f_std"], 3), s["f_h2"])
                    dve.wait_ge(s["f_gate"], 1)
                    lg = PS[:, 0, 0:T * E0].rearrange("p (t e) -> p t e", e=E0)
                    link(V.tensor_tensor(GW[:, :, :], lg, BG0[:, :].unsqueeze(1).broadcast_to([P, T, E0]), ALU.add))
                    link(V.tensor_reduce(GW2[:, :], GW[:, :, :], AX.X, ALU.max))
                    link(V.tensor_tensor(GW[:, :, :], GW[:, :, :], to3(GW2[:, :], E0), ALU.subtract))
                    dve.sem_inc(s["f_gexp_in"], 1)
                    dve.wait_ge(s["f_gexp"], 1)
                    link(V.tensor_reduce(GW2[:, :], GW[:, :, :], AX.X, ALU.add))
                    link(V.reciprocal(GW3[:, :], GW2[:, :]))
                    link(V.tensor_tensor(GW[:, :, :], GW[:, :, :], to3(GW3[:, :], E0), ALU.mult))
                    for t in range(T):
                        dve.wait_ge(s["f_y"], t + 1)
                        for e in range(E0):
                            ins = V.scalar_tensor_tensor(HX[:, t, :], PS[:, 2 + 2 * (t % 3) + e // 4, P * (e % 4):P * (e % 4) + P],
                                                         GW[:, t, e:e + 1], HX[:, t, :], ALU.mult, ALU.add)
                            link(ins)
                        dve.sem_inc(s["f_y_used"], 1)
                    for b in range(B):
                        t = slice(TB * b, TB * b + TB)
                        last = V.tensor_tensor(HX[:, t, :], HX[:, t, :], batch_row(0, b, 3), ALU.mult)
                    link(last)
                    link(V.tensor_tensor(X[:, :, :], X[:, :, :], HX[:, :, :], ALU.add))

            layernorm(s["g_stats"], (s["g_std"], 1), None)
            modulate(1)
            dve.sem_inc(s["g_cur"], G)
            dve.sem_inc(s["g_lg"], 1)
            dve.sem_inc(s["g_y_used"], 2)
            NL = 10
            with dve.Fori(0, R1) as r:
                base = r * (1 + G * (NL + 20))
                cnt = [0]

                def glink(ins):
                    cnt[0] += 1
                    ins.then_inc(s["g_step"], 1)
                    dve.wait_ge(s["g_step"], base + cnt[0])
                dve.wait_ge(s["g_lg"], r * G + 1)
                V.tensor_copy(WGC[:, :], WG1[:, r, :]).then_inc(s["g_wg"], 1)
                glink(V.tensor_copy(ST1[:, 0:E1], BG1[:, r, :]))
                for g in range(G):
                    t = slice(GT * g, GT * g + GT)
                    lw, th = GW[:, t, 0:E1], GW[:, t, E1:2 * E1]
                    cmp = SCR[:, 0, 0:GT, :].rearrange("p t (e f) -> p t e f", e=E1)
                    tie = CST[:, C_TIE:C_TIE + 16].rearrange("p (e f) -> p e f", e=E1).unsqueeze(1).broadcast_to([P, GT, E1, E1])
                    ce = SCR[:, 1, 0:GT, :].rearrange("p t (e f) -> p t e f", e=E1)
                    dve.wait_ge(s["g_lg"], r * G + g + 2)
                    glink(V.tensor_tensor(lw, PS[:, 1, 0:GT * E1].rearrange("p (t e) -> p t e", e=E1),
                                          ST1[:, 0:E1].unsqueeze(1).broadcast_to([P, GT, E1]), ALU.add))
                    mine = lw.unsqueeze(3).broadcast_to([P, GT, E1, E1])
                    other = lw.unsqueeze(2).broadcast_to([P, GT, E1, E1])
                    V.tensor_tensor(cmp, other, mine, ALU.is_gt)
                    glink(V.tensor_tensor(ce, other, mine, ALU.is_equal))
                    glink(V.tensor_tensor(ce, ce, tie, ALU.mult))
                    glink(V.tensor_tensor(cmp, cmp, ce, ALU.add))
                    glink(V.tensor_reduce(th, cmp, AX.X, ALU.add))
                    sel = SCR[:, 2, 0:GT, 0:E1]
                    tmp = SCR[:, 3, 0:GT, 0:E1]
                    glink(V.tensor_scalar(sel, th, 1.5, None, ALU.is_lt))
                    glink(V.tensor_tensor(tmp, sel, lw, ALU.mult))
                    glink(V.tensor_reduce(GW2[:, 0:GT], tmp, AX.X, ALU.add))
                    glink(V.tensor_scalar(GW2[:, 0:GT], GW2[:, 0:GT], 0.5, None, ALU.mult))
                    glink(V.tensor_tensor(th, lw, to3(GW2[:, 0:GT], E1), ALU.subtract))
                    dve.sem_inc(s["g_tanh_in"], 1)
                    dve.wait_ge(s["g_tanh"], r * G + g + 1)
                    glink(V.tensor_scalar(th, th, 0.5, 0.5, ALU.mult, ALU.add))
                    glink(V.tensor_tensor(lw, th, sel, ALU.mult))
                    dve.sem_inc(s["g_cw"], 1)
                    for e in range(E1):
                        dve.wait_ge(s["g_y"], (r * G + g) * 5 + e + 1)
                        for n in range(GT):
                            last = V.scalar_tensor_tensor(HX[:, GT * g + n, :], PS[:, 6 + e % 2, P * n:P * n + P],
                                                          GW[:, GT * g + n, e:e + 1], HX[:, GT * g + n, :], ALU.mult, ALU.add)
                        glink(last)
                        dve.sem_inc(s["g_y_used"], 1)
                    dve.wait_ge(s["g_y"], (r * G + g) * 5 + 5)
                    glink(V.tensor_tensor(HX[:, t, :], HX[:, t, :], PS[:, 1, :].rearrange("p (t d) -> p t d", t=GT), ALU.add))
                    dve.sem_inc(s["g_y_used"], 1)
                    dve.sem_inc(s["g_cur"], 1)
                while cnt[0] < 1 + G * (NL + 20):
                    glink(V.memset(ST2[:, 0:1], 0.0))
            for b in range(B):
                t = slice(TB * b, TB * b + TB)
                last = V.tensor_tensor(HX[:, t, :], HX[:, t, :], batch_row(1, b, 3), ALU.mult)
            link(last)
            V.tensor_tensor(X[:, :, :], X[:, :, :], HX[:, :, :], ALU.add).then_inc(s["g_fin"], 1)

        @block.gpsimd
        def _(pool):
            Q = nc.gpsimd
            pn = [0]

            def plink(ins):
                pn[0] += 1
                ins.then_inc(s["pool_init"], 1)
                pool.wait_ge(s["pool_init"], pn[0])
            Q.memset(QA[:, :, :, :].rearrange("p r x c -> p (r x c)"), 0.0)
            plink(Q.memset(KA[:, :, :, :].rearrange("p r x c -> p (r x c)"), 0.0))
            Q.memset(QA[:, :, :, 48:ROWS].rearrange("p r x c -> p (r x) c"), 1.0)
            plink(Q.memset(KA[:, :, :, ROWS:ROWSM].rearrange("p r x c -> p (r x) c"), 1.0))

            for l in range(2):
                per = [0]

                def pwait(sm, value):
                    pool.wait_ge(sm, value)
                    pool.sem_inc(s["pool_passed"], 1)

                def split(src, dst, at, base):
                    w = src.shape[2]
                    rest = RQ[:, :, 0:w]
                    cur = src
                    for n in range(3):
                        part = dst[:, :, at[n]:at[n] + w]
                        plinku(Q.tensor_copy(part, cur), base)
                        if n < 2:
                            plinku(Q.tensor_tensor(rest, cur, part, ALU.subtract), base)
                            cur = rest

                def plinku(ins, base):
                    per[0] += 1
                    ins.then_inc(s[f"pool_step{l}"], 1)
                    pwait(s[f"pool_step{l}"], base + per[0])

                def build_k(u, r, base):
                    kk = QU[:, u, 1, :].rearrange("p (x e) -> p x e", e=HD)
                    dst = KA[:, r, :, :]
                    split(kk, dst, (0, HD, 2 * HD), base)
                    Q.tensor_copy(dst[:, :, 3 * HD:5 * HD], dst[:, :, 0:2 * HD])
                    if l == 1:
                        plinku(Q.tensor_copy(dst[:, :, 5 * HD:6 * HD], dst[:, :, 0:HD]), base)
                        split(SV[:, u, :].unsqueeze(2), dst, (48, 49, 50), base)
                        Q.tensor_copy(RM[:, 0:1], RM[:, 1:2]).then_inc(s[f"k_built{l}"], 1)
                    else:
                        Q.tensor_copy(dst[:, :, 5 * HD:6 * HD], dst[:, :, 0:HD]).then_inc(s[f"k_built{l}"], 1)

                def build_qv(u, r, base):
                    qq = QU[:, u, 0, :].rearrange("p (x e) -> p x e", e=HD)
                    dst = QA[:, r, :, :]
                    split(qq, dst, (0, 3 * HD, 5 * HD), base)
                    Q.memset(dst[:, :, ROWS:ROWSM], 0.0)
                    Q.tensor_copy(dst[:, :, HD:2 * HD], dst[:, :, 0:HD])
                    Q.tensor_copy(dst[:, :, 2 * HD:3 * HD], dst[:, :, 0:HD])
                    Q.tensor_copy(dst[:, :, 4 * HD:5 * HD], dst[:, :, 3 * HD:4 * HD])
                    Q.tensor_copy(VA[:, r, :, 0:HD], QU[:, u, 2, :].rearrange("p (x e) -> p x e", e=HD))\
                        .then_inc(s[f"qv_built{l}"], 1)

                def build_m(u, r, base):
                    pwait(s[f"nm_ready{l}"], u + 1)
                    split(NM[:, r, :].unsqueeze(2), QA[:, r, :, :], (51, 52, 53), base)
                    Q.tensor_copy(RM[:, 0:1], RM[:, 1:2]).then_inc(s[f"mparts_built{l}"], 1)

                plink(Q.memset(RM[:, :], 0.0))
                pool.wait_ge(s[f"operands_ready{l}"], 1)
                for v in range(LEAD):
                    build_k(v, v, 0)
                    build_qv(v, v, 0)
                build_m(0, 0, 0)
                start = per[0]
                one = (5 + (6 if l == 1 else 0)) + 5 + 5

                def step(u, r, base):
                    per[0] = 0
                    build_m(u + 1, (r + 1) % RING, base)
                    pwait(s[f"qmT_psum{l}"], u + 1)
                    build_k(u + LEAD, (r + LEAD) % RING, base)
                    pwait(s[f"pv_done{l}"], u * (len(sched[l][0]) // 2) + 2)
                    build_qv(u + LEAD, (r + LEAD) % RING, base)
                    assert per[0] == one, per[0]

                with pool.Fori(0, U // RING) as it:
                    for r in range(RING):
                        u = it * RING + r
                        step(u, r, u * one + start)
                if l == 0:
                    pool.wait_ge(s["f_qkv_copied"], T)
                    pool.wait_ge(s["att_ready0"], U + 1)
                    for n in range(T):
                        t = 2 * (n % TB) + 1
                        dst = (PRD[:, 1], PRP)[n % 2]
                        if n >= 2:
                            pool.wait_ge(s["f_prod_used"], n - 1)
                        if n < TB:
                            q = QF[:, t, 0:P].rearrange("p (h d) -> p h d", h=H).unsqueeze(2).broadcast_to([P, H, H, HD])
                            kk = QF[:, t, P:3 * P].rearrange("p (g e) -> p g e", g=H)[:, :, 0:HD].unsqueeze(1).broadcast_to([P, H, H, HD])
                            Q.tensor_tensor(dst, q, kk, ALU.mult).then_inc(s["f_prod"], 1)
                        else:
                            pool.wait_ge(s["f_exp"], 2 if t >= TB else 1)
                            pr = SCR[:, t, :, :].unsqueeze(2).broadcast_to([P, H, HD, H])
                            vv = QF[:, t, P:3 * P].rearrange("p (g e) -> p e g", g=H)[:, HD:2 * HD, :].unsqueeze(1).broadcast_to([P, H, HD, H])
                            Q.tensor_tensor(dst.rearrange("p h g d -> p (h g d)").rearrange("p (h d g) -> p h d g", h=H, d=HD),
                                            pr, vv, ALU.mult).then_inc(s["f_prod"], 1)


_INS = ['L0_attn_x', 'L0_attn_Wq', 'L0_attn_Wk', 'L0_attn_Wv', 'L0_attn_Wo', 'L0_ffn_gamma1', 'L0_ffn_Wq', 'L0_ffn_bq',
        'L0_ffn_Wdown', 'L0_ffn_bdown', 'L0_ffn_Wup', 'L0_ffn_bup', 'L0_ffn_Wo', 'L0_ffn_bo', 'L0_ffn_gamma2', 'L0_ffn_Wg',
        'L0_ffn_bg', 'L0_ffn_We', 'L0_c', 'L0_wmod', 'L1_attn_Wq', 'L1_attn_bq', 'L1_attn_Wk', 'L1_attn_bk', 'L1_attn_Wv',
        'L1_attn_bv', 'L1_attn_Wo', 'L1_attn_bo', 'L1_attn_Wqs', 'L1_attn_bqs', 'L1_attn_Wks', 'L1_attn_bks', 'L1_attn_Wvs',
        'L1_attn_bvs', 'L1_attn_temp', 'L1_ffn_Wg', 'L1_ffn_bg', 'L1_ffn_W1', 'L1_ffn_b1', 'L1_ffn_W2', 'L1_ffn_b2', 'L1_c',
        'L1_wmod']


def constants():
    c = np.zeros((P, C_END), np.float32)
    c[:, C_ID:C_ID + P] = np.eye(P)
    c[:, C_MQ:C_MQ + P] = -BIG * np.triu(np.ones((P, P)), 1)
    c[:, C_MS:C_MS + P] = -BIG
    c[:, C_MS + P:C_MS + 2 * P] = -BIG * np.tril(np.ones((P, P)), -1)
    p = np.arange(P)
    c[p, C_HM + p // HD] = 1.0
    for a in range(2):
        for e in range(2):
            for d in range(HD):
                c[32 * (2 * a + e) + d, C_SEL + HD * a + d] = 1.0
            c[32 * (2 * a + e) + HD, C_SEL + 2 * HD + a] = 1.0
    c[p % HD, C_REP + p] = 1.0
    for e in range(E1):
        c[:, C_TIE + E1 * e:C_TIE + E1 * e + e] = 1.0
    inv = (1.0 / np.float32(10000.0) ** (np.arange(0, HD, 2, dtype=np.float32) / np.float32(HD))).astype(np.float32)
    ang = np.outer(np.arange(S, dtype=np.float32), inv).astype(np.float32)
    for at, fn in ((C_COS, np.cos), (C_SIN, np.sin)):
        v = fn(ang).astype(np.float32).reshape(TB, P, 1, 4).transpose(1, 0, 2, 3)
        v = np.broadcast_to(v[:, None], (P, 2, TB, 2, 4))
        c[:, at:at + P] = v.reshape(P, P)
    c[:, C_EPS], c[:, C_EPS + 1] = 1e-5, 1e-6
    return c


def kernel(**inputs):
    import numpy as _np
    import concourse.bacc as _bacc
    from concourse import mybir as _mybir
    from concourse.bass_utils import run_bass_kernel_spmd as _run

    nc = _bacc.Bacc("TRN2", target_bir_lowering=False, num_devices=1)
    arrays, io = {}, {}
    for name in _INS:
        a = _np.ascontiguousarray(inputs[name])
        if a.ndim == 0:
            a = a.reshape(1)
        arrays[f"in_{name}"] = a
        io[name] = nc.dram_tensor(f"in_{name}", a.shape, _mybir.dt.from_np(a.dtype), kind="ExternalInput").ap()
    arrays["in_consts"] = constants()
    io["consts"] = nc.dram_tensor("in_consts", (P, C_END), F32, kind="ExternalInput").ap()
    out = nc.dram_tensor("out_x", (B, S, D), F32, kind="ExternalOutput").ap()
    build(nc, io, out)
    r = _run(nc, [arrays], core_ids=[0])
    return r.results[0]["out_x"]
```

```python
from contextlib import ExitStack

import numpy as np

import concourse.bass as bass
from concourse import mybir

P = 128
B, S, D = 2, 1024, 128
H, HD = 16, 8
TB = S // P
T = B * TB
PAIRS = H // 2
U = B * PAIRS
LEAD = 3
RING = 4
L = 64
E0 = 8
E1, F1, R1 = 4, 512, 4
FC = F1 // P
G = 4
GT = T // G
BIG = 1e30
ROWS = 51
ROWSM = 54
KEYW = 2 * HD + 2

ALU = mybir.AluOpType
ACT = mybir.ActivationFunctionType
AX = mybir.AxisListType
F32 = mybir.dt.float32
F32R = mybir.dt.float32r
BF16 = mybir.dt.bfloat16

C_ID, C_MQ, C_MS, C_HM, C_SEL, C_REP, C_TIE, C_COS, C_SIN = 0, 128, 256, 512, 528, 546, 674, 690, 818
C_EPS = 946
C_END = 948


def schedule(causal):
    granules, chunks = [], []
    for half in range(2):
        for j in range(4 * (half + 1) if causal else TB):
            q0 = max(0, P * j - 512 * half) if causal else 0
            granules.append((half, j, q0))
    for i in range(TB):
        for a in range(2):
            keys = P * (i + 1) if causal else S
            for c in range((keys + 511) // 512):
                chunks.append((i, a, c, min(512, keys - 512 * c)))
    return granules, chunks


def event_at(l, k):
    return ({2: "sel", 3: "qm", 4: "tk", 5: "tq"}, {2: "sel", 4: "qm", 5: "tk", 7: "tq"})[l].get(k)


def build(nc, io, out):
    ctx = ExitStack()
    with ctx:
        def sb(name, shape, dt=F32):
            return ctx.enter_context(nc.sbuf_tensor(name, shape, dt))

        def sem(name):
            return ctx.enter_context(nc.semaphore(name))

        PS = ctx.enter_context(nc.psum_tensor("PS", [P, 8, 512], F32))

        X = sb("X", [P, T, D])
        HX = sb("HX", [P, T, D])
        XH = sb("XH", [P, T, D])
        hT = sb("hT", [P, T * P])
        CST = sb("CST", [P, C_END])
        IDB = sb("IDB", [P, P], BF16)
        MQB = sb("MQB", [P, P], BF16)
        MSB = sb("MSB", [P, 2 * P], BF16)
        ONES = sb("ONES", [1, P])
        STAT = sb("STAT", [P, T, 6])
        ST1, ST2, ST3, ST4 = (sb(f"ST{n}", [P, T]) for n in range(1, 5))
        IDF = CST[:, C_ID:C_ID + P]

        WN = hT[:, 0:8 * P].rearrange("p (n c) -> p n c", n=8)
        WT = sb("WT", [P, 8, P])
        W3 = sb("W3", [P, 160])
        WS5 = sb("WS5", [HD, 10])
        BD = sb("BD", [P, 2, H, 5])
        BCOL = sb("BCOL", [P, 2])
        BS5 = sb("BS5", [1, 10])
        BR = sb("BR", [1, 384 + 160])
        BO1 = sb("BO1", [1, P])
        WQS = sb("WQS", [P, 3, HD])
        BQS = sb("BQS", [P, 3])
        TEMP = sb("TEMP", [P, 1])
        CT = sb("CT", [P, 2, B])
        SC = sb("SC", [P, 2, B])
        SC2 = sb("SC2", [P, 2, B])
        HXF = HX[:, :, :].rearrange("p t d -> p (t d)")
        SCB = HXF[:, 0:4 * P].rearrange("p (l b n) -> p l b n", l=2, b=B)
        WMOD = XH[:, :, :].rearrange("p t d -> p (t d)")[:, 0:12 * D].rearrange("p (l n) -> p l n", l=2)
        MODC = sb("MODC", [P, 2, 4, B])
        MODR = sb("MODR", [P, 2, B, 4, D])
        SGN = HXF[:, 4 * P:8 * P].rearrange("p (l b n) -> p l b n", l=2, b=B)
        FW = sb("FW", [P, 3, P])
        WUP = sb("WUP", [L + 1, 2 * D])
        LT = sb("LT", [L + 1, T * P])
        FB = sb("FB", [1, 2, P])
        FCOL = sb("FCOL", [P, 3])
        WG0 = sb("WG0", [P, E0])
        BG0 = sb("BG0", [P, E0])
        WE = sb("WE", [P, E0, D])
        WG1 = sb("WG1", [P, R1 + 1, E1])
        WGC = sb("WGC", [P, E1])
        BG1 = sb("BG1", [P, R1 + 1, E1])
        W1 = sb("W1", [P, E1, F1])
        W2 = sb("W2", [P, E1, FC, D])
        B1 = sb("B1", [P, E1, FC])
        B2C = sb("B2C", [P, E1])
        GW = sb("GW", [P, T, E0])
        GW2 = sb("GW2", [P, T])
        GW3 = sb("GW3", [P, T])

        over = ExitStack()

        def att(name, shape, dt=F32):
            return over.enter_context(nc.sbuf_tensor(name, shape, dt))

        QU = att("QU", [P, U + LEAD, 3, TB * 2 * HD])
        QF = QU[:, 0:U, :, :].rearrange("p u s x -> p (u s x)").rearrange("p (t c) -> p t c", t=T)
        CR = att("CR", [P, U + LEAD, TB * 2, 3])
        SV = att("SV", [P, U + LEAD, TB * 2])
        ATT = att("ATT", [P, U + 1, TB, 2 * HD])
        QA = att("QA", [P, RING, TB * 2, 64], BF16)
        KA = att("KA", [P, RING, TB * 2, 64], BF16)
        VA = att("VA", [P, RING, TB * 2, 32])
        QKT = att("QKT", [P, RING * S])
        QT = QKT[:, 0:RING * S // 2].bitcast(BF16).rearrange("p (r n) -> p r n", r=RING)
        KT = QKT[:, RING * S // 2:RING * S].bitcast(BF16).rearrange("p (r n) -> p r n", r=RING)
        KB = att("KB", [P, RING, S], BF16)
        PB = att("PB", [P, 4, 2, 512])
        OT = att("OT", [P, 2, 512])
        NMA = att("NMA", [P, RING, TB * 2])
        NMB = att("NMB", [P, RING, TB * 2])
        NM = att("NM", [P, RING, TB * 2])
        RQ = att("RQ", [P, TB * 2, HD])
        RM = att("RM", [P, TB * 2])
        RD = att("RD", [P, TB, 2])
        PBF = PB[:, :, :, :].rearrange("p a b c -> p (a b c)")
        PRD = PBF.rearrange("p (a h g d) -> p a h g d", a=2, h=H, g=H)
        PRP = hT[:, :].rearrange("p (h g d) -> p h g d", h=H, g=H)
        C5 = PBF[:, 0:U * 2 * TB * 2 * 5].rearrange("p (u s x) -> p u s x", u=U, s=2)
        SCR = QKT[:, :].rearrange("p (t h g) -> p t h g", t=T, h=H)
        SCM = att("SCM", [P, T * H])
        SCL = att("SCL", [P, T * H])
        over.close()
        W1H, W1L = (sb(n, [P, E1, F1], F32R) for n in ("W1H", "W1L"))
        W2H, W2L = (sb(n, [P, E1, FC, D], F32R) for n in ("W2H", "W2L"))
        CTH, CTL = (sb(n, [P, T * P], F32R) for n in ("CTH", "CTL"))
        HMH, HML = (sb(n, [P, 2 * FC, 512], F32R) for n in ("HMH", "HML"))
        XF = XH[:, :, :].rearrange("p t d -> p (t d)")
        HMF = XF.rearrange("p (r n) -> p r n", r=FC)
        HF = HX[:, :, :].rearrange("p t d -> p (t d)")
        CWB = HF[:, 0:1024].rearrange("p (r n) -> p r n", r=2)
        YS = HF[:, 1024:2048].rearrange("p (r n) -> p r n", r=2)
        GWS = sb("GWS", [P, GT, 2 * E1], F32R)
        CWT = sb("CWT", [2 * E1, 512], F32R)
        SLW = sb("SLW", [2 * E1, E1, P], F32R)
        CMP, CEQ = (sb(n, [P, GT, E1, E1]) for n in ("CMP", "CEQ"))
        SELE, SELL = (sb(n, [P, GT, E1]) for n in ("SELE", "SELL"))

        names = """small_loaded x_loaded experts_loaded const_cast weights_transposed weights_copied
            rep_ready bd_ready w3_ready w3_copied silu_exp silu_ready mod_ready mod_copied mod_rows_copied
            mod_final dve_step pool_passed pool_init act_init out_done""".split()
        s = {n: sem(n) for n in names}
        for l in range(2):
            for n in """stats_var stats_std xhat_ready hT_psum hT_copied proj_psum proj_copied operands_ready
                k_built qv_built mparts_built kT_psum qT_psum qmT_psum sel_psum kT_ready qT_ready qmT_ready
                att_ready st_full exp_done pv_done o_copied mx_full mx_reduced nm_ready pool_step aT_psum
                aT_copied o_psum o_added x_done init_done""".split():
                s[f"{n}{l}"] = sem(f"{n}{l}")
        for n in """f_stats f_std f_h f_hT_psum f_hT_copied f_lat f_lat_copied f_qkv f_qkv_copied f_prod f_prod_used f_sc
            f_scmax f_exp f_prod2 f_prod2_used f_out f_oT f_oT_copied f_o f_x2 f_std2 f_h2 f_h2T f_h2T_copied f_gate f_gexp_in
            f_gexp f_y f_y_used f_done g_stats g_std g_wg g_xh g_hT g_hT_copied g_high g_split g_lg g_tanh_in g_tanh g_cw g_cwp g_cwr g_cwT g_cwb g_up
            g_gelu g_lo g_y g_y_read g_acc g_cur g_last g_last_added g_fin g_step g_pstep""".split():
            s[n] = sem(n)

        NSMALL = 0

        def to3(ap, n):
            return ap.unsqueeze(2).broadcast_to([ap.shape[0], ap.shape[1], n])

        sched = [schedule(True), schedule(False)]
        block = ctx.enter_context(nc.Block())

        small_dmas = []

        def small(dst, src):
            small_dmas.append((dst, src))

        for n, w in enumerate(["L0_attn_Wq", "L0_attn_Wk", "L0_attn_Wv", "L0_attn_Wo",
                               "L1_attn_Wq", "L1_attn_Wk", "L1_attn_Wv", "L1_attn_Wo"]):
            small(WN[:, n, :], io[w])
        for l in range(2):
            small(CT[:, l, :], io[f"L{l}_c"].rearrange("b k -> k b"))
            small(WMOD[:, l, :], io[f"L{l}_wmod"])
        for n, w in enumerate(["L1_attn_Wks", "L1_attn_Wvs"]):
            small(WS5[:, 5 * n:5 * n + 3], io[w].rearrange("c d -> d c"))
            small(WS5[:, 5 * n + 3:5 * n + 5], io[w][0:2, :].rearrange("c d -> d c"))

        def row(ap):
            return ap.rearrange("(a n) -> a n", a=1)

        def col(ap):
            return ap.rearrange("(n a) -> n a", a=1)

        for n, w in enumerate(["L1_attn_bks", "L1_attn_bvs"]):
            small(BS5[0:1, 5 * n:5 * n + 3], row(io[w]))
            small(BS5[0:1, 5 * n + 3:5 * n + 5], row(io[w][0:2]))
        for n, w in enumerate(["L1_attn_bq", "L1_attn_bk", "L1_attn_bv"]):
            small(BR[0:1, P * n:P * n + P], row(io[w]))
        small(BCOL[:, 0:1], col(io["L1_attn_bk"]))
        small(BCOL[:, 1:2], col(io["L1_attn_bv"]))
        small(BO1[0:1, :], row(io["L1_attn_bo"]))
        small(WQS[:, :, :].rearrange("p c d -> p (c d)"),
              io["L1_attn_Wqs"].rearrange("c d -> (c d)").partition_broadcast(P))
        small(BQS[:, :], io["L1_attn_bqs"].partition_broadcast(P))
        small(TEMP[:, :], io["L1_attn_temp"].partition_broadcast(P))
        small(FW[:, 0, :], io["L0_ffn_Wq"])
        small(FW[:, 1, 0:L], io["L0_ffn_Wdown"])
        small(FW[:, 2, :], io["L0_ffn_Wo"])
        small(WUP[0:L, :], io["L0_ffn_Wup"])
        small(WUP[L:L + 1, :], row(io["L0_ffn_bup"]))
        small(FB[0:1, 0, :], row(io["L0_ffn_bq"]))
        small(FB[0:1, 1, :], row(io["L0_ffn_bo"]))
        small(FCOL[:, 0:1], col(io["L0_ffn_gamma1"]))
        small(FCOL[:, 1:2], col(io["L0_ffn_gamma2"]))
        small(FCOL[0:L, 2:3], col(io["L0_ffn_bdown"]))
        small(WG0[:, :], io["L0_ffn_Wg"])
        small(BG0[:, :], io["L0_ffn_bg"].partition_broadcast(P))
        small(WG1[:, 0:R1, :], io["L1_ffn_Wg"].rearrange("r h e -> h r e"))
        small(BG1[:, 0:R1, :].rearrange("p r e -> p (r e)"), io["L1_ffn_bg"].rearrange("r e -> (r e)").partition_broadcast(P))
        small(B1[:, :, :].rearrange("p e c -> p (e c)"), io["L1_ffn_b1"].rearrange("e (c p) -> p (e c)", p=P))
        small(B2C[:, :], io["L1_ffn_b2"].rearrange("e h -> h e"))
        small(CST[:, :], io["consts"])
        NSMALL = 16 * len(small_dmas)

        @block.sync
        def _(sp):
            for dst, src in small_dmas:
                sp.dma_start(dst, src, allow_slow_non_contiguous=True).then_inc(s["small_loaded"], 16)
            sp.dma_start(X[:, :, :], io["L0_attn_x"].rearrange("b (t p) d -> p (b t) d", p=P)).then_inc(s["x_loaded"], 16)
            sp.dma_start(WE[:, :, :], io["L0_ffn_We"].rearrange("e d f -> d e f")).then_inc(s["experts_loaded"], 16)
            sp.dma_start(W1[:, :, :], io["L1_ffn_W1"].rearrange("e h f -> h e f")).then_inc(s["experts_loaded"], 16)
            for e in range(E1):
                sp.dma_start(W2[:, e, :, :], io["L1_ffn_W2"][e].rearrange("(c p) h -> p c h", p=P)).then_inc(s["experts_loaded"], 16)
            for g in range(G):
                sp.wait_ge(s["g_fin"], g + 1)
                sp.dma_start(out.rearrange("b (t p) d -> p (b t) d", p=P)[:, GT * g:GT * g + GT, :], X[:, GT * g:GT * g + GT, :])\
                    .then_inc(s["out_done"], 16)
            sp.wait_ge(s["out_done"], 16 * G)

        @block.tensor
        def _(pe):
            mm = nc.tensor.matmul
            tr = nc.tensor.transpose
            pe.wait_ge(s["small_loaded"], NSMALL)
            for n in range(8):
                last = tr(PS[:, n // 4, P * (n % 4):P * (n % 4) + P], WN[:, n, :], IDF)
            last.then_inc(s["weights_transposed"], 1)
            mm(PS[:, 2, 0:10], CST[0:HD, C_REP:C_REP + P], WS5[:, :], start=True, stop=True).then_inc(s["rep_ready"], 1)
            pe.wait_ge(s["bd_ready"], 1)
            for n in range(2):
                mm(PS[:, 2, 16 + 80 * n:96 + 80 * n], WN[:, 5 + n, :], BD[:, n, :, :].rearrange("p h c -> p (h c)"), start=True, stop=True)
                last = mm(PS[0:1, 3, 80 * n:80 * n + 80], BCOL[:, n:n + 1], BD[:, n, :, :].rearrange("p h c -> p (h c)"), start=True, stop=True)
            last.then_inc(s["w3_ready"], 1)
            pe.wait_ge(s["silu_ready"], 1)
            pe.wait_ge(s["w3_copied"], 1)
            for l in range(2):
                for n, piece in enumerate((0, 1, 3, 4)):
                    mm(PS[:, 3, 256 + 8 * l + 2 * n:258 + 8 * l + 2 * n], WMOD[:, l, P * piece:P * piece + P], SC2[:, l, :], start=True, stop=True)
                for b in range(B):
                    last = mm(PS[:, 4 + 2 * l + b, :], SCB[:, l, b, :], WMOD[:, l, 2 * P:6 * P], start=True, stop=True)
            last.then_inc(s["mod_ready"], 1)
            pe.wait_ge(s["mod_final"], 1)

            def transpose_tokens(src, full, copied, after):
                pe.wait_ge(*after)
                for g in range(G):
                    if g >= 2:
                        pe.wait_ge(copied, g - 1)
                    for t in range(GT):
                        last = tr(PS[:, g % 2, P * t:P * t + P], src(GT * g + t), IDF)
                    last.then_inc(full, 1)

            def attention(l):
                granules, chunks = sched[l]
                K = len(granules) // 2
                K0 = sum(1 for h, _, _ in granules if h == 0) // 2
                nch, ng = len(chunks), len(granules)
                TRB = PS[:, 7, :].bitcast(BF16)

                def transposes(src, full):
                    for t in range(TB):
                        last = tr(TRB[:, P * t:P * t + P], src[:, 2 * t:2 * t + 2, :].rearrange("p a c -> p (a c)"), IDB[:, :])
                    last.then_inc(full, 1)

                def max_chunk(u, r, n):
                    i, a, c, w = chunks[n]
                    pe_wait(s[f"mx_reduced{l}"], u * nch + n - 1, n >= 2, u)
                    diag = l == 0 and 512 * c + w == P * (i + 1)
                    ms = mm(PS[:, 4 + n % 2, 0:w], QT[:, r, P * i:P * i + P],
                            (KT, KB)[a][:, r, 512 * c:512 * c + w], start=True, stop=not diag)
                    if diag:
                        ms = mm(PS[:, 4 + n % 2, w - P:w], IDB[:, :], MQB[:, :], start=False, stop=True)
                    ms.then_inc(s[f"mx_full{l}"], 1)

                def pe_wait(sm, value, sure, u):
                    if sure or not isinstance(u, int) or u > 0:
                        pe.wait_ge(sm, value)

                def scores(u, r, g):
                    half, j, q0 = granules[g]
                    pe.wait_ge(s[f"exp_done{l}"], u * ng + g + 1)
                    first = l == 0 and half == 0 and j == 1
                    if first:
                        q0 = 0
                    for a in range(2):
                        o = PS[:, 2 * (g % 2) + a, q0:512]
                        diag = l == 0 and j >= 4 * half
                        last = mm(o, (KT, KB)[a][:, r, P * j:P * j + P],
                                  QT[:, r, 512 * half + q0:512 * half + 512], start=True, stop=not diag)
                        if diag:
                            w, m = (2 * P, MSB[:, :]) if first else (P, MSB[:, P:2 * P])
                            last = mm(PS[:, 2 * (g % 2) + a, q0:q0 + w], IDB[:, :], m, start=False, stop=True)
                    last.then_inc(s[f"st_full{l}"], 1)

                def values(u, r, k, extra=None):
                    start = k in (0, K0) if extra is None else True
                    for e in range(2):
                        half, j, q0 = granules[2 * k + e]
                        if l == 0 and half == 0 and j == 1 or extra:
                            q0 = 0
                        for a in range(2):
                            c0 = 32 * (2 * a + e)
                            last = mm(PS[c0:c0 + 32, 6, q0:512], VA[:, r, 2 * j + a, :],
                                      PB[:, (2 * k + e) % 4, a, q0:512], start=start,
                                      stop=(k in (K0 - 1, K - 1)) and extra is None)
                    return last

                def select(r):
                    o = PS[:, 7, 0:TB * KEYW]
                    for i in range(TB):
                        last = mm(o[:, KEYW * i:KEYW * i + KEYW], OT[:, i // 4, P * (i % 4):P * (i % 4) + P],
                                  CST[:, C_SEL:C_SEL + KEYW], start=True, stop=True)
                    last.then_inc(s[f"sel_psum{l}"], 1)

                for v in range(LEAD):
                    pe.wait_ge(s[f"k_built{l}"], v + 1)
                    if v:
                        pe.wait_ge(s[f"qT_ready{l}"], v)
                    transposes(KA[:, v, :, :], s[f"kT_psum{l}"])
                    pe.wait_ge(s[f"kT_ready{l}"], v + 1)
                    pe.wait_ge(s[f"qv_built{l}"], v + 1)
                    transposes(QA[:, v, :, :], s[f"qT_psum{l}"])
                pe.wait_ge(s[f"qT_ready{l}"], LEAD)
                for v in range(2):
                    for n in range(nch):
                        max_chunk(v, v, n)
                pe.wait_ge(s[f"mparts_built{l}"], 1)
                transposes(QA[:, 0, :, :], s[f"qmT_psum{l}"])
                values(None, RING - 1, K - 1, extra=True)

                def event(u, r, k):
                    e = event_at(l, k)
                    nxt = (r + 1) % RING
                    if e == "sel":
                        pe.wait_ge(s[f"o_copied{l}"], 2 * u + 1)
                        select(r)
                    elif e == "qm":
                        pe.wait_ge(s[f"att_ready{l}"], u + 1)
                        pe.wait_ge(s[f"mparts_built{l}"], u + 2)
                        transposes(QA[:, nxt, :, :], s[f"qmT_psum{l}"])
                    elif e == "tk":
                        pe.wait_ge(s[f"qmT_ready{l}"], u + 2)
                        pe.wait_ge(s[f"k_built{l}"], u + LEAD + 1)
                        transposes(KA[:, (r + LEAD) % RING, :, :], s[f"kT_psum{l}"])
                    elif e == "tq":
                        pe.wait_ge(s[f"kT_ready{l}"], u + LEAD + 1)
                        pe.wait_ge(s[f"qv_built{l}"], u + LEAD + 1)
                        transposes(QA[:, (r + LEAD) % RING, :, :], s[f"qT_psum{l}"])

                def step(u, r):
                    for k in range(K):
                        n = nch * k // K
                        assert nch * (k + 1) // K == n + 4
                        if k == 0:
                            pe.wait_ge(s[f"qT_ready{l}"], u + LEAD)
                        max_chunk(u + 2, (r + 2) % RING, n)
                        max_chunk(u + 2, (r + 2) % RING, n + 1)
                        if k == 0:
                            pe.wait_ge(s[f"qmT_ready{l}"], u + 1)
                        scores(u, r, 2 * k)
                        event(u, r, k)
                        scores(u, r, 2 * k + 1)
                        max_chunk(u + 2, (r + 2) % RING, n + 2)
                        max_chunk(u + 2, (r + 2) % RING, n + 3)
                        if k == 0:
                            last = values(u, (r + RING - 1) % RING, K - 1)
                        else:
                            if k - 1 in (0, K0):
                                pe.wait_ge(s[f"o_copied{l}"], 2 * u + (1 if k == 1 else 2))
                            last = values(u, r, k - 1)
                        last.then_inc(s[f"pv_done{l}"], 1)

                with pe.Fori(0, U // RING) as it:
                    for r in range(RING):
                        step(it * RING + r, r)
                pe.wait_ge(s[f"exp_done{l}"], U * ng + 2)
                values(None, RING - 1, K - 1).then_inc(s[f"pv_done{l}"], 1)
                pe.wait_ge(s[f"o_copied{l}"], 2 * U + 1)
                select(0)

            for l in range(2):
                transpose_tokens(lambda t: XH[:, t, :], s[f"hT_psum{l}"], s[f"hT_copied{l}"], (s[f"xhat_ready{l}"], 1))
                for t in range(T):
                    pe.wait_ge(s[f"hT_copied{l}"], t // GT + 1)
                    if t >= 3:
                        pe.wait_ge(s[f"proj_copied{l}"], t - 2)
                    bank = 2 + 2 * (t % 3)
                    lh = hT[:, P * t:P * t + P]
                    last = mm(PS[:, bank, 0:384], lh, WT[:, 4 * l:4 * l + 3, :].rearrange("p s n -> p (s n)"), start=True, stop=l == 0)
                    if l == 1:
                        mm(PS[:, bank, 0:384], ONES[0:1, :], BR[0:1, 0:384], start=False, stop=True)
                        mm(PS[:, bank + 1, 0:160], lh, W3[:, :], start=True, stop=False)
                        last = mm(PS[:, bank + 1, 0:160], ONES[0:1, :], BR[0:1, 384:544], start=False, stop=True)
                    last.then_inc(s[f"proj_psum{l}"], 1)
                pe.wait_ge(s[f"proj_copied{l}"], T)
                attention(l)
                transpose_tokens(lambda t: XH[:, t, :], s[f"aT_psum{l}"], s[f"aT_copied{l}"], (s[f"att_ready{l}"], U + 2))
                for t in range(T):
                    pe.wait_ge(s[f"aT_copied{l}"], t // GT + 1)
                    g = t // GT
                    if t % GT == 0 and g >= 2:
                        pe.wait_ge(s[f"o_added{l}"], g - 1)
                    o = PS[:, 2 + g % 2, P * (t % GT):P * (t % GT) + P]
                    last = mm(o, hT[:, P * t:P * t + P], WT[:, 4 * l + 3, :], start=True, stop=l == 0)
                    if l == 1:
                        last = mm(o, ONES[0:1, :], BO1[0:1, :], start=False, stop=True)
                    if t % GT == GT - 1:
                        last.then_inc(s[f"o_psum{l}"], 1)

                if l == 0:
                    pe.wait_ge(s["o_added0"], G)
                    transpose_tokens(lambda t: XH[:, t, :], s["f_hT_psum"], s["f_hT_copied"], (s["f_h"], 1))
                    for g in range(G):
                        pe.wait_ge(s["f_hT_copied"], g + 1)
                        if g >= 2:
                            pe.wait_ge(s["f_lat_copied"], g - 1)
                        mm(PS[0:L, 2 + g % 2, :], FW[:, 1, 0:L], hT[:, 512 * g:512 * g + 512], start=True, stop=True)\
                            .then_inc(s["f_lat"], 1)
                    for t in range(T):
                        pe.wait_ge(s["f_lat_copied"], t // GT + 1)
                        if t >= 4:
                            pe.wait_ge(s["f_qkv_copied"], t - 3)
                        bank = 4 + t % 4
                        mm(PS[:, bank, 0:P], hT[:, P * t:P * t + P], FW[:, 0, :], start=True, stop=False)
                        mm(PS[:, bank, 0:P], ONES[0:1, :], FB[0:1, 0, :], start=False, stop=True)
                        mm(PS[:, bank, P:3 * P], LT[:, P * t:P * t + P], WUP[:, :], start=True, stop=True)\
                            .then_inc(s["f_qkv"], 1)
                    transpose_tokens(lambda t: XH[:, t, :], s["f_oT"], s["f_oT_copied"], (s["f_out"], 1))
                    for t in range(T):
                        g = t // GT
                        pe.wait_ge(s["f_oT_copied"], g + 1)
                        if t % GT == 0 and g >= 2:
                            pe.wait_ge(s["f_x2"], g - 1)
                        o = PS[:, 2 + g % 2, P * (t % GT):P * (t % GT) + P]
                        mm(o, hT[:, P * t:P * t + P], FW[:, 2, :], start=True, stop=False)
                        last = mm(o, ONES[0:1, :], FB[0:1, 1, :], start=False, stop=True)
                        if t % GT == GT - 1:
                            last.then_inc(s["f_o"], 1)
                    transpose_tokens(lambda t: XH[:, t, :], s["f_h2T"], s["f_h2T_copied"], (s["f_h2"], 1))
                    pe.wait_ge(s["f_h2T_copied"], G)
                    for t in range(T):
                        last = mm(PS[:, 0, E0 * t:E0 * t + E0], hT[:, P * t:P * t + P], WG0[:, :], start=True, stop=True)
                    last.then_inc(s["f_gate"], 1)
                    pe.wait_ge(s["experts_loaded"], 96)
                    for t in range(T):
                        if t >= 3:
                            pe.wait_ge(s["f_y_used"], t - 2)
                        for hf in range(2):
                            last = mm(PS[:, 2 + 2 * (t % 3) + hf, :], hT[:, P * t:P * t + P],
                                      WE[:, 4 * hf:4 * hf + 4, :].rearrange("p e f -> p (e f)"), start=True, stop=True)
                        last.then_inc(s["f_y"], 1)
                    pe.wait_ge(s["f_y_used"], T)

            transpose_tokens(lambda t: XH[:, t, :], s["g_hT"], s["g_hT_copied"], (s["g_xh"], 1))
            pe.wait_ge(s["g_hT_copied"], G)
            pe.wait_ge(s["g_split"], 1)

            def product(o, wh, wl, xh, xl, start, stop):
                mm(o, wh, xl, start=start, stop=False)
                mm(o, wl, xh, start=False, stop=False)
                return mm(o, wh, xh, start=False, stop=stop)

            def up(x, g, e):
                tok = slice(512 * g, 512 * g + 512)
                for f in range(FC):
                    pe.wait_ge(s["g_gelu"], x * 16 + FC * e + f + 1)
                    product(PS[:, 2 + f, :], W1H[:, e, P * f:P * f + P], W1L[:, e, P * f:P * f + P],
                            CTH[:, tok], CTL[:, tok], True, True).then_inc(s["g_up"], 1)

            def down(x, e):
                pe.wait_ge(s["g_y_read"], x * E1 + e + 1)
                for f in range(FC):
                    pe.wait_ge(s["g_lo"], x * 16 + FC * e + f + 5)
                    n = (FC * e + f) % (2 * FC)
                    last = product(PS[:, 6 + e % 2, :], W2H[:, e, f, :], W2L[:, e, f, :], HMH[:, n, :], HML[:, n, :],
                                   f == 0, f == FC - 1)
                last.then_inc(s["g_y"], 1)

            def weights(x, g, e):
                if e == 0:
                    pe.wait_ge(s["g_cwr"], x + 1)
                elif e >= 2:
                    pe.wait_ge(s["g_cwb"], x * E1 + 2 * e - 2)
                mm(PS[:, int(e == 1), :], SLW[:, e, :], CWT[:, :], start=True, stop=True).then_inc(s["g_cwT"], 1)

            def turn_weights(x):
                pe.wait_ge(s["g_cw"], x + 1)
                pe.wait_ge(s["g_cwb"], x * E1 + 1)
                for t in range(GT):
                    last = tr(PS[0:2 * E1, 0, P * t:P * t + P], GWS[:, t, :].bitcast(F32), IDF)
                last.then_inc(s["g_cwp"], 1)

            def logits(x, g):
                pe.wait_ge(s["g_cur"], x + 1)
                for t in range(GT):
                    last = mm(PS[:, 1, E1 * t:E1 * t + E1], hT[:, 512 * g + P * t:512 * g + P * t + P], WGC[:, :], start=True, stop=True)
                last.then_inc(s["g_lg"], 1)

            pe.wait_ge(s["g_wg"], 1)
            logits(0, 0)
            up(0, 0, 0)
            with pe.Fori(0, R1) as r:
                for g in range(G):
                    x = r * G + g
                    up(x, g, 1)
                    turn_weights(x)
                    down(x, 0)
                    up(x, g, 2)
                    weights(x, g, 0)
                    down(x, 1)
                    weights(x, g, 1)
                    up(x, g, 3)
                    weights(x, g, 2)
                    down(x, 2)
                    if g == G - 1:
                        pe.wait_ge(s["g_wg"], r + 2)
                    pe.wait_ge(s["g_cwb"], x * E1 + 3)
                    logits(x + 1, (g + 1) % G)
                    up(x + 1, (g + 1) % G, 0)
                    weights(x, g, 3)
                    down(x, 3)
            pe.wait_ge(s["g_cur"], R1 * G + G)
            for g in range(G):
                if g >= 2:
                    pe.wait_ge(s["g_last_added"], g - 1)
                for t in range(GT):
                    last = tr(PS[:, 2 + g % 2, P * t:P * t + P], hT[:, 512 * g + P * t:512 * g + P * t + P], IDF)
                last.then_inc(s["g_last"], 1)

        @block.scalar
        def _(act):
            A = nc.scalar.activation
            act.wait_ge(s["small_loaded"], NSMALL)
            A(SC[:, :, :], CT[:, :, :], ACT.Exp, scale=-1.0).then_inc(s["silu_exp"], 1)
            act.wait_ge(s["weights_transposed"], 1)
            A(WT[:, :, :].rearrange("p (a n) c -> p a (n c)", a=2), PS[:, 0:2, :], ACT.Copy).then_inc(s["weights_copied"], 1)
            act.wait_ge(s["mod_ready"], 1)
            A(MODR[:, :, :, :, :].rearrange("p l b k d -> p (l b) (k d)"), PS[:, 4:8, :], ACT.Copy).then_inc(s["mod_rows_copied"], 1)

            def attention(l):
                granules, chunks = sched[l]
                K = len(granules) // 2
                K0 = sum(1 for h, _, _ in granules if h == 0) // 2
                ng = len(granules)
                TRB = PS[:, 7, :].bitcast(BF16)
                scale = float(HD) ** -0.5 if l == 0 else 1.0

                def copy_t(dst, full, count, ready):
                    act.wait_ge(full, count)
                    A(dst, TRB, ACT.Copy).then_inc(ready, 1)

                def copy_k(r, count, head):
                    if head == 0:
                        act.wait_ge(s[f"kT_psum{l}"], count)
                        A(KT[0:64, r, :], TRB[0:64, :], ACT.Copy)
                    else:
                        A(KB[64:P, r, :], TRB[64:P, :], ACT.Copy).then_inc(s[f"kT_ready{l}"], 1)

                act.wait_ge(s[f"init_done{l}"], 1)
                for v in range(LEAD):
                    copy_k(v, v + 1, 0)
                    copy_k(v, v + 1, 1)
                    copy_t(QT[:, v, :], s[f"qT_psum{l}"], v + 1, s[f"qT_ready{l}"])
                copy_t(QT[:, 0, :], s[f"qmT_psum{l}"], 1, s[f"qmT_ready{l}"])
                act.sem_inc(s[f"exp_done{l}"], 2)

                def exp(u, r, g):
                    half, j, q0 = granules[g]
                    if l == 0 and half == 0 and j == 1:
                        q0 = 0
                    act.wait_ge(s[f"st_full{l}"], u * ng + g + 1)
                    act.wait_ge(s[f"pv_done{l}"], u * K + g // 2 - 1 + 2)
                    A(PB[:, g % 4, :, q0:512], PS[:, 2 * (g % 2):2 * (g % 2) + 2, q0:512], ACT.Exp, scale=scale)\
                        .then_inc(s[f"exp_done{l}"], 1)

                def copy_sums(half, groups, count):
                    act.wait_ge(s[f"pv_done{l}"], groups + 1)
                    act.wait_ge(s[f"sel_psum{l}"], count)
                    A(OT[:, half, :], PS[:, 6, :], ACT.Copy).then_inc(s[f"o_copied{l}"], 1)

                def step(u, r):
                    for k in range(K):
                        exp(u, r, 2 * k)
                        e = event_at(l, k)
                        if e == "qm":
                            copy_t(QT[:, (r + 1) % RING, :], s[f"qmT_psum{l}"], u + 2, s[f"qmT_ready{l}"])
                        elif e == "tk":
                            copy_k((r + LEAD) % RING, u + LEAD + 1, 0)
                        elif e == "tq":
                            copy_t(QT[:, (r + LEAD) % RING, :], s[f"qT_psum{l}"], u + LEAD + 1, s[f"qT_ready{l}"])
                        exp(u, r, 2 * k + 1)
                        if e == "tk":
                            copy_k((r + LEAD) % RING, u + LEAD + 1, 1)
                        if k == 0:
                            act.wait_ge(s[f"pv_done{l}"], u * K + 2)
                            A(OT[:, 1, :], PS[:, 6, :], ACT.Copy).then_inc(s[f"o_copied{l}"], 1)
                        elif k == K0:
                            act.wait_ge(s[f"pv_done{l}"], u * K + K0 + 2)
                            act.wait_ge(s[f"sel_psum{l}"], u + 1)
                            A(OT[:, 0, :], PS[:, 6, :], ACT.Copy).then_inc(s[f"o_copied{l}"], 1)
                act.sem_inc(s[f"pv_done{l}"], 1)
                with act.Fori(0, U // RING) as it:
                    for r in range(RING):
                        step(it * RING + r, r)
                act.wait_ge(s[f"pv_done{l}"], U * K + 2)
                A(OT[:, 1, :], PS[:, 6, :], ACT.Copy).then_inc(s[f"o_copied{l}"], 1)

            def copy_hT(full, copied, scale=None, bias=None):
                for g in range(G):
                    act.wait_ge(full, g + 1)
                    if scale is None:
                        A(hT[:, 512 * g:512 * g + 512], PS[:, g % 2, :], ACT.Copy).then_inc(copied, 1)
                    elif bias is None:
                        A(hT[:, 512 * g:512 * g + 512], PS[:, g % 2, :], ACT.Copy, scale=scale(g)).then_inc(copied, 1)
                    else:
                        A(hT[:, 512 * g:512 * g + 512], PS[:, g % 2, :], ACT.Identity, scale=scale(g), bias=bias(g))\
                            .then_inc(copied, 1)

            EPS5 = CST[:, C_EPS:C_EPS + 1]
            EPS6 = CST[:, C_EPS + 1:C_EPS + 2]
            for l in range(2):
                act.wait_ge(s[f"stats_var{l}"], 1)
                A(ST3[:, :], ST2[:, :], ACT.Sqrt, scale=1.0 / D, bias=EPS5).then_inc(s[f"stats_std{l}"], 1)
                act.wait_ge(s["mod_final"], 1)
                copy_hT(s[f"hT_psum{l}"], s[f"hT_copied{l}"],
                        scale=lambda g: MODC[:, l, 1, 2 * g // G:2 * g // G + 1], bias=lambda g: MODC[:, l, 0, 2 * g // G:2 * g // G + 1])
                for t in range(T):
                    act.wait_ge(s[f"proj_psum{l}"], t + 1)
                    bank = 2 + 2 * (t % 3)
                    b0 = PAIRS * (t // TB)
                    tt = 16 * (t % TB)
                    src = PS[:, bank, 0:384].rearrange("p (s r c) -> p r s c", s=3, r=PAIRS)
                    dst = QU[:, b0:b0 + PAIRS, :, tt:tt + 16]
                    if l == 0:
                        A(dst, src, ACT.Copy).then_inc(s["proj_copied0"], 1)
                    else:
                        A(dst[:, :, 0, :], src[:, :, 0, :], ACT.Copy, scale=TEMP[:, :])
                        A(dst[:, :, 1:3, :], src[:, :, 1:3, :], ACT.Copy)
                        A(C5[:, b0:b0 + PAIRS, :, 10 * (t % TB):10 * (t % TB) + 10],
                          PS[:, bank + 1, 0:160].rearrange("p (s r c) -> p r s c", s=2, r=PAIRS), ACT.Copy)\
                            .then_inc(s["proj_copied1"], 1)
                attention(l)
                copy_hT(s[f"aT_psum{l}"], s[f"aT_copied{l}"])
                if l == 0:
                    act.wait_ge(s["f_stats"], 1)
                    A(ST3[:, :], ST2[:, :], ACT.Sqrt, scale=1.0 / D, bias=EPS5).then_inc(s["f_std"], 1)
                    act.wait_ge(s["f_stats"], 2)
                    A(ST3[:, :], ST2[:, :], ACT.Sqrt, scale=1.0 / D, bias=EPS6).then_inc(s["f_std"], 1)
                    copy_hT(s["f_hT_psum"], s["f_hT_copied"], scale=lambda g: FCOL[:, 0:1])
                    for g in range(G):
                        act.wait_ge(s["f_lat"], g + 1)
                        A(LT[0:L, 512 * g:512 * g + 512], PS[0:L, 2 + g % 2, :], ACT.Identity, bias=FCOL[0:L, 2:3])\
                            .then_inc(s["f_lat_copied"], 1)
                    for t in range(T):
                        act.wait_ge(s["f_qkv"], t + 1)
                        A(QF[:, t, :], PS[:, 4 + t % 4, 0:384], ACT.Copy).then_inc(s["f_qkv_copied"], 1)
                    for c in range(2):
                        act.wait_ge(s["f_scmax"], c + 1)
                        half = SCR[:, TB * c:TB * c + TB, :, :].rearrange("p t h g -> p (t h g)")
                        A(half, half, ACT.Exp, scale=float(HD) ** -0.5).then_inc(s["f_exp"], 1)
                    copy_hT(s["f_oT"], s["f_oT_copied"])
                    act.wait_ge(s["f_stats"], 3)
                    A(ST3[:, :], ST2[:, :], ACT.Sqrt, scale=1.0 / D, bias=EPS6).then_inc(s["f_std"], 1)
                    copy_hT(s["f_h2T"], s["f_h2T_copied"], scale=lambda g: FCOL[:, 1:2])
                    act.wait_ge(s["f_gexp_in"], 1)
                    A(GW[:, :, :], GW[:, :, :], ACT.Exp).then_inc(s["f_gexp"], 1)
            act.wait_ge(s["g_stats"], 1)
            A(ST3[:, :], ST2[:, :], ACT.Sqrt, scale=1.0 / D, bias=EPS5).then_inc(s["g_std"], 1)
            act.wait_ge(s["att_ready1"], U + 2)
            A(W1H[:, :, :].rearrange("p e n -> p (e n)"), W1[:, :, :].rearrange("p e n -> p (e n)"), ACT.Copy)
            A(W2H[:, :, :, :].rearrange("p e f n -> p (e f n)"), W2[:, :, :, :].rearrange("p e f n -> p (e f n)"), ACT.Copy)\
                .then_inc(s["g_high"], 1)
            copy_hT(s["g_hT"], s["g_hT_copied"],
                    scale=lambda g: MODC[:, 1, 3, 2 * g // G:2 * g // G + 1], bias=lambda g: MODC[:, 1, 2, 2 * g // G:2 * g // G + 1])
            act.sem_inc(s["g_gelu"], 4)
            def gelu(x, e):
                for f in range(FC):
                    n = FC * e + f
                    act.wait_ge(s["g_up"], x * 16 + n + 1)
                    act.wait_ge(s["g_lo"], x * 16 + n + 1)
                    A(HMF[:, f, :], PS[:, 2 + f, :], ACT.Gelu_apprx_tanh, bias=B1[:, e, f:f + 1])
                    if f == 0:
                        act.wait_ge(s["g_y"], x * E1 + e + 1)
                    A(HMH[:, n % (2 * FC), :], PS[:, 2 + f, :], ACT.Gelu_apprx_tanh, bias=B1[:, e, f:f + 1])\
                        .then_inc(s["g_gelu"], 1)

            def tanh(x, g):
                act.wait_ge(s["g_tanh_in"], x + 1)
                A(GW[:, GT * g:GT * g + GT, E1:2 * E1], GW[:, GT * g:GT * g + GT, E1:2 * E1], ACT.Tanh).then_inc(s["g_tanh"], 1)

            gelu(0, 0)
            tanh(0, 0)
            with act.Fori(0, R1) as r:
                for g in range(G):
                    x = r * G + g
                    gelu(x, 1)
                    gelu(x, 2)
                    gelu(x, 3)
                    gelu(x + 1, 0)
                    tanh(x + 1, (g + 1) % G)

        @block.vector
        def _(dve):
            V = nc.vector
            step_n = [0]

            def link(ins):
                step_n[0] += 1
                ins.then_inc(s["dve_step"], 1)
                dve.wait_ge(s["dve_step"], step_n[0])

            V.memset(ONES[:, :], 1.0)
            V.memset(QU[:, U:U + LEAD, :, :].rearrange("p u s x -> p (u s x)"), 0.0)
            V.memset(SV[:, U:U + LEAD, :].rearrange("p u x -> p (u x)"), 0.0)
            V.memset(PBF, 1.0)
            V.memset(VA[:, :, :, :].rearrange("p r x c -> p (r x) c"), 0.0)
            V.memset(OT[:, :, :].rearrange("p a n -> p (a n)"), 1.0)
            V.memset(LT[L:L + 1, :], 1.0)
            V.memset(WG1[:, R1, :], 0.0)
            V.memset(BG1[:, R1, :], 0.0)
            link(V.memset(ST1[:, :], 0.0))
            link(V.memset(VA[:, :, :, HD:HD + 1].rearrange("p r x c -> p (r x) c"), 1.0))
            dve.wait_ge(s["small_loaded"], NSMALL)
            V.tensor_copy(IDB[:, :], CST[:, C_ID:C_ID + P])
            V.tensor_copy(MQB[:, :], CST[:, C_MQ:C_MQ + P])
            link(V.tensor_copy(MSB[:, :], CST[:, C_MS:C_MS + 2 * P]))
            dve.wait_ge(s["silu_exp"], 1)
            link(V.tensor_scalar_add(SC2[:, :, :], SC[:, :, :], 1.0))
            link(V.reciprocal(SC[:, :, :], SC2[:, :, :]))
            link(V.tensor_tensor(SC2[:, :, :], CT[:, :, :], SC[:, :, :], ALU.mult))
            V.tensor_copy(SCB[:, :, :, :].rearrange("p l b n -> p (l b) n"),
                          to3(SC2[:, :, :].rearrange("p l b -> p (l b)"), P)).then_inc(s["silu_ready"], 1)
            dve.wait_ge(s["rep_ready"], 1)
            for n in range(2):
                last = V.tensor_tensor(BD[:, n, :, :], to3(CST[:, C_HM:C_HM + H], 5),
                                       PS[:, 2, 5 * n:5 * n + 5].unsqueeze(1).broadcast_to([P, H, 5]), ALU.mult)
            last.then_inc(s["bd_ready"], 1)
            dve.wait_ge(s["w3_ready"], 1)
            V.tensor_copy(W3[:, :], PS[:, 2, 16:176])
            for n in range(2):
                last = V.tensor_tensor(BR[0:1, 384 + 80 * n:464 + 80 * n].rearrange("p (h c) -> p h c", h=H),
                                       PS[0:1, 3, 80 * n:80 * n + 80].rearrange("p (h c) -> p h c", h=H),
                                       BS5[0:1, 5 * n:5 * n + 5].unsqueeze(1).broadcast_to([1, H, 5]), ALU.add)
            last.then_inc(s["w3_copied"], 1)
            dve.wait_ge(s["mod_ready"], 1)
            link(V.tensor_copy(MODC[:, :, :, :].rearrange("p l n b -> p (l n b)"), PS[:, 3, 256:272]))
            for l in range(2):
                V.tensor_scalar_add(MODC[:, l, 1:4:2, :], MODC[:, l, 1:4:2, :], 1.0)
            dve.wait_ge(s["mod_rows_copied"], 1)
            MR = MODR[:, :, :, :, :].rearrange("p l b k d -> p (l b) k d")
            SG = SGN[:, :, :, :].rearrange("p l b d -> p (l b) d")
            for k in (0, 3):
                link(V.tensor_scalar(SG, MR[:, :, k, :], 0.0, 2.0, ALU.is_ge, ALU.mult))
                link(V.tensor_scalar(SG, SG, -1.0, None, ALU.add))
                link(V.tensor_tensor(MR[:, :, k, :], MR[:, :, k, :], SG, ALU.mult))
                link(V.tensor_scalar(MR[:, :, k, :], MR[:, :, k, :], 0.25, None, ALU.max))
                link(V.tensor_tensor(MR[:, :, k, :], MR[:, :, k, :], SG, ALU.mult))
            link(V.tensor_scalar(MR[:, :, 2, :], MR[:, :, 2, :], 1.0, None, ALU.add))
            dve.sem_inc(s["mod_final"], 1)

            def batch_row(l, b, k):
                return MODR[:, l, b, k, :].unsqueeze(1).broadcast_to([P, TB, D])

            def layernorm(var, std, ready):
                for t in range(T):
                    last = V.bn_stats(STAT[:, t, :], X[:, t, :])
                link(last)
                V.tensor_tensor(ST1[:, :], STAT[:, :, 1], STAT[:, :, 4], ALU.subtract)
                V.tensor_tensor(ST2[:, :], STAT[:, :, 2], STAT[:, :, 5], ALU.add)
                link(V.tensor_tensor(ST4[:, :], STAT[:, :, 1], STAT[:, :, 4], ALU.add))
                V.tensor_scalar(ST4[:, :], ST4[:, :], 0.5, None, ALU.mult)
                link(V.tensor_tensor(ST1[:, :], ST1[:, :], ST1[:, :], ALU.mult))
                link(V.scalar_tensor_tensor(ST2[:, :], ST1[:, :], D / 4.0, ST2[:, :], ALU.mult, ALU.add))
                dve.sem_inc(var, 1)
                link(V.tensor_tensor(XH[:, :, :], X[:, :, :], to3(ST4[:, :], D), ALU.subtract))
                dve.wait_ge(*std)
                link(V.reciprocal(ST1[:, :], ST3[:, :]))
                link(V.tensor_tensor(XH[:, :, :], XH[:, :, :], to3(ST1[:, :], D), ALU.mult))
                if ready is not None:
                    dve.sem_inc(ready, 1)

            def rmsnorm(var, std, ready):
                link(V.tensor_tensor(XH[:, :, :], HX[:, :, :], HX[:, :, :], ALU.mult))
                link(V.tensor_reduce(ST2[:, :], XH[:, :, :], AX.X, ALU.add))
                dve.sem_inc(var, 1)
                dve.wait_ge(*std)
                link(V.reciprocal(ST1[:, :], ST3[:, :]))
                link(V.tensor_tensor(XH[:, :, :], HX[:, :, :], to3(ST1[:, :], D), ALU.mult))
                dve.sem_inc(ready, 1)

            def modulate(l):
                for b in range(B):
                    t = slice(TB * b, TB * b + TB)
                    V.tensor_tensor(HX[:, t, :], XH[:, t, :], batch_row(l, b, 2), ALU.mult)
                link(V.memset(ST1[:, :], 0.0))
                for b in range(B):
                    t = slice(TB * b, TB * b + TB)
                    last = V.tensor_tensor(HX[:, t, :], HX[:, t, :], batch_row(l, b, 1), ALU.add)
                link(last)

            def attention(l):
                granules, chunks = sched[l]
                K = len(granules) // 2
                nch = len(chunks)

                def reduce(u, r, n):
                    i, a, c, w = chunks[n]
                    dve.wait_ge(s[f"mx_full{l}"], u * nch + n + 1)
                    V.tensor_reduce((NMA, NMB)[c][:, r, 2 * i + a:2 * i + a + 1], PS[:, 4 + n % 2, 0:w], AX.X, ALU.max, negate=True)\
                        .then_inc(s[f"mx_reduced{l}"], 1)

                def combine(u, r):
                    dve.wait_ge(s[f"mx_reduced{l}"], u * nch + nch)
                    if l == 0:
                        V.tensor_copy(NM[:, r, 0:TB], NMA[:, r, 0:TB])
                    lo = TB if l == 0 else 0
                    V.tensor_tensor(NM[:, r, lo:2 * TB], NMA[:, r, lo:2 * TB], NMB[:, r, lo:2 * TB], ALU.min)\
                        .then_inc(s[f"nm_ready{l}"], 1)

                def normalise(u, count):
                    o = PS[:, 7, 0:TB * KEYW].rearrange("p (t c) -> p t c", c=KEYW)
                    dve.wait_ge(s[f"sel_psum{l}"], count)
                    V.reciprocal(RD[:, :, :], o[:, :, 2 * HD:KEYW]).then_inc(s[f"init_done{l}"], 1)
                    dve.wait_ge(s[f"init_done{l}"], count + 1)
                    V.tensor_tensor(ATT[:, u, :, :].rearrange("p t (a d) -> p t a d", a=2),
                                    o[:, :, 0:2 * HD].rearrange("p t (a d) -> p t a d", a=2),
                                    RD[:, :, :].unsqueeze(3).broadcast_to([P, TB, 2, HD]), ALU.mult)\
                        .then_inc(s[f"att_ready{l}"], 1)

                for v in range(2):
                    for n in range(nch):
                        reduce(v, v, n)
                    combine(v, v)

                def step(u, r):
                    for k in range(K):
                        n0, n1 = nch * k // K, nch * (k + 1) // K
                        for n in range(n0, n1):
                            reduce(u + 2, (r + 2) % RING, n)
                            if n == n0 + 1 and event_at(l, k) == "sel":
                                normalise(u, u + 1)
                    combine(u + 2, (r + 2) % RING)

                with dve.Fori(0, U // RING) as it:
                    for r in range(RING):
                        step(it * RING + r, r)
                normalise(U, U + 1)
                dve.wait_ge(s[f"att_ready{l}"], U + 1)
                for b in range(B):
                    last = V.tensor_copy(XH[:, TB * b:TB * b + TB, :].rearrange("p t (u c) -> p u t c", u=PAIRS),
                                         ATT[:, 1 + PAIRS * b:1 + PAIRS * b + PAIRS, :, :])
                last.then_inc(s[f"att_ready{l}"], 1)

            def residual(l, full, added, k):
                for g in range(G):
                    dve.wait_ge(full, g + 1)
                    t = slice(GT * g, GT * g + GT)
                    b = GT * g // TB
                    link(V.tensor_tensor(XH[:, t, :], PS[:, 2 + g % 2, :].rearrange("p (t d) -> p t d", t=GT),
                                         MODR[:, l, b, k, :].unsqueeze(1).broadcast_to([P, GT, D]), ALU.mult))
                    dve.sem_inc(added, 1)
                    link(V.tensor_tensor(X[:, t, :], X[:, t, :], XH[:, t, :], ALU.add))

            for l in range(2):
                if l == 0:
                    dve.wait_ge(s["x_loaded"], 16)
                layernorm(s[f"stats_var{l}"], (s[f"stats_std{l}"], 1), s[f"xhat_ready{l}"])
                if l == 0:
                    dve.wait_ge(s["proj_copied0"], T)
                    w = QU[:, 0:U, 0:2, :].rearrange("p u s x -> p u (s x)").rearrange("p u (x e) -> p u x e", e=HD)
                    lo, hi = w[:, :, :, 0:4], w[:, :, :, 4:8]
                    cos = CST[:, C_COS:C_COS + P].rearrange("p (x e) -> p x e", e=4).unsqueeze(1).broadcast_to([P, U, 32, 4])
                    sin = CST[:, C_SIN:C_SIN + P].rearrange("p (x e) -> p x e", e=4).unsqueeze(1).broadcast_to([P, U, 32, 4])
                    t1 = XH[:, :, :].rearrange("p t (x e) -> p t x e", e=4)
                    t2 = HX[:, :, :].rearrange("p t (x e) -> p t x e", e=4)
                    V.tensor_tensor(t1, lo, sin, ALU.mult)
                    link(V.tensor_tensor(t2, hi, sin, ALU.mult))
                    V.tensor_tensor(lo, lo, cos, ALU.mult)
                    link(V.tensor_tensor(hi, hi, cos, ALU.mult))
                    V.tensor_tensor(lo, lo, t2, ALU.subtract)
                    link(V.tensor_tensor(hi, hi, t1, ALU.add))
                    dve.sem_inc(s["operands_ready0"], 1)
                else:
                    dve.wait_ge(s["proj_copied1"], T)
                    a5 = C5[:, :, 0, :].rearrange("p u (x c) -> p u x c", c=5)
                    b5 = C5[:, :, 1, :].rearrange("p u (x c) -> p u x c", c=5)
                    t1 = XH[:, :, :].rearrange("p t d -> p (t d)")[:, 0:U * 48].rearrange("p (u x c) -> p u x c", u=U, c=3)
                    t2 = HX[:, :, :].rearrange("p t (x e) -> p t x e", e=HD)
                    cr = CR[:, 0:U, :, :]
                    V.tensor_tensor(t1, a5[:, :, :, 2:5], b5[:, :, :, 1:4], ALU.mult)
                    link(V.tensor_tensor(cr, a5[:, :, :, 1:4], b5[:, :, :, 2:5], ALU.mult))
                    link(V.tensor_tensor(cr, cr, t1, ALU.subtract))
                    kk = QU[:, 0:U, 1, :].rearrange("p u (x e) -> p u x e", e=HD)
                    for c in range(3):
                        link(V.tensor_tensor(t2, cr[:, :, :, c].unsqueeze(3).broadcast_to([P, U, 16, HD]),
                                             WQS[:, c, :].unsqueeze(1).unsqueeze(1).broadcast_to([P, U, 16, HD]), ALU.mult))
                        link(V.tensor_tensor(kk, kk, t2, ALU.add))
                    link(V.tensor_tensor(cr, cr, BQS[:, :].unsqueeze(1).unsqueeze(1).broadcast_to([P, U, 16, 3]), ALU.mult))
                    link(V.tensor_reduce(SV[:, 0:U, :], cr, AX.X, ALU.add))
                    link(V.tensor_scalar(SV[:, 0:U, :], SV[:, 0:U, :], TEMP[:, 0:1], None, ALU.mult))
                    V.memset(PBF, 1.0)
                    V.memset(VA[:, :, :, :].rearrange("p r x c -> p (r x) c"), 0.0)
                    link(V.memset(ST1[:, :], 0.0))
                    link(V.memset(VA[:, :, :, HD:HD + 1].rearrange("p r x c -> p (r x) c"), 1.0))
                    V.memset(QU[:, U:U + LEAD, :, :].rearrange("p u s x -> p (u s x)"), 0.0)
                    link(V.memset(ST1[:, :], 0.0))
                    dve.sem_inc(s["operands_ready1"], 1)
                V.memset(KT[64:P, :, :].rearrange("p r n -> p (r n)"), 0.0)
                link(V.memset(KB[0:64, :, :].rearrange("p r n -> p (r n)"), 0.0))
                dve.sem_inc(s[f"init_done{l}"], 1)
                attention(l)
                residual(l, s[f"o_psum{l}"], s[f"o_added{l}"], 0)

                if l == 0:
                    layernorm(s["f_stats"], (s["f_std"], 1), None)
                    modulate(0)
                    rmsnorm(s["f_stats"], (s["f_std"], 2), s["f_h"])
                    dve.wait_ge(s["f_qkv_copied"], T)

                    def pair_products(dst, t):
                        q = QF[:, t, 0:P].rearrange("p (h d) -> p h d", h=H).unsqueeze(2).broadcast_to([P, H, H, HD])
                        kk = QF[:, t, P:3 * P].rearrange("p (g e) -> p g e", g=H)[:, :, 0:HD].unsqueeze(1).broadcast_to([P, H, H, HD])
                        return V.tensor_tensor(dst, q, kk, ALU.mult)

                    def value_products(dst, t):
                        pr = SCR[:, t, :, :].unsqueeze(2).broadcast_to([P, H, HD, H])
                        vv = QF[:, t, P:3 * P].rearrange("p (g e) -> p e g", g=H)[:, HD:2 * HD, :].unsqueeze(1).broadcast_to([P, H, HD, H])
                        return V.tensor_tensor(dst.rearrange("p h g d -> p (h g d)").rearrange("p (h d g) -> p h d g", h=H, d=HD), pr, vv, ALU.mult)

                    for t in range(0, T, 2):
                        link(pair_products(PRD[:, 0, :, :, :], t))
                        link(V.tensor_reduce(SCR[:, t, :, :], PRD[:, 0, :, :, :], AX.X, ALU.add))
                        dve.wait_ge(s["f_prod"], t // 2 + 1)
                        pb = (PRD[:, 1], PRP)[t // 2 % 2]
                        V.tensor_reduce(SCR[:, t + 1, :, :], pb, AX.X, ALU.add).then_inc(s["f_prod_used"], 1)
                    link(V.memset(ST1[:, :], 0.0))
                    scr = SCR[:, :, :, :].rearrange("p t h g -> p (t h) g")
                    for c in range(2):
                        hf = slice(TB * H * c, TB * H * c + TB * H)
                        link(V.tensor_reduce(SCM[:, hf], scr[:, hf, :], AX.X, ALU.max))
                        link(V.tensor_tensor(scr[:, hf, :], scr[:, hf, :], to3(SCM[:, hf], H), ALU.subtract))
                        dve.sem_inc(s["f_scmax"], 1)
                    for c in range(2):
                        hf = slice(TB * H * c, TB * H * c + TB * H)
                        dve.wait_ge(s["f_exp"], c + 1)
                        link(V.tensor_reduce(SCL[:, hf], scr[:, hf, :], AX.X, ALU.add))
                    link(V.reciprocal(SCM[:, :], SCL[:, :]))
                    for t in range(0, T, 2):
                        link(value_products(PRD[:, 0, :, :, :], t))
                        dd = PRD[:, 0].rearrange("p h g d -> p (h g d)").rearrange("p (x g) -> p x g", g=H)
                        link(V.tensor_reduce(XH[:, t, :], dd, AX.X, ALU.add))
                        dve.wait_ge(s["f_prod"], TB + t // 2 + 1)
                        pb = (PRD[:, 1], PRP)[t // 2 % 2].rearrange("p h g d -> p (h g d)").rearrange("p (x g) -> p x g", g=H)
                        V.tensor_reduce(XH[:, t + 1, :], pb, AX.X, ALU.add).then_inc(s["f_prod_used"], 1)
                    link(V.memset(ST1[:, :], 0.0))
                    xo = XH[:, :, :].rearrange("p t (h d) -> p (t h) d", h=H)
                    link(V.tensor_tensor(xo, xo, to3(SCM[:, :], HD), ALU.mult))
                    dve.sem_inc(s["f_out"], 1)
                    for g in range(G):
                        dve.wait_ge(s["f_o"], g + 1)
                        t = slice(GT * g, GT * g + GT)
                        link(V.tensor_tensor(HX[:, t, :], HX[:, t, :], PS[:, 2 + g % 2, :].rearrange("p (t d) -> p t d", t=GT), ALU.add))
                        dve.sem_inc(s["f_x2"], 1)
                    rmsnorm(s["f_stats"], (s["f_std"], 3), s["f_h2"])
                    dve.wait_ge(s["f_gate"], 1)
                    lg = PS[:, 0, 0:T * E0].rearrange("p (t e) -> p t e", e=E0)
                    link(V.tensor_tensor(GW[:, :, :], lg, BG0[:, :].unsqueeze(1).broadcast_to([P, T, E0]), ALU.add))
                    link(V.tensor_reduce(GW2[:, :], GW[:, :, :], AX.X, ALU.max))
                    link(V.tensor_tensor(GW[:, :, :], GW[:, :, :], to3(GW2[:, :], E0), ALU.subtract))
                    dve.sem_inc(s["f_gexp_in"], 1)
                    dve.wait_ge(s["f_gexp"], 1)
                    link(V.tensor_reduce(GW2[:, :], GW[:, :, :], AX.X, ALU.add))
                    link(V.reciprocal(GW3[:, :], GW2[:, :]))
                    link(V.tensor_tensor(GW[:, :, :], GW[:, :, :], to3(GW3[:, :], E0), ALU.mult))
                    for t in range(T):
                        dve.wait_ge(s["f_y"], t + 1)
                        for e in range(E0):
                            ins = V.scalar_tensor_tensor(HX[:, t, :], PS[:, 2 + 2 * (t % 3) + e // 4, P * (e % 4):P * (e % 4) + P],
                                                         GW[:, t, e:e + 1], HX[:, t, :], ALU.mult, ALU.add)
                            link(ins)
                        dve.sem_inc(s["f_y_used"], 1)
                    for b in range(B):
                        t = slice(TB * b, TB * b + TB)
                        last = V.tensor_tensor(HX[:, t, :], HX[:, t, :], batch_row(0, b, 3), ALU.mult)
                    link(last)
                    link(V.tensor_tensor(X[:, :, :], X[:, :, :], HX[:, :, :], ALU.add))

            layernorm(s["g_stats"], (s["g_std"], 1), s["g_xh"])
            dve.wait_ge(s["g_high"], 1)
            V.tensor_tensor(W1L[:, :, :].rearrange("p e n -> p (e n)"), W1[:, :, :].rearrange("p e n -> p (e n)"),
                            W1H[:, :, :].rearrange("p e n -> p (e n)").bitcast(F32), ALU.subtract)
            V.tensor_tensor(W2L[:, :, :, :].rearrange("p e f n -> p (e f n)"), W2[:, :, :, :].rearrange("p e f n -> p (e f n)"),
                            W2H[:, :, :, :].rearrange("p e f n -> p (e f n)").bitcast(F32), ALU.subtract).then_inc(s["g_split"], 1)
            dve.sem_inc(s["g_cwb"], 1)
            dve.sem_inc(s["g_lo"], 4)
            dve.sem_inc(s["g_y"], 2)
            dve.sem_inc(s["g_y_read"], 2)
            dve.sem_inc(s["g_acc"], 2)
            cnt = [0]

            def glink(ins, base):
                cnt[0] += 1
                ins.then_inc(s["g_step"], 1)
                dve.wait_ge(s["g_step"], base + cnt[0])

            def gate(r, base):
                V.tensor_copy(WGC[:, :], WG1[:, r, :]).then_inc(s["g_wg"], 1)
                glink(V.tensor_copy(ST1[:, 0:E1], BG1[:, r, :]), base)

            def choose(x, g, base):
                t = slice(GT * g, GT * g + GT)
                lw, th = GW[:, t, 0:E1], GW[:, t, E1:2 * E1]
                tie = CST[:, C_TIE:C_TIE + 16].rearrange("p (e f) -> p e f", e=E1).unsqueeze(1).broadcast_to([P, GT, E1, E1])
                dve.wait_ge(s["g_lg"], x + 1)
                glink(V.tensor_tensor(lw, PS[:, 1, 0:GT * E1].rearrange("p (t e) -> p t e", e=E1),
                                      ST1[:, 0:E1].unsqueeze(1).broadcast_to([P, GT, E1]), ALU.add), base)
                mine = lw.unsqueeze(3).broadcast_to([P, GT, E1, E1])
                other = lw.unsqueeze(2).broadcast_to([P, GT, E1, E1])
                V.tensor_tensor(CMP[:, :, :, :], other, mine, ALU.is_gt)
                glink(V.tensor_tensor(CEQ[:, :, :, :], other, mine, ALU.is_equal), base)
                glink(V.tensor_tensor(CEQ[:, :, :, :], CEQ[:, :, :, :], tie, ALU.mult), base)
                glink(V.tensor_tensor(CMP[:, :, :, :], CMP[:, :, :, :], CEQ[:, :, :, :], ALU.add), base)
                glink(V.tensor_reduce(th, CMP[:, :, :, :], AX.X, ALU.add), base)
                glink(V.tensor_scalar(SELE[:, :, :], th, 1.5, None, ALU.is_lt), base)
                glink(V.tensor_tensor(SELL[:, :, :], SELE[:, :, :], lw, ALU.mult), base)
                glink(V.tensor_reduce(GW2[:, 0:GT], SELL[:, :, :], AX.X, ALU.add), base)
                glink(V.tensor_scalar(GW2[:, 0:GT], GW2[:, 0:GT], 0.5, None, ALU.mult), base)
                glink(V.tensor_tensor(th, lw, to3(GW2[:, 0:GT], E1), ALU.subtract), base)
                dve.sem_inc(s["g_tanh_in"], 1)

            def chosen_weights(x, g, base):
                t = slice(GT * g, GT * g + GT)
                lw, th = GW[:, t, 0:E1], GW[:, t, E1:2 * E1]
                dve.wait_ge(s["g_tanh"], x + 1)
                glink(V.tensor_scalar(th, th, 0.5, 0.5, ALU.mult, ALU.add), base)
                glink(V.tensor_tensor(lw, th, SELE[:, :, :], ALU.mult), base)
                glink(V.tensor_copy(GWS[:, :, 0:E1], lw), base)
                V.tensor_tensor(GWS[:, :, E1:2 * E1], lw, GWS[:, :, 0:E1].bitcast(F32), ALU.subtract).then_inc(s["g_cw"], 1)

            def rows_of_weights(x):
                dve.wait_ge(s["g_cwp"], x + 1)
                V.tensor_copy(CWT[:, :], PS[0:2 * E1, 0, :]).then_inc(s["g_cwr"], 1)

            def lows(x, e):
                for f in range(FC):
                    n = FC * e + f
                    dve.wait_ge(s["g_gelu"], x * 16 + n + 5)
                    V.tensor_tensor(HML[:, n % (2 * FC), :], HMF[:, f, :], HMH[:, n % (2 * FC), :].bitcast(F32), ALU.subtract)\
                        .then_inc(s["g_lo"], 1)

            def spread(x, e):
                dve.wait_ge(s["g_cwT"], x * E1 + e + 1)
                dve.wait_ge(s["g_y_read"], x * E1 + e + 1)
                V.tensor_copy(CWB[:, e % 2, :], PS[:, int(e == 1), :]).then_inc(s["g_cwb"], 1)

            def weigh(x, e):
                dve.wait_ge(s["g_y"], x * E1 + e + 3)
                dve.wait_ge(s["g_cwb"], x * E1 + e + 2)
                dve.wait_ge(s["g_acc"], x * E1 + e + 1)
                V.scalar_tensor_tensor(YS[:, e % 2, :], PS[:, 6 + e % 2, :], B2C[:, e:e + 1], CWB[:, e % 2, :], ALU.add, ALU.mult)\
                    .then_inc(s["g_y_read"], 1)

            V.tensor_tensor(SLW[:, :, :], to3(IDF[0:2 * E1, 0:E1], P), to3(IDF[0:2 * E1, E1:2 * E1], P), ALU.add)
            gate(0, 0)
            choose(0, 0, 0)
            lows(0, 0)
            ahead = cnt[0]
            with dve.Fori(0, R1) as r:
                cnt[0] = 0
                base = r * (1 + G * 13) + ahead
                for g in range(G):
                    x = r * G + g
                    chosen_weights(x, g, base)
                    lows(x, 1)
                    rows_of_weights(x)
                    lows(x, 2)
                    spread(x, 0)
                    weigh(x, 0)
                    spread(x, 1)
                    weigh(x, 1)
                    lows(x, 3)
                    spread(x, 2)
                    weigh(x, 2)
                    if g == G - 1:
                        gate(r + 1, base)
                    choose(x + 1, (g + 1) % G, base)
                    lows(x + 1, 0)
                    spread(x, 3)
                    weigh(x, 3)
                assert cnt[0] == 1 + G * 13, cnt[0]
            for g in range(G):
                dve.wait_ge(s["g_last"], g + 1)
                t = slice(GT * g, GT * g + GT)
                link(V.tensor_tensor(XH[:, t, :], PS[:, 2 + g % 2, :].rearrange("p (t d) -> p t d", t=GT),
                                     MODR[:, 1, GT * g // TB, 3, :].unsqueeze(1).broadcast_to([P, GT, D]), ALU.mult))
                dve.sem_inc(s["g_last_added"], 1)
                V.tensor_tensor(X[:, t, :], X[:, t, :], XH[:, t, :], ALU.add).then_inc(s["g_fin"], 1)

        @block.gpsimd
        def _(pool):
            Q = nc.gpsimd
            pn = [0]

            def plink(ins):
                pn[0] += 1
                ins.then_inc(s["pool_init"], 1)
                pool.wait_ge(s["pool_init"], pn[0])
            Q.memset(QA[:, :, :, :].rearrange("p r x c -> p (r x c)"), 0.0)
            plink(Q.memset(KA[:, :, :, :].rearrange("p r x c -> p (r x c)"), 0.0))
            Q.memset(QA[:, :, :, 48:ROWS].rearrange("p r x c -> p (r x) c"), 1.0)
            plink(Q.memset(KA[:, :, :, ROWS:ROWSM].rearrange("p r x c -> p (r x) c"), 1.0))

            for l in range(2):
                per = [0]

                def pwait(sm, value):
                    pool.wait_ge(sm, value)
                    pool.sem_inc(s["pool_passed"], 1)

                def split(src, dst, at, base):
                    w = src.shape[2]
                    rest = RQ[:, :, 0:w]
                    cur = src
                    for n in range(3):
                        part = dst[:, :, at[n]:at[n] + w]
                        plinku(Q.tensor_copy(part, cur), base)
                        if n < 2:
                            plinku(Q.tensor_tensor(rest, cur, part, ALU.subtract), base)
                            cur = rest

                def plinku(ins, base):
                    per[0] += 1
                    ins.then_inc(s[f"pool_step{l}"], 1)
                    pwait(s[f"pool_step{l}"], base + per[0])

                def build_k(u, r, base):
                    kk = QU[:, u, 1, :].rearrange("p (x e) -> p x e", e=HD)
                    dst = KA[:, r, :, :]
                    split(kk, dst, (0, HD, 2 * HD), base)
                    Q.tensor_copy(dst[:, :, 3 * HD:5 * HD], dst[:, :, 0:2 * HD])
                    if l == 1:
                        plinku(Q.tensor_copy(dst[:, :, 5 * HD:6 * HD], dst[:, :, 0:HD]), base)
                        split(SV[:, u, :].unsqueeze(2), dst, (48, 49, 50), base)
                        Q.tensor_copy(RM[:, 0:1], RM[:, 1:2]).then_inc(s[f"k_built{l}"], 1)
                    else:
                        Q.tensor_copy(dst[:, :, 5 * HD:6 * HD], dst[:, :, 0:HD]).then_inc(s[f"k_built{l}"], 1)

                def build_qv(u, r, base):
                    qq = QU[:, u, 0, :].rearrange("p (x e) -> p x e", e=HD)
                    dst = QA[:, r, :, :]
                    split(qq, dst, (0, 3 * HD, 5 * HD), base)
                    Q.memset(dst[:, :, ROWS:ROWSM], 0.0)
                    Q.tensor_copy(dst[:, :, HD:2 * HD], dst[:, :, 0:HD])
                    Q.tensor_copy(dst[:, :, 2 * HD:3 * HD], dst[:, :, 0:HD])
                    Q.tensor_copy(dst[:, :, 4 * HD:5 * HD], dst[:, :, 3 * HD:4 * HD])
                    Q.tensor_copy(VA[:, r, :, 0:HD], QU[:, u, 2, :].rearrange("p (x e) -> p x e", e=HD))\
                        .then_inc(s[f"qv_built{l}"], 1)

                def build_m(u, r, base):
                    pwait(s[f"nm_ready{l}"], u + 1)
                    split(NM[:, r, :].unsqueeze(2), QA[:, r, :, :], (51, 52, 53), base)
                    Q.tensor_copy(RM[:, 0:1], RM[:, 1:2]).then_inc(s[f"mparts_built{l}"], 1)

                plink(Q.memset(RM[:, :], 0.0))
                pool.wait_ge(s[f"operands_ready{l}"], 1)
                for v in range(LEAD):
                    build_k(v, v, 0)
                    build_qv(v, v, 0)
                build_m(0, 0, 0)
                start = per[0]
                one = (5 + (6 if l == 1 else 0)) + 5 + 5

                def step(u, r, base):
                    per[0] = 0
                    build_m(u + 1, (r + 1) % RING, base)
                    pwait(s[f"qmT_psum{l}"], u + 1)
                    build_k(u + LEAD, (r + LEAD) % RING, base)
                    pwait(s[f"pv_done{l}"], u * (len(sched[l][0]) // 2) + 2)
                    build_qv(u + LEAD, (r + LEAD) % RING, base)
                    assert per[0] == one, per[0]

                with pool.Fori(0, U // RING) as it:
                    for r in range(RING):
                        u = it * RING + r
                        step(u, r, u * one + start)
                if l == 0:
                    pool.wait_ge(s["f_qkv_copied"], T)
                    pool.wait_ge(s["att_ready0"], U + 1)
                    for n in range(T):
                        t = 2 * (n % TB) + 1
                        dst = (PRD[:, 1], PRP)[n % 2]
                        if n >= 2:
                            pool.wait_ge(s["f_prod_used"], n - 1)
                        if n < TB:
                            q = QF[:, t, 0:P].rearrange("p (h d) -> p h d", h=H).unsqueeze(2).broadcast_to([P, H, H, HD])
                            kk = QF[:, t, P:3 * P].rearrange("p (g e) -> p g e", g=H)[:, :, 0:HD].unsqueeze(1).broadcast_to([P, H, H, HD])
                            Q.tensor_tensor(dst, q, kk, ALU.mult).then_inc(s["f_prod"], 1)
                        else:
                            pool.wait_ge(s["f_exp"], 2 if t >= TB else 1)
                            pr = SCR[:, t, :, :].unsqueeze(2).broadcast_to([P, H, HD, H])
                            vv = QF[:, t, P:3 * P].rearrange("p (g e) -> p e g", g=H)[:, HD:2 * HD, :].unsqueeze(1).broadcast_to([P, H, HD, H])
                            Q.tensor_tensor(dst.rearrange("p h g d -> p (h g d)").rearrange("p (h d g) -> p h d g", h=H, d=HD),
                                            pr, vv, ALU.mult).then_inc(s["f_prod"], 1)

            def parts(g):
                tok = slice(512 * g, 512 * g + 512)
                Q.tensor_copy(CTH[:, tok], hT[:, tok]).then_inc(s["g_pstep"], 1)
                return tok

            for g in range(G):
                pool.wait_ge(s["g_hT_copied"], g + 1)
                tok = parts(g)
                pool.wait_ge(s["g_pstep"], g + 1)
                Q.tensor_tensor(CTL[:, tok], hT[:, tok], CTH[:, tok].bitcast(F32), ALU.subtract).then_inc(s["g_cur"], 1)
            with pool.Fori(0, R1) as r:
                for g in range(G):
                    x = r * G + g
                    tok = slice(512 * g, 512 * g + 512)
                    for e in range(E1):
                        pool.wait_ge(s["g_y_read"], x * E1 + e + 3)
                        pool.wait_ge(s["g_acc"], x * E1 + e + 2)
                        Q.tensor_tensor(hT[:, tok], hT[:, tok], YS[:, e % 2, :], ALU.add).then_inc(s["g_acc"], 1)
                    pool.wait_ge(s["g_acc"], x * E1 + 6)
                    pool.sem_inc(s["pool_passed"], 1)
                    parts(g)
                    pool.wait_ge(s["g_pstep"], x + G + 1)
                    Q.tensor_tensor(CTL[:, tok], hT[:, tok], CTH[:, tok].bitcast(F32), ALU.subtract).then_inc(s["g_cur"], 1)


_INS = ['L0_attn_x', 'L0_attn_Wq', 'L0_attn_Wk', 'L0_attn_Wv', 'L0_attn_Wo', 'L0_ffn_gamma1', 'L0_ffn_Wq', 'L0_ffn_bq',
        'L0_ffn_Wdown', 'L0_ffn_bdown', 'L0_ffn_Wup', 'L0_ffn_bup', 'L0_ffn_Wo', 'L0_ffn_bo', 'L0_ffn_gamma2', 'L0_ffn_Wg',
        'L0_ffn_bg', 'L0_ffn_We', 'L0_c', 'L0_wmod', 'L1_attn_Wq', 'L1_attn_bq', 'L1_attn_Wk', 'L1_attn_bk', 'L1_attn_Wv',
        'L1_attn_bv', 'L1_attn_Wo', 'L1_attn_bo', 'L1_attn_Wqs', 'L1_attn_bqs', 'L1_attn_Wks', 'L1_attn_bks', 'L1_attn_Wvs',
        'L1_attn_bvs', 'L1_attn_temp', 'L1_ffn_Wg', 'L1_ffn_bg', 'L1_ffn_W1', 'L1_ffn_b1', 'L1_ffn_W2', 'L1_ffn_b2', 'L1_c',
        'L1_wmod']


def constants():
    c = np.zeros((P, C_END), np.float32)
    c[:, C_ID:C_ID + P] = np.eye(P)
    c[:, C_MQ:C_MQ + P] = -BIG * np.triu(np.ones((P, P)), 1)
    c[:, C_MS:C_MS + P] = -BIG
    c[:, C_MS + P:C_MS + 2 * P] = -BIG * np.tril(np.ones((P, P)), -1)
    p = np.arange(P)
    c[p, C_HM + p // HD] = 1.0
    for a in range(2):
        for e in range(2):
            for d in range(HD):
                c[32 * (2 * a + e) + d, C_SEL + HD * a + d] = 1.0
            c[32 * (2 * a + e) + HD, C_SEL + 2 * HD + a] = 1.0
    c[p % HD, C_REP + p] = 1.0
    for e in range(E1):
        c[:, C_TIE + E1 * e:C_TIE + E1 * e + e] = 1.0
    inv = (1.0 / np.float32(10000.0) ** (np.arange(0, HD, 2, dtype=np.float32) / np.float32(HD))).astype(np.float32)
    ang = np.outer(np.arange(S, dtype=np.float32), inv).astype(np.float32)
    for at, fn in ((C_COS, np.cos), (C_SIN, np.sin)):
        v = fn(ang).astype(np.float32).reshape(TB, P, 1, 4).transpose(1, 0, 2, 3)
        v = np.broadcast_to(v[:, None], (P, 2, TB, 2, 4))
        c[:, at:at + P] = v.reshape(P, P)
    c[:, C_EPS], c[:, C_EPS + 1] = 1e-5, 1e-6
    return c


def kernel(**inputs):
    import numpy as _np
    import concourse.bacc as _bacc
    from concourse import mybir as _mybir
    from concourse.bass_utils import run_bass_kernel_spmd as _run

    nc = _bacc.Bacc("TRN2", target_bir_lowering=False, num_devices=1)
    arrays, io = {}, {}
    for name in _INS:
        a = _np.ascontiguousarray(inputs[name])
        if a.ndim == 0:
            a = a.reshape(1)
        arrays[f"in_{name}"] = a
        io[name] = nc.dram_tensor(f"in_{name}", a.shape, _mybir.dt.from_np(a.dtype), kind="ExternalInput").ap()
    arrays["in_consts"] = constants()
    io["consts"] = nc.dram_tensor("in_consts", (P, C_END), F32, kind="ExternalInput").ap()
    out = nc.dram_tensor("out_x", (B, S, D), F32, kind="ExternalOutput").ap()
    build(nc, io, out)
    r = _run(nc, [arrays], core_ids=[0])
    return r.results[0]["out_x"]
```

```python
from contextlib import ExitStack

import numpy as np

import concourse.bass as bass
from concourse import mybir

P = 128
B, S, D = 2, 1024, 128
H, HD = 16, 8
TB = S // P
T = B * TB
PAIRS = H // 2
U = B * PAIRS
LEAD = 3
RING = 4
L = 64
E0 = 8
E1, F1, R1 = 4, 512, 4
FC = F1 // P
G = 4
GT = T // G
BIG = 1e30
ROWS = 51
ROWSM = 54
KEYW = 2 * HD + 2

ALU = mybir.AluOpType
ACT = mybir.ActivationFunctionType
AX = mybir.AxisListType
F32 = mybir.dt.float32
F32R = mybir.dt.float32r
BF16 = mybir.dt.bfloat16

C_ID, C_MQ, C_MS, C_HM, C_SEL, C_REP, C_TIE, C_COS, C_SIN = 0, 128, 256, 512, 528, 546, 674, 690, 818
C_END = 946


POOL_SCORES = [1, 5, 6, 8, 9, 11, 12, 14, 15]
POOL_VALUES = [0, 2, 4, 5, 7, 9, 10, 12, 13, 15]


def schedule(causal):
    granules, chunks = [], []
    for half in range(2):
        for j in range(4 * (half + 1) if causal else TB):
            q0 = max(0, P * j - 512 * half) if causal else 0
            granules.append((half, j, q0))
    for i in range(TB):
        for a in range(2):
            keys = P * (i + 1) if causal else S
            for c in range((keys + 511) // 512):
                chunks.append((i, a, c, min(512, keys - 512 * c)))
    return granules, chunks


def event_at(l, k):
    return ({2: "sel", 3: "qm", 4: "tk", 5: "tq"}, {2: "sel", 4: "qm", 5: "tk", 7: "tq"})[l].get(k)


def build(nc, io, out):
    ctx = ExitStack()
    with ctx:
        def sb(name, shape, dt=F32):
            return ctx.enter_context(nc.sbuf_tensor(name, shape, dt))

        def sem(name):
            return ctx.enter_context(nc.semaphore(name))

        PS = ctx.enter_context(nc.psum_tensor("PS", [P, 8, 512], F32))

        X = sb("X", [P, T, D])
        HX = sb("HX", [P, T, D])
        XH = sb("XH", [P, T, D])
        hT = sb("hT", [P, T * P])
        CST = sb("CST", [P, C_END])
        IDB = sb("IDB", [P, P], BF16)
        MQB = sb("MQB", [P, P], BF16)
        MSB = sb("MSB", [P, 2 * P], BF16)
        ONES = sb("ONES", [1, P])
        STAT = sb("STAT", [P, T, 6])
        ST1, ST2, ST3, ST4 = (sb(f"ST{n}", [P, T]) for n in range(1, 5))
        IDF = CST[:, C_ID:C_ID + P]

        WN = hT[:, 0:8 * P].rearrange("p (n c) -> p n c", n=8)
        WT = sb("WT", [P, 8, P])
        EPS = sb("EPS", [P, 2])
        W3 = sb("W3", [P, 160])
        WS5 = sb("WS5", [HD, 10])
        BD = sb("BD", [P, 2, H, 5])
        BCOL = sb("BCOL", [P, 2])
        BS5 = sb("BS5", [1, 10])
        BR = sb("BR", [1, 384 + 160])
        BO1 = sb("BO1", [1, P])
        WQS = sb("WQS", [P, 3, HD])
        BQS = sb("BQS", [P, 3])
        TEMP = sb("TEMP", [P, 1])
        CT = sb("CT", [P, 2, B])
        SC = sb("SC", [P, 2, B])
        SC2 = sb("SC2", [P, 2, B])
        HXF = HX[:, :, :].rearrange("p t d -> p (t d)")
        SCB = HXF[:, 0:4 * P].rearrange("p (l b n) -> p l b n", l=2, b=B)
        MODC = sb("MODC", [P, 2, 4, B])
        MODR = sb("MODR", [P, 2, B, 4, D])
        SGN = HXF[:, 4 * P:8 * P].rearrange("p (l b n) -> p l b n", l=2, b=B)
        FW = sb("FW", [P, 3, P])
        WUP = sb("WUP", [L + 1, 2 * D])
        LT = sb("LT", [L + 1, T * P])
        FB = sb("FB", [1, 2, P])
        FCOL = sb("FCOL", [P, 3])
        WG0 = sb("WG0", [P, E0])
        BG0 = sb("BG0", [P, E0])
        WE = sb("WE", [P, E0, D])
        WG1 = sb("WG1", [P, R1 + 1, E1])
        WGC = sb("WGC", [P, E1])
        BG1 = sb("BG1", [P, R1 + 1, E1])
        W1 = sb("W1", [P, E1, F1])
        W2 = sb("W2", [P, E1, FC, D])
        B1 = sb("B1", [P, E1, FC])
        B2C = sb("B2C", [P, E1])
        GW = sb("GW", [P, T, E0])
        GW2 = sb("GW2", [P, T])
        GW3 = sb("GW3", [P, T])

        over = ExitStack()

        def att(name, shape, dt=F32):
            return over.enter_context(nc.sbuf_tensor(name, shape, dt))

        QU = att("QU", [P, U + LEAD, 3, TB * 2 * HD])
        QF = QU[:, 0:U, :, :].rearrange("p u s x -> p (u s x)").rearrange("p (t c) -> p t c", t=T)
        CR = att("CR", [P, U + LEAD, TB * 2, 3])
        SV = att("SV", [P, U + LEAD, TB * 2])
        ATT = att("ATT", [P, U + 1, TB, 2 * HD])
        QA = att("QA", [P, RING, TB * 2, 64], BF16)
        KA = att("KA", [P, RING, TB * 2, 64], BF16)
        VA = att("VA", [P, RING, TB * 2, 32])
        QKT = att("QKT", [P, RING * S])
        QT = QKT[:, 0:RING * S // 2].bitcast(BF16).rearrange("p (r n) -> p r n", r=RING)
        KT = QKT[:, RING * S // 2:RING * S].bitcast(BF16).rearrange("p (r n) -> p r n", r=RING)
        WMOD = QKT[:, 0:12 * D].rearrange("p (l n) -> p l n", l=2)
        KB = att("KB", [P, RING, S], BF16)
        PB = att("PB", [P, 4, 2, 512])
        OT = att("OT", [P, 2, 512])
        NMA = att("NMA", [P, RING, TB * 2])
        NMB = att("NMB", [P, RING, TB * 2])
        NM = att("NM", [P, RING, TB * 2])
        RQ = att("RQ", [P, TB * 2, HD])
        RM = att("RM", [P, TB * 2])
        RD = att("RD", [P, TB, 2])
        PBF = PB[:, :, :, :].rearrange("p a b c -> p (a b c)")
        PRD = PBF.rearrange("p (a h g d) -> p a h g d", a=2, h=H, g=H)
        PRP = hT[:, :].rearrange("p (h g d) -> p h g d", h=H, g=H)
        C5 = PBF[:, 0:U * 2 * TB * 2 * 5].rearrange("p (u s x) -> p u s x", u=U, s=2)
        SCR = QKT[:, :].rearrange("p (t h g) -> p t h g", t=T, h=H)
        SCM = att("SCM", [P, T * H])
        SCL = att("SCL", [P, T * H])
        over.close()
        W1H, W1L = (sb(n, [P, E1, F1], F32R) for n in ("W1H", "W1L"))
        W2H, W2L = (sb(n, [P, E1, FC, D], F32R) for n in ("W2H", "W2L"))
        CTH, CTL = (sb(n, [P, T * P], F32R) for n in ("CTH", "CTL"))
        HMH, HML = (sb(n, [P, 2 * FC, 512], F32R) for n in ("HMH", "HML"))
        XF = XH[:, :, :].rearrange("p t d -> p (t d)")
        HMF = XF.rearrange("p (r n) -> p r n", r=FC)
        HF = HX[:, :, :].rearrange("p t d -> p (t d)")
        CWB = HF[:, 0:1024].rearrange("p (r n) -> p r n", r=2)
        YS = HF[:, 1024:2048].rearrange("p (r n) -> p r n", r=2)
        GWS = sb("GWS", [P, GT, 2 * E1], F32R)
        CWT = sb("CWT", [2 * E1, 512], F32R)
        SLW = sb("SLW", [2 * E1, E1, P], F32R)
        CMP, CEQ = (sb(n, [P, GT, E1, E1]) for n in ("CMP", "CEQ"))
        SELE, SELL = (sb(n, [P, GT, E1]) for n in ("SELE", "SELL"))

        names = """small_loaded later_loaded x_loaded experts_loaded weights_transposed weights_copied
            rep_ready bd_ready w3_ready w3_copied silu_exp silu_ready mod_ready mod_rows_copied
            mod_final dve_step pool_passed pool_init out_done""".split()
        s = {n: sem(n) for n in names}
        for l in range(2):
            for n in """stats_var stats_std xhat_ready hT_psum hT_copied proj_psum proj_copied operands_ready
                k_built qv_built mparts_built kT_psum qT_psum qmT_psum sel_psum kT_ready qT_ready qmT_ready
                att_ready st_full exp_done pv_done o_copied mx_full mx_reduced nm_ready pool_step aT_psum
                aT_copied o_psum o_added init_done""".split():
                s[f"{n}{l}"] = sem(f"{n}{l}")
        for n in """f_stats f_std f_h f_hT_psum f_hT_copied f_lat f_lat_copied f_qkv f_qkv_copied f_prod f_prod_used
            f_scmax f_exp f_out f_oT f_oT_copied f_o f_x2 f_h2 f_h2T f_h2T_copied f_gate f_gexp_in
            f_gexp f_y f_y_used g_stats g_std g_wg g_xh g_hT g_hT_copied g_high g_split g_lg g_tanh_in g_tanh g_cw
            g_cwp g_cwr g_cwT g_cwb g_up g_gelu g_lo g_y g_y_read g_acc g_cur g_last g_last_added g_fin g_step g_pstep""".split():
            s[n] = sem(n)

        def to3(ap, n):
            return ap.unsqueeze(2).broadcast_to([ap.shape[0], ap.shape[1], n])

        sched = [schedule(True), schedule(False)]
        block = ctx.enter_context(nc.Block())

        small_dmas, later_dmas = [], []

        def small(dst, src):
            small_dmas.append((dst, src))

        def later(dst, src):
            later_dmas.append((dst, src))

        small(CST[:, :], io["consts"])
        for n, w in enumerate(["L0_attn_Wq", "L0_attn_Wk", "L0_attn_Wv", "L0_attn_Wo",
                               "L1_attn_Wq", "L1_attn_Wk", "L1_attn_Wv", "L1_attn_Wo"]):
            small(WN[:, n, :], io[w])
        for l in range(2):
            small(CT[:, l, :], io[f"L{l}_c"].rearrange("b k -> k b"))
            small(WMOD[:, l, :], io[f"L{l}_wmod"])
        for n, w in enumerate(["L1_attn_Wks", "L1_attn_Wvs"]):
            small(WS5[:, 5 * n:5 * n + 3], io[w].rearrange("c d -> d c"))
            small(WS5[:, 5 * n + 3:5 * n + 5], io[w][0:2, :].rearrange("c d -> d c"))

        def row(ap):
            return ap.rearrange("(a n) -> a n", a=1)

        def col(ap):
            return ap.rearrange("(n a) -> n a", a=1)

        for n, w in enumerate(["L1_attn_bks", "L1_attn_bvs"]):
            small(BS5[0:1, 5 * n:5 * n + 3], row(io[w]))
            small(BS5[0:1, 5 * n + 3:5 * n + 5], row(io[w][0:2]))
        for n, w in enumerate(["L1_attn_bq", "L1_attn_bk", "L1_attn_bv"]):
            small(BR[0:1, P * n:P * n + P], row(io[w]))
        small(BCOL[:, 0:1], col(io["L1_attn_bk"]))
        small(BCOL[:, 1:2], col(io["L1_attn_bv"]))
        later(BO1[0:1, :], row(io["L1_attn_bo"]))
        later(WQS[:, :, :].rearrange("p c d -> p (c d)"),
              io["L1_attn_Wqs"].rearrange("c d -> (c d)").partition_broadcast(P))
        later(BQS[:, :], io["L1_attn_bqs"].partition_broadcast(P))
        later(TEMP[:, :], io["L1_attn_temp"].partition_broadcast(P))
        later(FW[:, 0, :], io["L0_ffn_Wq"])
        later(FW[:, 1, 0:L], io["L0_ffn_Wdown"])
        later(FW[:, 2, :], io["L0_ffn_Wo"])
        later(WUP[0:L, :], io["L0_ffn_Wup"])
        later(WUP[L:L + 1, :], row(io["L0_ffn_bup"]))
        later(FB[0:1, 0, :], row(io["L0_ffn_bq"]))
        later(FB[0:1, 1, :], row(io["L0_ffn_bo"]))
        later(FCOL[:, 0:1], col(io["L0_ffn_gamma1"]))
        later(FCOL[:, 1:2], col(io["L0_ffn_gamma2"]))
        later(FCOL[0:L, 2:3], col(io["L0_ffn_bdown"]))
        later(WG0[:, :], io["L0_ffn_Wg"])
        later(BG0[:, :], io["L0_ffn_bg"].partition_broadcast(P))
        later(WG1[:, 0:R1, :], io["L1_ffn_Wg"].rearrange("r h e -> h r e"))
        later(BG1[:, 0:R1, :].rearrange("p r e -> p (r e)"), io["L1_ffn_bg"].rearrange("r e -> (r e)").partition_broadcast(P))
        later(B1[:, :, :].rearrange("p e c -> p (e c)"), io["L1_ffn_b1"].rearrange("e (c p) -> p (e c)", p=P))
        later(B2C[:, :], io["L1_ffn_b2"].rearrange("e h -> h e"))
        NSMALL, NLATER = 16 * len(small_dmas), 16 * len(later_dmas)

        @block.sync
        def _(sp):
            sp.dma_start(X[:, :, :], io["L0_attn_x"].rearrange("b (t p) d -> p (b t) d", p=P)).then_inc(s["x_loaded"], 16)
            for dst, src in small_dmas:
                sp.dma_start(dst, src, allow_slow_non_contiguous=True).then_inc(s["small_loaded"], 16)
            for dst, src in later_dmas:
                sp.dma_start(dst, src, allow_slow_non_contiguous=True).then_inc(s["later_loaded"], 16)
            sp.dma_start(WE[:, :, :], io["L0_ffn_We"].rearrange("e d f -> d e f")).then_inc(s["experts_loaded"], 16)
            sp.dma_start(W1[:, :, :], io["L1_ffn_W1"].rearrange("e h f -> h e f")).then_inc(s["experts_loaded"], 16)
            for e in range(E1):
                sp.dma_start(W2[:, e, :, :], io["L1_ffn_W2"][e].rearrange("(c p) h -> p c h", p=P)).then_inc(s["experts_loaded"], 16)
            for g in range(G):
                sp.wait_ge(s["g_fin"], g + 1)
                sp.dma_start(out.rearrange("b (t p) d -> p (b t) d", p=P)[:, GT * g:GT * g + GT, :], X[:, GT * g:GT * g + GT, :])\
                    .then_inc(s["out_done"], 16)
            sp.wait_ge(s["out_done"], 16 * G)

        @block.tensor
        def _(pe):
            mm = nc.tensor.matmul
            tr = nc.tensor.transpose
            pe.wait_ge(s["small_loaded"], NSMALL)
            for n in range(8):
                last = tr(PS[:, n // 4, P * (n % 4):P * (n % 4) + P], WN[:, n, :], IDF)
            last.then_inc(s["weights_transposed"], 1)
            mm(PS[:, 2, 0:10], CST[0:HD, C_REP:C_REP + P], WS5[:, :], start=True, stop=True).then_inc(s["rep_ready"], 1)
            pe.wait_ge(s["bd_ready"], 1)
            for n in range(2):
                mm(PS[:, 2, 16 + 80 * n:96 + 80 * n], WN[:, 5 + n, :], BD[:, n, :, :].rearrange("p h c -> p (h c)"), start=True, stop=True)
                last = mm(PS[0:1, 3, 80 * n:80 * n + 80], BCOL[:, n:n + 1], BD[:, n, :, :].rearrange("p h c -> p (h c)"), start=True, stop=True)
            last.then_inc(s["w3_ready"], 1)
            pe.wait_ge(s["silu_ready"], 1)
            pe.wait_ge(s["w3_copied"], 1)
            for l in range(2):
                for n, piece in enumerate((0, 1, 3, 4)):
                    mm(PS[:, 3, 256 + 8 * l + 2 * n:258 + 8 * l + 2 * n], WMOD[:, l, P * piece:P * piece + P], SC2[:, l, :], start=True, stop=True)
                for b in range(B):
                    last = mm(PS[:, 4 + 2 * l + b, :], SCB[:, l, b, :], WMOD[:, l, 2 * P:6 * P], start=True, stop=True)
            last.then_inc(s["mod_ready"], 1)
            pe.wait_ge(s["mod_final"], 1)
            pe.wait_ge(s["mod_rows_copied"], 1)

            def each(g):
                return g + 1

            def transpose_tokens(src, full, copied, after):
                sm, value = after
                for g in range(G):
                    pe.wait_ge(sm, value(g))
                    if g >= 2:
                        pe.wait_ge(copied, g - 1)
                    for t in range(GT):
                        last = tr(PS[:, g % 2, P * t:P * t + P], src(GT * g + t), IDF)
                    last.then_inc(full, 1)

            def attention(l):
                granules, chunks = sched[l]
                K = len(granules) // 2
                K0 = sum(1 for h, _, _ in granules if h == 0) // 2
                nch, ng = len(chunks), len(granules)
                TRB = PS[:, 7, :].bitcast(BF16)

                def transposes(src, full):
                    for t in range(TB):
                        last = tr(TRB[:, P * t:P * t + P], src[:, 2 * t:2 * t + 2, :].rearrange("p a c -> p (a c)"), IDB[:, :])
                    last.then_inc(full, 1)

                def max_chunk(u, r, n):
                    i, a, c, w = chunks[n]
                    pe_wait(s[f"mx_reduced{l}"], u * nch + n - 1, n >= 2, u)
                    diag = l == 0 and 512 * c + w == P * (i + 1)
                    ms = mm(PS[:, 4 + n % 2, 0:w], QT[:, r, P * i:P * i + P],
                            (KT, KB)[a][:, r, 512 * c:512 * c + w], start=True, stop=not diag)
                    if diag:
                        ms = mm(PS[:, 4 + n % 2, w - P:w], IDB[:, :], MQB[:, :], start=False, stop=True)
                    ms.then_inc(s[f"mx_full{l}"], 1)

                def pe_wait(sm, value, sure, u):
                    if sure or not isinstance(u, int) or u > 0:
                        pe.wait_ge(sm, value)

                def scores(u, r, g):
                    half, j, q0 = granules[g]
                    pe.wait_ge(s[f"exp_done{l}"], u * ng + g + 1)
                    first = l == 0 and half == 0 and j == 1
                    if first:
                        q0 = 0
                    for a in range(2):
                        o = PS[:, 2 * (g % 2) + a, q0:512]
                        diag = l == 0 and j >= 4 * half
                        last = mm(o, (KT, KB)[a][:, r, P * j:P * j + P],
                                  QT[:, r, 512 * half + q0:512 * half + 512], start=True, stop=not diag)
                        if diag:
                            w, m = (2 * P, MSB[:, :]) if first else (P, MSB[:, P:2 * P])
                            last = mm(PS[:, 2 * (g % 2) + a, q0:q0 + w], IDB[:, :], m, start=False, stop=True)
                    last.then_inc(s[f"st_full{l}"], 1)

                def values(u, r, k, extra=None):
                    start = k in (0, K0) if extra is None else True
                    for e in range(2):
                        half, j, q0 = granules[2 * k + e]
                        if l == 0 and half == 0 and j == 1 or extra:
                            q0 = 0
                        for a in range(2):
                            c0 = 32 * (2 * a + e)
                            last = mm(PS[c0:c0 + 32, 6, q0:512], VA[:, r, 2 * j + a, :],
                                      PB[:, (2 * k + e) % 4, a, q0:512], start=start,
                                      stop=(k in (K0 - 1, K - 1)) and extra is None)
                    return last

                def select(r):
                    o = PS[:, 7, 0:TB * KEYW]
                    for i in range(TB):
                        last = mm(o[:, KEYW * i:KEYW * i + KEYW], OT[:, i // 4, P * (i % 4):P * (i % 4) + P],
                                  CST[:, C_SEL:C_SEL + KEYW], start=True, stop=True)
                    last.then_inc(s[f"sel_psum{l}"], 1)

                for v in range(LEAD):
                    pe.wait_ge(s[f"k_built{l}"], v + 1)
                    if v:
                        pe.wait_ge(s[f"qT_ready{l}"], v)
                    transposes(KA[:, v, :, :], s[f"kT_psum{l}"])
                    pe.wait_ge(s[f"kT_ready{l}"], v + 1)
                    pe.wait_ge(s[f"qv_built{l}"], v + 1)
                    transposes(QA[:, v, :, :], s[f"qT_psum{l}"])
                    if v < 2:
                        pe.wait_ge(s[f"qT_ready{l}"], v + 1)
                        for n in range(nch):
                            max_chunk(v, v, n)
                pe.wait_ge(s[f"qT_ready{l}"], LEAD)
                pe.wait_ge(s[f"mparts_built{l}"], 1)
                transposes(QA[:, 0, :, :], s[f"qmT_psum{l}"])
                values(None, RING - 1, K - 1, extra=True)

                def event(u, r, k):
                    e = event_at(l, k)
                    nxt = (r + 1) % RING
                    if e == "sel":
                        pe.wait_ge(s[f"o_copied{l}"], 2 * u + 1)
                        select(r)
                    elif e == "qm":
                        pe.wait_ge(s[f"att_ready{l}"], u + 1)
                        pe.wait_ge(s[f"mparts_built{l}"], u + 2)
                        transposes(QA[:, nxt, :, :], s[f"qmT_psum{l}"])
                    elif e == "tk":
                        pe.wait_ge(s[f"qmT_ready{l}"], u + 2)
                        pe.wait_ge(s[f"k_built{l}"], u + LEAD + 1)
                        transposes(KA[:, (r + LEAD) % RING, :, :], s[f"kT_psum{l}"])
                    elif e == "tq":
                        pe.wait_ge(s[f"kT_ready{l}"], u + LEAD + 1)
                        pe.wait_ge(s[f"qv_built{l}"], u + LEAD + 1)
                        transposes(QA[:, (r + LEAD) % RING, :, :], s[f"qT_psum{l}"])

                def step(u, r):
                    for k in range(K):
                        n = nch * k // K
                        assert nch * (k + 1) // K == n + 4
                        if k == 0:
                            pe.wait_ge(s[f"qT_ready{l}"], u + LEAD)
                        max_chunk(u + 2, (r + 2) % RING, n)
                        max_chunk(u + 2, (r + 2) % RING, n + 1)
                        if k == 0:
                            pe.wait_ge(s[f"qmT_ready{l}"], u + 1)
                        scores(u, r, 2 * k)
                        event(u, r, k)
                        scores(u, r, 2 * k + 1)
                        max_chunk(u + 2, (r + 2) % RING, n + 2)
                        max_chunk(u + 2, (r + 2) % RING, n + 3)
                        if k == 0:
                            last = values(u, (r + RING - 1) % RING, K - 1)
                        else:
                            if k - 1 in (0, K0):
                                pe.wait_ge(s[f"o_copied{l}"], 2 * u + (1 if k == 1 else 2))
                            last = values(u, r, k - 1)
                        last.then_inc(s[f"pv_done{l}"], 1)

                with pe.Fori(0, U // RING) as it:
                    for r in range(RING):
                        step(it * RING + r, r)
                pe.wait_ge(s[f"exp_done{l}"], U * ng + 2)
                values(None, RING - 1, K - 1).then_inc(s[f"pv_done{l}"], 1)
                pe.wait_ge(s[f"o_copied{l}"], 2 * U + 1)
                select(0)

            for l in range(2):
                transpose_tokens(lambda t: XH[:, t, :], s[f"hT_psum{l}"], s[f"hT_copied{l}"], (s[f"xhat_ready{l}"], each))
                for t in range(T):
                    pe.wait_ge(s[f"hT_copied{l}"], t // GT + 1)
                    if t >= 3:
                        pe.wait_ge(s[f"proj_copied{l}"], t - 2)
                    bank = 2 + 2 * (t % 3)
                    lh = hT[:, P * t:P * t + P]
                    last = mm(PS[:, bank, 0:384], lh, WT[:, 4 * l:4 * l + 3, :].rearrange("p s n -> p (s n)"), start=True, stop=l == 0)
                    if l == 1:
                        mm(PS[:, bank, 0:384], ONES[0:1, :], BR[0:1, 0:384], start=False, stop=True)
                        mm(PS[:, bank + 1, 0:160], lh, W3[:, :], start=True, stop=False)
                        last = mm(PS[:, bank + 1, 0:160], ONES[0:1, :], BR[0:1, 384:544], start=False, stop=True)
                    last.then_inc(s[f"proj_psum{l}"], 1)
                pe.wait_ge(s[f"proj_copied{l}"], T)
                attention(l)
                transpose_tokens(lambda t: XH[:, t, :], s[f"aT_psum{l}"], s[f"aT_copied{l}"], (s[f"att_ready{l}"], lambda g: U + 2 + GT * g // TB))
                for t in range(T):
                    pe.wait_ge(s[f"aT_copied{l}"], t // GT + 1)
                    g = t // GT
                    if t % GT == 0 and g >= 2:
                        pe.wait_ge(s[f"o_added{l}"], g - 1)
                    o = PS[:, 2 + g % 2, P * (t % GT):P * (t % GT) + P]
                    last = mm(o, hT[:, P * t:P * t + P], WT[:, 4 * l + 3, :], start=True, stop=l == 0)
                    if l == 1:
                        last = mm(o, ONES[0:1, :], BO1[0:1, :], start=False, stop=True)
                    if t % GT == GT - 1:
                        last.then_inc(s[f"o_psum{l}"], 1)

                if l == 0:
                    pe.wait_ge(s["later_loaded"], NLATER)
                    pe.wait_ge(s["o_added0"], G)
                    transpose_tokens(lambda t: XH[:, t, :], s["f_hT_psum"], s["f_hT_copied"], (s["f_h"], each))
                    for g in range(G):
                        pe.wait_ge(s["f_hT_copied"], g + 1)
                        if g >= 2:
                            pe.wait_ge(s["f_lat_copied"], g - 1)
                        mm(PS[0:L, 2 + g % 2, :], FW[:, 1, 0:L], hT[:, 512 * g:512 * g + 512], start=True, stop=True)\
                            .then_inc(s["f_lat"], 1)
                    for t in range(T):
                        pe.wait_ge(s["f_lat_copied"], t // GT + 1)
                        if t >= 4:
                            pe.wait_ge(s["f_qkv_copied"], t - 3)
                        bank = 4 + t % 4
                        mm(PS[:, bank, 0:P], hT[:, P * t:P * t + P], FW[:, 0, :], start=True, stop=False)
                        mm(PS[:, bank, 0:P], ONES[0:1, :], FB[0:1, 0, :], start=False, stop=True)
                        mm(PS[:, bank, P:3 * P], LT[:, P * t:P * t + P], WUP[:, :], start=True, stop=True)\
                            .then_inc(s["f_qkv"], 1)
                    transpose_tokens(lambda t: XH[:, t, :], s["f_oT"], s["f_oT_copied"], (s["f_out"], each))
                    for t in range(T):
                        g = t // GT
                        pe.wait_ge(s["f_oT_copied"], g + 1)
                        if t % GT == 0 and g >= 2:
                            pe.wait_ge(s["f_x2"], g - 1)
                        o = PS[:, 2 + g % 2, P * (t % GT):P * (t % GT) + P]
                        mm(o, hT[:, P * t:P * t + P], FW[:, 2, :], start=True, stop=False)
                        last = mm(o, ONES[0:1, :], FB[0:1, 1, :], start=False, stop=True)
                        if t % GT == GT - 1:
                            last.then_inc(s["f_o"], 1)
                    transpose_tokens(lambda t: XH[:, t, :], s["f_h2T"], s["f_h2T_copied"], (s["f_h2"], each))
                    pe.wait_ge(s["f_h2T_copied"], G)
                    for t in range(T):
                        last = mm(PS[:, 0, E0 * t:E0 * t + E0], hT[:, P * t:P * t + P], WG0[:, :], start=True, stop=True)
                    last.then_inc(s["f_gate"], 1)
                    pe.wait_ge(s["experts_loaded"], 96)
                    for t in range(T):
                        if t == 3:
                            pe.wait_ge(s["f_gexp_in"], 1)
                        elif t >= 4:
                            pe.wait_ge(s["f_y_used"], t - 3)
                        for hf in range(2):
                            last = mm(PS[:, (2 + 2 * (t % 4)) % 8 + hf, :], hT[:, P * t:P * t + P],
                                      WE[:, 4 * hf:4 * hf + 4, :].rearrange("p e f -> p (e f)"), start=True, stop=True)
                        last.then_inc(s["f_y"], 1)
                    pe.wait_ge(s["f_y_used"], T)

            transpose_tokens(lambda t: XH[:, t, :], s["g_hT"], s["g_hT_copied"], (s["g_xh"], each))
            pe.wait_ge(s["g_hT_copied"], G)
            pe.wait_ge(s["g_split"], 1)

            def product(o, wh, wl, xh, xl, start, stop):
                mm(o, wh, xl, start=start, stop=False)
                mm(o, wl, xh, start=False, stop=False)
                return mm(o, wh, xh, start=False, stop=stop)

            def up(x, g, e):
                tok = slice(512 * g, 512 * g + 512)
                for f in range(FC):
                    pe.wait_ge(s["g_gelu"], x * 16 + FC * e + f + 1)
                    product(PS[:, 2 + f, :], W1H[:, e, P * f:P * f + P], W1L[:, e, P * f:P * f + P],
                            CTH[:, tok], CTL[:, tok], True, True).then_inc(s["g_up"], 1)

            def down(x, e):
                pe.wait_ge(s["g_y_read"], x * E1 + e + 1)
                for f in range(FC):
                    pe.wait_ge(s["g_lo"], x * 16 + FC * e + f + 5)
                    n = (FC * e + f) % (2 * FC)
                    last = product(PS[:, 6 + e % 2, :], W2H[:, e, f, :], W2L[:, e, f, :], HMH[:, n, :], HML[:, n, :],
                                   f == 0, f == FC - 1)
                last.then_inc(s["g_y"], 1)

            def weights(x, e):
                if e == 0:
                    pe.wait_ge(s["g_cwr"], x + 1)
                elif e >= 2:
                    pe.wait_ge(s["g_cwb"], x * E1 + 2 * e - 2)
                mm(PS[:, int(e == 1), :], SLW[:, e, :], CWT[:, :], start=True, stop=True).then_inc(s["g_cwT"], 1)

            def turn_weights(x):
                pe.wait_ge(s["g_cw"], x + 1)
                pe.wait_ge(s["g_cwb"], x * E1 + 1)
                for t in range(GT):
                    last = tr(PS[0:2 * E1, 0, P * t:P * t + P], GWS[:, t, :].bitcast(F32), IDF)
                last.then_inc(s["g_cwp"], 1)

            def logits(x, g):
                pe.wait_ge(s["g_cur"], x + 1)
                for t in range(GT):
                    last = mm(PS[:, 1, E1 * t:E1 * t + E1], hT[:, 512 * g + P * t:512 * g + P * t + P], WGC[:, :], start=True, stop=True)
                last.then_inc(s["g_lg"], 1)

            pe.wait_ge(s["g_wg"], 1)
            logits(0, 0)
            up(0, 0, 0)
            with pe.Fori(0, R1) as r:
                for g in range(G):
                    x = r * G + g
                    up(x, g, 1)
                    turn_weights(x)
                    down(x, 0)
                    up(x, g, 2)
                    weights(x, 0)
                    down(x, 1)
                    weights(x, 1)
                    up(x, g, 3)
                    weights(x, 2)
                    down(x, 2)
                    if g == G - 1:
                        pe.wait_ge(s["g_wg"], r + 2)
                    pe.wait_ge(s["g_cwb"], x * E1 + 3)
                    logits(x + 1, (g + 1) % G)
                    up(x + 1, (g + 1) % G, 0)
                    weights(x, 3)
                    down(x, 3)
            pe.wait_ge(s["g_cur"], R1 * G + G)
            for g in range(G):
                if g >= 2:
                    pe.wait_ge(s["g_last_added"], g - 1)
                for t in range(GT):
                    last = tr(PS[:, 2 + g % 2, P * t:P * t + P], hT[:, 512 * g + P * t:512 * g + P * t + P], IDF)
                last.then_inc(s["g_last"], 1)

        @block.scalar
        def _(act):
            A = nc.scalar.activation
            EPS5, EPS6 = EPS[:, 0:1], EPS[:, 1:2]
            act.wait_ge(s["stats_var0"], 1)
            A(ST3[:, :], ST2[:, :], ACT.Sqrt, scale=1.0 / D, bias=EPS5).then_inc(s["stats_std0"], 1)
            act.wait_ge(s["small_loaded"], NSMALL)
            A(SC[:, :, :], CT[:, :, :], ACT.Exp, scale=-1.0).then_inc(s["silu_exp"], 1)
            act.wait_ge(s["weights_transposed"], 1)
            A(WT[:, :, :].rearrange("p (a n) c -> p a (n c)", a=2), PS[:, 0:2, :], ACT.Copy).then_inc(s["weights_copied"], 1)
            act.wait_ge(s["mod_ready"], 1)
            A(MODR[:, :, :, :, :].rearrange("p l b k d -> p (l b) (k d)"), PS[:, 4:8, :], ACT.Copy).then_inc(s["mod_rows_copied"], 1)

            def attention(l):
                granules, chunks = sched[l]
                K = len(granules) // 2
                K0 = sum(1 for h, _, _ in granules if h == 0) // 2
                ng = len(granules)
                TRB = PS[:, 7, :].bitcast(BF16)
                scale = float(HD) ** -0.5 if l == 0 else 1.0

                def copy_t(dst, full, count, ready):
                    act.wait_ge(full, count)
                    A(dst, TRB, ACT.Copy).then_inc(ready, 1)

                def copy_k(r, count, head):
                    if head == 0:
                        act.wait_ge(s[f"kT_psum{l}"], count)
                        A(KT[0:64, r, :], TRB[0:64, :], ACT.Copy)
                    else:
                        A(KB[64:P, r, :], TRB[64:P, :], ACT.Copy).then_inc(s[f"kT_ready{l}"], 1)

                act.wait_ge(s[f"init_done{l}"], 1)
                for v in range(LEAD):
                    copy_k(v, v + 1, 0)
                    copy_k(v, v + 1, 1)
                    copy_t(QT[:, v, :], s[f"qT_psum{l}"], v + 1, s[f"qT_ready{l}"])
                copy_t(QT[:, 0, :], s[f"qmT_psum{l}"], 1, s[f"qmT_ready{l}"])
                act.sem_inc(s[f"exp_done{l}"], 2)

                def exp(u, r, g):
                    half, j, q0 = granules[g]
                    if l == 0 and half == 0 and j == 1:
                        q0 = 0
                    act.wait_ge(s[f"st_full{l}"], u * ng + g + 1)
                    act.wait_ge(s[f"pv_done{l}"], u * K + g // 2 - 1 + 2)
                    A(PB[:, g % 4, :, q0:512], PS[:, 2 * (g % 2):2 * (g % 2) + 2, q0:512], ACT.Exp, scale=scale)\
                        .then_inc(s[f"exp_done{l}"], 1)

                def step(u, r):
                    for k in range(K):
                        exp(u, r, 2 * k)
                        e = event_at(l, k)
                        if e == "qm":
                            copy_t(QT[:, (r + 1) % RING, :], s[f"qmT_psum{l}"], u + 2, s[f"qmT_ready{l}"])
                        elif e == "tk":
                            copy_k((r + LEAD) % RING, u + LEAD + 1, 0)
                        elif e == "tq":
                            copy_t(QT[:, (r + LEAD) % RING, :], s[f"qT_psum{l}"], u + LEAD + 1, s[f"qT_ready{l}"])
                        exp(u, r, 2 * k + 1)
                        if e == "tk":
                            copy_k((r + LEAD) % RING, u + LEAD + 1, 1)
                        if k == 0:
                            act.wait_ge(s[f"pv_done{l}"], u * K + 2)
                            A(OT[:, 1, :], PS[:, 6, :], ACT.Copy).then_inc(s[f"o_copied{l}"], 1)
                        elif k == K0:
                            act.wait_ge(s[f"pv_done{l}"], u * K + K0 + 2)
                            act.wait_ge(s[f"sel_psum{l}"], u + 1)
                            A(OT[:, 0, :], PS[:, 6, :], ACT.Copy).then_inc(s[f"o_copied{l}"], 1)
                act.sem_inc(s[f"pv_done{l}"], 1)
                with act.Fori(0, U // RING) as it:
                    for r in range(RING):
                        step(it * RING + r, r)
                act.wait_ge(s[f"pv_done{l}"], U * K + 2)
                A(OT[:, 1, :], PS[:, 6, :], ACT.Copy).then_inc(s[f"o_copied{l}"], 1)

            def copy_hT(full, copied, scale=None, bias=None):
                for g in range(G):
                    act.wait_ge(full, g + 1)
                    if scale is None:
                        A(hT[:, 512 * g:512 * g + 512], PS[:, g % 2, :], ACT.Copy).then_inc(copied, 1)
                    elif bias is None:
                        A(hT[:, 512 * g:512 * g + 512], PS[:, g % 2, :], ACT.Copy, scale=scale(g)).then_inc(copied, 1)
                    else:
                        A(hT[:, 512 * g:512 * g + 512], PS[:, g % 2, :], ACT.Identity, scale=scale(g), bias=bias(g))\
                            .then_inc(copied, 1)

            for l in range(2):
                if l == 1:
                    act.wait_ge(s["stats_var1"], 1)
                    A(ST3[:, :], ST2[:, :], ACT.Sqrt, scale=1.0 / D, bias=EPS5).then_inc(s["stats_std1"], 1)
                act.wait_ge(s["mod_final"], 1)
                copy_hT(s[f"hT_psum{l}"], s[f"hT_copied{l}"],
                        scale=lambda g: MODC[:, l, 1, 2 * g // G:2 * g // G + 1], bias=lambda g: MODC[:, l, 0, 2 * g // G:2 * g // G + 1])
                for t in range(T):
                    act.wait_ge(s[f"proj_psum{l}"], t + 1)
                    bank = 2 + 2 * (t % 3)
                    b0 = PAIRS * (t // TB)
                    tt = 16 * (t % TB)
                    src = PS[:, bank, 0:384].rearrange("p (s r c) -> p r s c", s=3, r=PAIRS)
                    dst = QU[:, b0:b0 + PAIRS, :, tt:tt + 16]
                    if l == 0:
                        A(dst, src, ACT.Copy).then_inc(s["proj_copied0"], 1)
                    else:
                        A(dst[:, :, 0, :], src[:, :, 0, :], ACT.Copy, scale=TEMP[:, :])
                        A(dst[:, :, 1:3, :], src[:, :, 1:3, :], ACT.Copy)
                        A(C5[:, b0:b0 + PAIRS, :, 10 * (t % TB):10 * (t % TB) + 10],
                          PS[:, bank + 1, 0:160].rearrange("p (s r c) -> p r s c", s=2, r=PAIRS), ACT.Copy)\
                            .then_inc(s["proj_copied1"], 1)
                attention(l)
                copy_hT(s[f"aT_psum{l}"], s[f"aT_copied{l}"])
                if l == 0:
                    act.wait_ge(s["later_loaded"], NLATER)
                    act.wait_ge(s["f_stats"], 1)
                    A(ST3[:, :], ST2[:, :], ACT.Sqrt, scale=1.0 / D, bias=EPS5).then_inc(s["f_std"], 1)
                    act.wait_ge(s["f_stats"], 2)
                    A(ST3[:, :], ST2[:, :], ACT.Sqrt, scale=1.0 / D, bias=EPS6).then_inc(s["f_std"], 1)
                    copy_hT(s["f_hT_psum"], s["f_hT_copied"], scale=lambda g: FCOL[:, 0:1])
                    for g in range(G):
                        act.wait_ge(s["f_lat"], g + 1)
                        A(LT[0:L, 512 * g:512 * g + 512], PS[0:L, 2 + g % 2, :], ACT.Identity, bias=FCOL[0:L, 2:3])\
                            .then_inc(s["f_lat_copied"], 1)
                    for t in range(T):
                        act.wait_ge(s["f_qkv"], t + 1)
                        A(QF[:, t, :], PS[:, 4 + t % 4, 0:384], ACT.Copy).then_inc(s["f_qkv_copied"], 1)
                    for c in range(2):
                        act.wait_ge(s["f_scmax"], c + 1)
                        half = SCR[:, TB * c:TB * c + TB, :, :].rearrange("p t h g -> p (t h g)")
                        A(half, half, ACT.Exp, scale=float(HD) ** -0.5).then_inc(s["f_exp"], 1)
                    copy_hT(s["f_oT"], s["f_oT_copied"])
                    act.wait_ge(s["f_stats"], 3)
                    A(ST3[:, :], ST2[:, :], ACT.Sqrt, scale=1.0 / D, bias=EPS6).then_inc(s["f_std"], 1)
                    copy_hT(s["f_h2T"], s["f_h2T_copied"], scale=lambda g: FCOL[:, 1:2])
                    act.wait_ge(s["f_gexp_in"], 1)
                    A(GW[:, :, :], GW[:, :, :], ACT.Exp).then_inc(s["f_gexp"], 1)
            act.wait_ge(s["g_stats"], 1)
            A(ST3[:, :], ST2[:, :], ACT.Sqrt, scale=1.0 / D, bias=EPS5).then_inc(s["g_std"], 1)
            act.wait_ge(s["att_ready1"], U + 2)
            A(W1H[:, :, :].rearrange("p e n -> p (e n)"), W1[:, :, :].rearrange("p e n -> p (e n)"), ACT.Copy)
            A(W2H[:, :, :, :].rearrange("p e f n -> p (e f n)"), W2[:, :, :, :].rearrange("p e f n -> p (e f n)"), ACT.Copy)\
                .then_inc(s["g_high"], 1)
            copy_hT(s["g_hT"], s["g_hT_copied"],
                    scale=lambda g: MODC[:, 1, 3, 2 * g // G:2 * g // G + 1], bias=lambda g: MODC[:, 1, 2, 2 * g // G:2 * g // G + 1])
            act.sem_inc(s["g_gelu"], 4)
            def gelu(x, e):
                for f in range(FC):
                    n = FC * e + f
                    act.wait_ge(s["g_up"], x * 16 + n + 1)
                    act.wait_ge(s["g_lo"], x * 16 + n + 1)
                    A(HMF[:, f, :], PS[:, 2 + f, :], ACT.Gelu_apprx_tanh, bias=B1[:, e, f:f + 1])
                    if f == 0:
                        act.wait_ge(s["g_y"], x * E1 + e + 1)
                    A(HMH[:, n % (2 * FC), :], PS[:, 2 + f, :], ACT.Gelu_apprx_tanh, bias=B1[:, e, f:f + 1])\
                        .then_inc(s["g_gelu"], 1)

            def tanh(x, g):
                act.wait_ge(s["g_tanh_in"], x + 1)
                A(GW[:, GT * g:GT * g + GT, E1:2 * E1], GW[:, GT * g:GT * g + GT, E1:2 * E1], ACT.Tanh).then_inc(s["g_tanh"], 1)

            gelu(0, 0)
            tanh(0, 0)
            with act.Fori(0, R1) as r:
                for g in range(G):
                    x = r * G + g
                    gelu(x, 1)
                    gelu(x, 2)
                    gelu(x, 3)
                    gelu(x + 1, 0)
                    tanh(x + 1, (g + 1) % G)

        @block.vector
        def _(dve):
            V = nc.vector
            step_n = [0]

            def link(ins):
                step_n[0] += 1
                ins.then_inc(s["dve_step"], 1)
                dve.wait_ge(s["dve_step"], step_n[0])

            def settle():
                link(V.memset(ST1[:, :], 0.0))

            def batch_row(l, b, k):
                return MODR[:, l, b, k, :].unsqueeze(1).broadcast_to([P, TB, D])

            def scale_groups(src, ready):
                for g in range(G):
                    t = slice(GT * g, GT * g + GT)
                    V.tensor_tensor(XH[:, t, :], src[:, t, :], to3(ST1[:, t], D), ALU.mult).then_inc(ready, 1)
                dve.wait_ge(ready, G)

            def layernorm(var, std, ready):
                for t in range(T):
                    last = V.bn_stats(STAT[:, t, :], X[:, t, :])
                link(last)
                V.tensor_tensor(ST1[:, :], STAT[:, :, 1], STAT[:, :, 4], ALU.subtract)
                V.tensor_tensor(ST2[:, :], STAT[:, :, 2], STAT[:, :, 5], ALU.add)
                link(V.tensor_tensor(ST4[:, :], STAT[:, :, 1], STAT[:, :, 4], ALU.add))
                V.tensor_scalar(ST4[:, :], ST4[:, :], 0.5, None, ALU.mult)
                link(V.tensor_tensor(ST1[:, :], ST1[:, :], ST1[:, :], ALU.mult))
                link(V.scalar_tensor_tensor(ST2[:, :], ST1[:, :], D / 4.0, ST2[:, :], ALU.mult, ALU.add))
                dve.sem_inc(var, 1)
                link(V.tensor_tensor(XH[:, :, :], X[:, :, :], to3(ST4[:, :], D), ALU.subtract))
                dve.wait_ge(*std)
                link(V.reciprocal(ST1[:, :], ST3[:, :]))
                if ready is None:
                    link(V.tensor_tensor(XH[:, :, :], XH[:, :, :], to3(ST1[:, :], D), ALU.mult))
                else:
                    scale_groups(XH, ready)

            def squares(t):
                link(V.tensor_tensor(XH[:, t, :], HX[:, t, :], HX[:, t, :], ALU.mult))
                link(V.tensor_reduce(ST2[:, t], XH[:, t, :], AX.X, ALU.add))

            def rmsnorm(var, std, ready):
                dve.sem_inc(var, 1)
                dve.wait_ge(*std)
                link(V.reciprocal(ST1[:, :], ST3[:, :]))
                scale_groups(HX, ready)

            def modulate(l):
                for b in range(B):
                    t = slice(TB * b, TB * b + TB)
                    V.tensor_tensor(HX[:, t, :], XH[:, t, :], batch_row(l, b, 2), ALU.mult)
                settle()
                for b in range(B):
                    t = slice(TB * b, TB * b + TB)
                    last = V.tensor_tensor(HX[:, t, :], HX[:, t, :], batch_row(l, b, 1), ALU.add)
                link(last)

            def attention(l):
                granules, chunks = sched[l]
                K = len(granules) // 2
                nch = len(chunks)

                def reduce(u, r, n):
                    i, a, c, w = chunks[n]
                    dve.wait_ge(s[f"mx_full{l}"], u * nch + n + 1)
                    V.tensor_reduce((NMA, NMB)[c][:, r, 2 * i + a:2 * i + a + 1], PS[:, 4 + n % 2, 0:w], AX.X, ALU.max, negate=True)\
                        .then_inc(s[f"mx_reduced{l}"], 1)

                def combine(u, r):
                    dve.wait_ge(s[f"mx_reduced{l}"], u * nch + nch)
                    if l == 0:
                        V.tensor_copy(NM[:, r, 0:TB], NMA[:, r, 0:TB])
                    lo = TB if l == 0 else 0
                    V.tensor_tensor(NM[:, r, lo:2 * TB], NMA[:, r, lo:2 * TB], NMB[:, r, lo:2 * TB], ALU.min)\
                        .then_inc(s[f"nm_ready{l}"], 1)

                def normalise(u, count):
                    o = PS[:, 7, 0:TB * KEYW].rearrange("p (t c) -> p t c", c=KEYW)
                    dve.wait_ge(s[f"sel_psum{l}"], count)
                    V.reciprocal(RD[:, :, :], o[:, :, 2 * HD:KEYW]).then_inc(s[f"init_done{l}"], 1)
                    dve.wait_ge(s[f"init_done{l}"], count + 1)
                    V.tensor_tensor(ATT[:, u, :, :].rearrange("p t (a d) -> p t a d", a=2),
                                    o[:, :, 0:2 * HD].rearrange("p t (a d) -> p t a d", a=2),
                                    RD[:, :, :].unsqueeze(3).broadcast_to([P, TB, 2, HD]), ALU.mult)\
                        .then_inc(s[f"att_ready{l}"], 1)

                for v in range(2):
                    for n in range(nch):
                        reduce(v, v, n)
                    combine(v, v)

                def step(u, r):
                    for k in range(K):
                        n0, n1 = nch * k // K, nch * (k + 1) // K
                        for n in range(n0, n1):
                            reduce(u + 2, (r + 2) % RING, n)
                            if n == n0 + 1 and event_at(l, k) == "sel":
                                normalise(u, u + 1)
                    combine(u + 2, (r + 2) % RING)

                with dve.Fori(0, U // RING) as it:
                    for r in range(RING):
                        step(it * RING + r, r)
                normalise(U, U + 1)
                dve.wait_ge(s[f"att_ready{l}"], U + 1)
                for b in range(B):
                    V.tensor_copy(XH[:, TB * b:TB * b + TB, :].rearrange("p t (u c) -> p u t c", u=PAIRS),
                                  ATT[:, 1 + PAIRS * b:1 + PAIRS * b + PAIRS, :, :]).then_inc(s[f"att_ready{l}"], 1)

            def residual(l, full, added, k):
                for g in range(G):
                    dve.wait_ge(full, g + 1)
                    t = slice(GT * g, GT * g + GT)
                    b = GT * g // TB
                    link(V.tensor_tensor(XH[:, t, :], PS[:, 2 + g % 2, :].rearrange("p (t d) -> p t d", t=GT),
                                         MODR[:, l, b, k, :].unsqueeze(1).broadcast_to([P, GT, D]), ALU.mult))
                    dve.sem_inc(added, 1)
                    link(V.tensor_tensor(X[:, t, :], X[:, t, :], XH[:, t, :], ALU.add))

            V.memset(EPS[:, 0:1], 1e-5)
            link(V.memset(EPS[:, 1:2], 1e-6))
            dve.wait_ge(s["x_loaded"], 16)
            layernorm(s["stats_var0"], (s["stats_std0"], 1), s["xhat_ready0"])
            V.memset(ONES[:, :], 1.0)
            V.memset(QU[:, U:U + LEAD, :, :].rearrange("p u s x -> p (u s x)"), 0.0)
            V.memset(SV[:, U:U + LEAD, :].rearrange("p u x -> p (u x)"), 0.0)
            V.memset(PBF, 1.0)
            V.memset(VA[:, :, :, :].rearrange("p r x c -> p (r x) c"), 0.0)
            V.memset(OT[:, :, :].rearrange("p a n -> p (a n)"), 1.0)
            V.memset(LT[L:L + 1, :], 1.0)
            V.memset(WG1[:, R1, :], 0.0)
            V.memset(BG1[:, R1, :], 0.0)
            settle()
            link(V.memset(VA[:, :, :, HD:HD + 1].rearrange("p r x c -> p (r x) c"), 1.0))
            dve.wait_ge(s["small_loaded"], NSMALL)
            V.tensor_copy(IDB[:, :], CST[:, C_ID:C_ID + P])
            V.tensor_copy(MQB[:, :], CST[:, C_MQ:C_MQ + P])
            link(V.tensor_copy(MSB[:, :], CST[:, C_MS:C_MS + 2 * P]))
            dve.wait_ge(s["silu_exp"], 1)
            link(V.tensor_scalar_add(SC2[:, :, :], SC[:, :, :], 1.0))
            link(V.reciprocal(SC[:, :, :], SC2[:, :, :]))
            link(V.tensor_tensor(SC2[:, :, :], CT[:, :, :], SC[:, :, :], ALU.mult))
            V.tensor_copy(SCB[:, :, :, :].rearrange("p l b n -> p (l b) n"),
                          to3(SC2[:, :, :].rearrange("p l b -> p (l b)"), P)).then_inc(s["silu_ready"], 1)
            dve.wait_ge(s["rep_ready"], 1)
            for n in range(2):
                last = V.tensor_tensor(BD[:, n, :, :], to3(CST[:, C_HM:C_HM + H], 5),
                                       PS[:, 2, 5 * n:5 * n + 5].unsqueeze(1).broadcast_to([P, H, 5]), ALU.mult)
            last.then_inc(s["bd_ready"], 1)
            dve.wait_ge(s["w3_ready"], 1)
            V.tensor_copy(W3[:, :], PS[:, 2, 16:176])
            for n in range(2):
                last = V.tensor_tensor(BR[0:1, 384 + 80 * n:464 + 80 * n].rearrange("p (h c) -> p h c", h=H),
                                       PS[0:1, 3, 80 * n:80 * n + 80].rearrange("p (h c) -> p h c", h=H),
                                       BS5[0:1, 5 * n:5 * n + 5].unsqueeze(1).broadcast_to([1, H, 5]), ALU.add)
            last.then_inc(s["w3_copied"], 1)
            dve.wait_ge(s["mod_ready"], 1)
            link(V.tensor_copy(MODC[:, :, :, :].rearrange("p l n b -> p (l n b)"), PS[:, 3, 256:272]))
            for l in range(2):
                last = V.tensor_scalar_add(MODC[:, l, 1:4:2, :], MODC[:, l, 1:4:2, :], 1.0)
            link(last)
            dve.sem_inc(s["mod_final"], 1)

            for l in range(2):
                if l == 0:
                    dve.wait_ge(s["mod_rows_copied"], 1)
                    MR = MODR[:, :, :, :, :].rearrange("p l b k d -> p (l b) k d")
                    SG = SGN[:, :, :, :].rearrange("p l b d -> p (l b) d")
                    for k in (0, 3):
                        link(V.tensor_scalar(SG, MR[:, :, k, :], 0.0, 2.0, ALU.is_ge, ALU.mult))
                        link(V.tensor_scalar(SG, SG, -1.0, None, ALU.add))
                        link(V.tensor_tensor(MR[:, :, k, :], MR[:, :, k, :], SG, ALU.mult))
                        link(V.tensor_scalar(MR[:, :, k, :], MR[:, :, k, :], 0.25, None, ALU.max))
                        link(V.tensor_tensor(MR[:, :, k, :], MR[:, :, k, :], SG, ALU.mult))
                    link(V.tensor_scalar(MR[:, :, 2, :], MR[:, :, 2, :], 1.0, None, ALU.add))
                else:
                    layernorm(s["stats_var1"], (s["stats_std1"], 1), s["xhat_ready1"])
                link(V.memset(KT[64:P, :, :].rearrange("p r n -> p (r n)"), 0.0))
                if l == 0:
                    link(V.memset(KB[0:64, :, :].rearrange("p r n -> p (r n)"), 0.0))
                else:
                    V.memset(QU[:, U:U + LEAD, :, :].rearrange("p u s x -> p (u s x)"), 0.0)
                    link(V.memset(VA[:, :, :, :].rearrange("p r x c -> p (r x) c"), 0.0))
                    link(V.memset(VA[:, :, :, HD:HD + 1].rearrange("p r x c -> p (r x) c"), 1.0))
                dve.sem_inc(s[f"operands_ready{l}"], 1)
                dve.wait_ge(s[f"hT_copied{l}"], G)
                for b in range(B):
                    dve.wait_ge(s[f"proj_copied{l}"], TB * b + TB)
                    us = slice(PAIRS * b, PAIRS * b + PAIRS)
                    if l == 0:
                        w = QU[:, us, 0:2, :].rearrange("p u s x -> p u (s x)").rearrange("p u (x e) -> p u x e", e=HD)
                        lo, hi = w[:, :, :, 0:4], w[:, :, :, 4:8]
                        cos = CST[:, C_COS:C_COS + P].rearrange("p (x e) -> p x e", e=4).unsqueeze(1).broadcast_to([P, PAIRS, 32, 4])
                        sin = CST[:, C_SIN:C_SIN + P].rearrange("p (x e) -> p x e", e=4).unsqueeze(1).broadcast_to([P, PAIRS, 32, 4])
                        t1 = XH[:, us, :].rearrange("p t (x e) -> p t x e", e=4)
                        t2 = HX[:, us, :].rearrange("p t (x e) -> p t x e", e=4)
                        V.tensor_tensor(t1, lo, sin, ALU.mult)
                        link(V.tensor_tensor(t2, hi, sin, ALU.mult))
                        V.tensor_tensor(lo, lo, cos, ALU.mult)
                        link(V.tensor_tensor(hi, hi, cos, ALU.mult))
                        V.tensor_tensor(lo, lo, t2, ALU.subtract)
                        link(V.tensor_tensor(hi, hi, t1, ALU.add))
                    else:
                        a5 = C5[:, us, 0, :].rearrange("p u (x c) -> p u x c", c=5)
                        b5 = C5[:, us, 1, :].rearrange("p u (x c) -> p u x c", c=5)
                        t1 = XH[:, :, :].rearrange("p t d -> p (t d)")[:, 0:PAIRS * 48].rearrange("p (u x c) -> p u x c", u=PAIRS, c=3)
                        t2 = HX[:, us, :].rearrange("p t (x e) -> p t x e", e=HD)
                        cr = CR[:, us, :, :]
                        V.tensor_tensor(t1, a5[:, :, :, 2:5], b5[:, :, :, 1:4], ALU.mult)
                        link(V.tensor_tensor(cr, a5[:, :, :, 1:4], b5[:, :, :, 2:5], ALU.mult))
                        link(V.tensor_tensor(cr, cr, t1, ALU.subtract))
                        kk = QU[:, us, 1, :].rearrange("p u (x e) -> p u x e", e=HD)
                        for c in range(3):
                            link(V.tensor_tensor(t2, cr[:, :, :, c].unsqueeze(3).broadcast_to([P, PAIRS, 16, HD]),
                                                 WQS[:, c, :].unsqueeze(1).unsqueeze(1).broadcast_to([P, PAIRS, 16, HD]), ALU.mult))
                            link(V.tensor_tensor(kk, kk, t2, ALU.add))
                        link(V.tensor_tensor(cr, cr, BQS[:, :].unsqueeze(1).unsqueeze(1).broadcast_to([P, PAIRS, 16, 3]), ALU.mult))
                        link(V.tensor_reduce(SV[:, us, :], cr, AX.X, ALU.add))
                        link(V.tensor_scalar(SV[:, us, :], SV[:, us, :], TEMP[:, 0:1], None, ALU.mult))
                    dve.sem_inc(s[f"operands_ready{l}"], 1)
                if l == 1:
                    link(V.memset(PBF, 1.0))
                dve.sem_inc(s[f"init_done{l}"], 1)
                attention(l)
                residual(l, s[f"o_psum{l}"], s[f"o_added{l}"], 0)

                if l == 0:
                    dve.wait_ge(s["later_loaded"], NLATER)
                    layernorm(s["f_stats"], (s["f_std"], 1), None)
                    modulate(0)
                    squares(slice(0, T))
                    rmsnorm(s["f_stats"], (s["f_std"], 2), s["f_h"])

                    def pair_products(dst, t):
                        q = QF[:, t, 0:P].rearrange("p (h d) -> p h d", h=H).unsqueeze(2).broadcast_to([P, H, H, HD])
                        kk = QF[:, t, P:3 * P].rearrange("p (g e) -> p g e", g=H)[:, :, 0:HD].unsqueeze(1).broadcast_to([P, H, H, HD])
                        return V.tensor_tensor(dst, q, kk, ALU.mult)

                    def value_products(dst, t):
                        pr = SCR[:, t, :, :].unsqueeze(2).broadcast_to([P, H, HD, H])
                        vv = QF[:, t, P:3 * P].rearrange("p (g e) -> p e g", g=H)[:, HD:2 * HD, :].unsqueeze(1).broadcast_to([P, H, HD, H])
                        return V.tensor_tensor(dst.rearrange("p h g d -> p (h g d)").rearrange("p (h d g) -> p h d g", h=H, d=HD), pr, vv, ALU.mult)

                    scr = SCR[:, :, :, :].rearrange("p t h g -> p (t h) g")

                    def head_scores(c):
                        for t in range(TB * c, TB * c + TB):
                            if t in POOL_SCORES:
                                n = POOL_SCORES.index(t)
                                dve.wait_ge(s["f_prod"], n + 1)
                                last = V.tensor_reduce(SCR[:, t, :, :], (PRD[:, 1], PRP)[n % 2], AX.X, ALU.add)
                                last.then_inc(s["f_prod_used"], 1)
                            else:
                                dve.wait_ge(s["f_qkv_copied"], t + 1)
                                link(pair_products(PRD[:, 0, :, :, :], t))
                                link(V.tensor_reduce(SCR[:, t, :, :], PRD[:, 0, :, :, :], AX.X, ALU.add))
                        dve.wait_ge(s["f_prod_used"], sum(t < TB * c + TB for t in POOL_SCORES))
                        hf = slice(TB * H * c, TB * H * c + TB * H)
                        link(V.tensor_reduce(SCM[:, hf], scr[:, hf, :], AX.X, ALU.max))
                        link(V.tensor_tensor(scr[:, hf, :], scr[:, hf, :], to3(SCM[:, hf], H), ALU.subtract))
                        dve.sem_inc(s["f_scmax"], 1)

                    def head_values(c):
                        hf = slice(TB * H * c, TB * H * c + TB * H)
                        dve.wait_ge(s["f_exp"], c + 1)
                        link(V.tensor_reduce(SCL[:, hf], scr[:, hf, :], AX.X, ALU.add))
                        for t in range(TB * c, TB * c + TB):
                            if t in POOL_VALUES:
                                n = POOL_VALUES.index(t) + len(POOL_SCORES)
                                dve.wait_ge(s["f_prod"], n + 1)
                                pb = (PRD[:, 1], PRP)[n % 2].rearrange("p h g d -> p (h g d)").rearrange("p (x g) -> p x g", g=H)
                                V.tensor_reduce(XH[:, t, :], pb, AX.X, ALU.add).then_inc(s["f_prod_used"], 1)
                            else:
                                link(value_products(PRD[:, 0, :, :, :], t))
                                dd = PRD[:, 0].rearrange("p h g d -> p (h g d)").rearrange("p (x g) -> p x g", g=H)
                                link(V.tensor_reduce(XH[:, t, :], dd, AX.X, ALU.add))

                    for c in range(2):
                        head_scores(c)
                    for c in range(2):
                        head_values(c)
                    dve.wait_ge(s["f_prod_used"], len(POOL_SCORES) + len(POOL_VALUES))
                    link(V.reciprocal(SCM[:, :], SCL[:, :]))
                    settle()
                    xo = XH[:, :, :].rearrange("p t (h d) -> p (t h) d", h=H)
                    for g in range(G):
                        x = slice(GT * H * g, GT * H * g + GT * H)
                        V.tensor_tensor(xo[:, x, :], xo[:, x, :], to3(SCM[:, x], HD), ALU.mult).then_inc(s["f_out"], 1)
                    dve.wait_ge(s["f_out"], G)
                    for g in range(G):
                        dve.wait_ge(s["f_o"], g + 1)
                        t = slice(GT * g, GT * g + GT)
                        link(V.tensor_tensor(HX[:, t, :], HX[:, t, :], PS[:, 2 + g % 2, :].rearrange("p (t d) -> p t d", t=GT), ALU.add))
                        dve.sem_inc(s["f_x2"], 1)
                        squares(t)
                    rmsnorm(s["f_stats"], (s["f_std"], 3), s["f_h2"])
                    dve.wait_ge(s["f_gate"], 1)
                    lg = PS[:, 0, 0:T * E0].rearrange("p (t e) -> p t e", e=E0)
                    link(V.tensor_tensor(GW[:, :, :], lg, BG0[:, :].unsqueeze(1).broadcast_to([P, T, E0]), ALU.add))
                    link(V.tensor_reduce(GW2[:, :], GW[:, :, :], AX.X, ALU.max))
                    link(V.tensor_tensor(GW[:, :, :], GW[:, :, :], to3(GW2[:, :], E0), ALU.subtract))
                    dve.sem_inc(s["f_gexp_in"], 1)
                    dve.wait_ge(s["f_gexp"], 1)
                    link(V.tensor_reduce(GW2[:, :], GW[:, :, :], AX.X, ALU.add))
                    link(V.reciprocal(GW3[:, :], GW2[:, :]))
                    link(V.tensor_tensor(GW[:, :, :], GW[:, :, :], to3(GW3[:, :], E0), ALU.mult))
                    for t0 in range(0, T, 2):
                        dve.wait_ge(s["f_y"], t0 + 2)
                        for e in range(E0):
                            for t in (t0, t0 + 1):
                                V.scalar_tensor_tensor(HX[:, t, :], PS[:, (2 + 2 * (t % 4)) % 8 + e // 4, P * (e % 4):P * (e % 4) + P],
                                                       GW[:, t, e:e + 1], HX[:, t, :], ALU.mult, ALU.add).then_inc(s["dve_step"], 1)
                                step_n[0] += 1
                                dve.wait_ge(s["dve_step"], step_n[0] - 1)
                        dve.wait_ge(s["dve_step"], step_n[0])
                        dve.sem_inc(s["f_y_used"], 2)
                    for b in range(B):
                        t = slice(TB * b, TB * b + TB)
                        last = V.tensor_tensor(HX[:, t, :], HX[:, t, :], batch_row(0, b, 3), ALU.mult)
                    link(last)
                    link(V.tensor_tensor(X[:, :, :], X[:, :, :], HX[:, :, :], ALU.add))

            layernorm(s["g_stats"], (s["g_std"], 1), s["g_xh"])
            dve.wait_ge(s["g_high"], 1)
            V.tensor_tensor(W1L[:, :, :].rearrange("p e n -> p (e n)"), W1[:, :, :].rearrange("p e n -> p (e n)"),
                            W1H[:, :, :].rearrange("p e n -> p (e n)").bitcast(F32), ALU.subtract)
            V.tensor_tensor(W2L[:, :, :, :].rearrange("p e f n -> p (e f n)"), W2[:, :, :, :].rearrange("p e f n -> p (e f n)"),
                            W2H[:, :, :, :].rearrange("p e f n -> p (e f n)").bitcast(F32), ALU.subtract).then_inc(s["g_split"], 1)
            dve.sem_inc(s["g_cwb"], 1)
            dve.sem_inc(s["g_lo"], 4)
            dve.sem_inc(s["g_y"], 2)
            dve.sem_inc(s["g_y_read"], 2)
            dve.sem_inc(s["g_acc"], 2)
            cnt = [0]

            def glink(ins, base):
                cnt[0] += 1
                ins.then_inc(s["g_step"], 1)
                dve.wait_ge(s["g_step"], base + cnt[0])

            def gate(r, base):
                V.tensor_copy(WGC[:, :], WG1[:, r, :]).then_inc(s["g_wg"], 1)
                glink(V.tensor_copy(ST1[:, 0:E1], BG1[:, r, :]), base)

            def choose(x, g, base):
                t = slice(GT * g, GT * g + GT)
                lw, th = GW[:, t, 0:E1], GW[:, t, E1:2 * E1]
                tie = CST[:, C_TIE:C_TIE + 16].rearrange("p (e f) -> p e f", e=E1).unsqueeze(1).broadcast_to([P, GT, E1, E1])
                dve.wait_ge(s["g_lg"], x + 1)
                glink(V.tensor_tensor(lw, PS[:, 1, 0:GT * E1].rearrange("p (t e) -> p t e", e=E1),
                                      ST1[:, 0:E1].unsqueeze(1).broadcast_to([P, GT, E1]), ALU.add), base)
                mine = lw.unsqueeze(3).broadcast_to([P, GT, E1, E1])
                other = lw.unsqueeze(2).broadcast_to([P, GT, E1, E1])
                V.tensor_tensor(CMP[:, :, :, :], other, mine, ALU.is_gt)
                glink(V.tensor_tensor(CEQ[:, :, :, :], other, mine, ALU.is_equal), base)
                glink(V.tensor_tensor(CEQ[:, :, :, :], CEQ[:, :, :, :], tie, ALU.mult), base)
                glink(V.tensor_tensor(CMP[:, :, :, :], CMP[:, :, :, :], CEQ[:, :, :, :], ALU.add), base)
                glink(V.tensor_reduce(th, CMP[:, :, :, :], AX.X, ALU.add), base)
                glink(V.tensor_scalar(SELE[:, :, :], th, 1.5, None, ALU.is_lt), base)
                glink(V.tensor_tensor(SELL[:, :, :], SELE[:, :, :], lw, ALU.mult), base)
                glink(V.tensor_reduce(GW2[:, 0:GT], SELL[:, :, :], AX.X, ALU.add), base)
                glink(V.tensor_scalar(GW2[:, 0:GT], GW2[:, 0:GT], 0.5, None, ALU.mult), base)
                glink(V.tensor_tensor(th, lw, to3(GW2[:, 0:GT], E1), ALU.subtract), base)
                dve.sem_inc(s["g_tanh_in"], 1)

            def chosen_weights(x, g, base):
                t = slice(GT * g, GT * g + GT)
                lw, th = GW[:, t, 0:E1], GW[:, t, E1:2 * E1]
                dve.wait_ge(s["g_tanh"], x + 1)
                glink(V.tensor_scalar(th, th, 0.5, 0.5, ALU.mult, ALU.add), base)
                glink(V.tensor_tensor(lw, th, SELE[:, :, :], ALU.mult), base)
                glink(V.tensor_copy(GWS[:, :, 0:E1], lw), base)
                V.tensor_tensor(GWS[:, :, E1:2 * E1], lw, GWS[:, :, 0:E1].bitcast(F32), ALU.subtract).then_inc(s["g_cw"], 1)

            def rows_of_weights(x):
                dve.wait_ge(s["g_cwp"], x + 1)
                V.tensor_copy(CWT[:, :], PS[0:2 * E1, 0, :]).then_inc(s["g_cwr"], 1)

            def lows(x, e):
                for f in range(FC):
                    n = FC * e + f
                    dve.wait_ge(s["g_gelu"], x * 16 + n + 5)
                    V.tensor_tensor(HML[:, n % (2 * FC), :], HMF[:, f, :], HMH[:, n % (2 * FC), :].bitcast(F32), ALU.subtract)\
                        .then_inc(s["g_lo"], 1)

            def spread(x, e):
                dve.wait_ge(s["g_cwT"], x * E1 + e + 1)
                dve.wait_ge(s["g_y_read"], x * E1 + e + 1)
                V.tensor_copy(CWB[:, e % 2, :], PS[:, int(e == 1), :]).then_inc(s["g_cwb"], 1)

            def weigh(x, e):
                dve.wait_ge(s["g_y"], x * E1 + e + 3)
                dve.wait_ge(s["g_cwb"], x * E1 + e + 2)
                dve.wait_ge(s["g_acc"], x * E1 + e + 1)
                V.scalar_tensor_tensor(YS[:, e % 2, :], PS[:, 6 + e % 2, :], B2C[:, e:e + 1], CWB[:, e % 2, :], ALU.add, ALU.mult)\
                    .then_inc(s["g_y_read"], 1)

            V.tensor_tensor(SLW[:, :, :], to3(IDF[0:2 * E1, 0:E1], P), to3(IDF[0:2 * E1, E1:2 * E1], P), ALU.add)
            gate(0, 0)
            choose(0, 0, 0)
            lows(0, 0)
            ahead = cnt[0]
            with dve.Fori(0, R1) as r:
                cnt[0] = 0
                base = r * (1 + G * 13) + ahead
                for g in range(G):
                    x = r * G + g
                    chosen_weights(x, g, base)
                    lows(x, 1)
                    rows_of_weights(x)
                    lows(x, 2)
                    spread(x, 0)
                    weigh(x, 0)
                    spread(x, 1)
                    weigh(x, 1)
                    lows(x, 3)
                    spread(x, 2)
                    weigh(x, 2)
                    if g == G - 1:
                        gate(r + 1, base)
                    choose(x + 1, (g + 1) % G, base)
                    lows(x + 1, 0)
                    spread(x, 3)
                    weigh(x, 3)
                assert cnt[0] == 1 + G * 13, cnt[0]
            for g in range(G):
                dve.wait_ge(s["g_last"], g + 1)
                t = slice(GT * g, GT * g + GT)
                link(V.tensor_tensor(XH[:, t, :], PS[:, 2 + g % 2, :].rearrange("p (t d) -> p t d", t=GT),
                                     MODR[:, 1, GT * g // TB, 3, :].unsqueeze(1).broadcast_to([P, GT, D]), ALU.mult))
                dve.sem_inc(s["g_last_added"], 1)
                V.tensor_tensor(X[:, t, :], X[:, t, :], XH[:, t, :], ALU.add).then_inc(s["g_fin"], 1)

        @block.gpsimd
        def _(pool):
            Q = nc.gpsimd
            pn = [0]

            def plink(ins):
                pn[0] += 1
                ins.then_inc(s["pool_init"], 1)
                pool.wait_ge(s["pool_init"], pn[0])
            Q.memset(QA[:, :, :, :].rearrange("p r x c -> p (r x c)"), 0.0)
            plink(Q.memset(KA[:, :, :, :].rearrange("p r x c -> p (r x c)"), 0.0))
            Q.memset(QA[:, :, :, 48:ROWS].rearrange("p r x c -> p (r x) c"), 1.0)
            plink(Q.memset(KA[:, :, :, ROWS:ROWSM].rearrange("p r x c -> p (r x) c"), 1.0))

            for l in range(2):
                per = [0]

                def pwait(sm, value):
                    pool.wait_ge(sm, value)
                    pool.sem_inc(s["pool_passed"], 1)

                def split(src, dst, at, base):
                    w = src.shape[2]
                    rest = RQ[:, :, 0:w]
                    cur = src
                    for n in range(3):
                        part = dst[:, :, at[n]:at[n] + w]
                        plinku(Q.tensor_copy(part, cur), base)
                        if n < 2:
                            plinku(Q.tensor_tensor(rest, cur, part, ALU.subtract), base)
                            cur = rest

                def plinku(ins, base):
                    per[0] += 1
                    ins.then_inc(s[f"pool_step{l}"], 1)
                    pwait(s[f"pool_step{l}"], base + per[0])

                def build_k(u, r, base):
                    kk = QU[:, u, 1, :].rearrange("p (x e) -> p x e", e=HD)
                    dst = KA[:, r, :, :]
                    split(kk, dst, (0, HD, 2 * HD), base)
                    Q.tensor_copy(dst[:, :, 3 * HD:5 * HD], dst[:, :, 0:2 * HD])
                    if l == 1:
                        plinku(Q.tensor_copy(dst[:, :, 5 * HD:6 * HD], dst[:, :, 0:HD]), base)
                        split(SV[:, u, :].unsqueeze(2), dst, (48, 49, 50), base)
                        Q.tensor_copy(RM[:, 0:1], RM[:, 1:2]).then_inc(s[f"k_built{l}"], 1)
                    else:
                        Q.tensor_copy(dst[:, :, 5 * HD:6 * HD], dst[:, :, 0:HD]).then_inc(s[f"k_built{l}"], 1)

                def build_qv(u, r, base):
                    qq = QU[:, u, 0, :].rearrange("p (x e) -> p x e", e=HD)
                    dst = QA[:, r, :, :]
                    split(qq, dst, (0, 3 * HD, 5 * HD), base)
                    Q.memset(dst[:, :, ROWS:ROWSM], 0.0)
                    Q.tensor_copy(dst[:, :, HD:2 * HD], dst[:, :, 0:HD])
                    Q.tensor_copy(dst[:, :, 2 * HD:3 * HD], dst[:, :, 0:HD])
                    Q.tensor_copy(dst[:, :, 4 * HD:5 * HD], dst[:, :, 3 * HD:4 * HD])
                    Q.tensor_copy(VA[:, r, :, 0:HD], QU[:, u, 2, :].rearrange("p (x e) -> p x e", e=HD))\
                        .then_inc(s[f"qv_built{l}"], 1)

                def build_m(u, r, base):
                    pwait(s[f"nm_ready{l}"], u + 1)
                    split(NM[:, r, :].unsqueeze(2), QA[:, r, :, :], (51, 52, 53), base)
                    Q.tensor_copy(RM[:, 0:1], RM[:, 1:2]).then_inc(s[f"mparts_built{l}"], 1)

                plink(Q.memset(RM[:, :], 0.0))
                pool.wait_ge(s[f"operands_ready{l}"], 2 - l)
                pool.wait_ge(s[f"proj_copied{l}"], TB)
                if l == 0:
                    for v in range(LEAD):
                        build_k(v, v, 0)
                        build_qv(v, v, 0)
                else:
                    for v in range(LEAD):
                        build_qv(v, v, 0)
                    pool.wait_ge(s["operands_ready1"], 2)
                    for v in range(LEAD):
                        build_k(v, v, 0)
                pool.wait_ge(s[f"operands_ready{l}"], 3)
                pool.wait_ge(s[f"proj_copied{l}"], T)
                build_m(0, 0, 0)
                start = per[0]
                one = (5 + (6 if l == 1 else 0)) + 5 + 5

                def step(u, r, base):
                    per[0] = 0
                    build_m(u + 1, (r + 1) % RING, base)
                    pwait(s[f"qmT_psum{l}"], u + 1)
                    build_k(u + LEAD, (r + LEAD) % RING, base)
                    pwait(s[f"pv_done{l}"], u * (len(sched[l][0]) // 2) + 2)
                    build_qv(u + LEAD, (r + LEAD) % RING, base)
                    assert per[0] == one, per[0]

                with pool.Fori(0, U // RING) as it:
                    for r in range(RING):
                        u = it * RING + r
                        step(u, r, u * one + start)
                if l == 0:
                    pool.wait_ge(s["f_qkv_copied"], POOL_SCORES[0] + 1)
                    pool.wait_ge(s["att_ready0"], U + 1)
                    for n, t in enumerate(POOL_SCORES + POOL_VALUES):
                        dst = (PRD[:, 1], PRP)[n % 2]
                        if n == 1:
                            pool.wait_ge(s["f_qkv_copied"], T)
                        if n >= 2:
                            pool.wait_ge(s["f_prod_used"], n - 1)
                        if n < len(POOL_SCORES):
                            q = QF[:, t, 0:P].rearrange("p (h d) -> p h d", h=H).unsqueeze(2).broadcast_to([P, H, H, HD])
                            kk = QF[:, t, P:3 * P].rearrange("p (g e) -> p g e", g=H)[:, :, 0:HD].unsqueeze(1).broadcast_to([P, H, H, HD])
                            Q.tensor_tensor(dst, q, kk, ALU.mult).then_inc(s["f_prod"], 1)
                        else:
                            pool.wait_ge(s["f_exp"], 2 if t >= TB else 1)
                            pr = SCR[:, t, :, :].unsqueeze(2).broadcast_to([P, H, HD, H])
                            vv = QF[:, t, P:3 * P].rearrange("p (g e) -> p e g", g=H)[:, HD:2 * HD, :].unsqueeze(1).broadcast_to([P, H, HD, H])
                            Q.tensor_tensor(dst.rearrange("p h g d -> p (h g d)").rearrange("p (h d g) -> p h d g", h=H, d=HD),
                                            pr, vv, ALU.mult).then_inc(s["f_prod"], 1)

            def parts(g):
                tok = slice(512 * g, 512 * g + 512)
                Q.tensor_copy(CTH[:, tok], hT[:, tok]).then_inc(s["g_pstep"], 1)
                return tok

            for g in range(G):
                pool.wait_ge(s["g_hT_copied"], g + 1)
                tok = parts(g)
                pool.wait_ge(s["g_pstep"], g + 1)
                Q.tensor_tensor(CTL[:, tok], hT[:, tok], CTH[:, tok].bitcast(F32), ALU.subtract).then_inc(s["g_cur"], 1)
            with pool.Fori(0, R1) as r:
                for g in range(G):
                    x = r * G + g
                    tok = slice(512 * g, 512 * g + 512)
                    for e in range(E1):
                        pool.wait_ge(s["g_y_read"], x * E1 + e + 3)
                        pool.wait_ge(s["g_acc"], x * E1 + e + 2)
                        Q.tensor_tensor(hT[:, tok], hT[:, tok], YS[:, e % 2, :], ALU.add).then_inc(s["g_acc"], 1)
                    pool.wait_ge(s["g_acc"], x * E1 + 6)
                    pool.sem_inc(s["pool_passed"], 1)
                    parts(g)
                    pool.wait_ge(s["g_pstep"], x + G + 1)
                    Q.tensor_tensor(CTL[:, tok], hT[:, tok], CTH[:, tok].bitcast(F32), ALU.subtract).then_inc(s["g_cur"], 1)


_INS = ['L0_attn_x', 'L0_attn_Wq', 'L0_attn_Wk', 'L0_attn_Wv', 'L0_attn_Wo', 'L0_ffn_gamma1', 'L0_ffn_Wq', 'L0_ffn_bq',
        'L0_ffn_Wdown', 'L0_ffn_bdown', 'L0_ffn_Wup', 'L0_ffn_bup', 'L0_ffn_Wo', 'L0_ffn_bo', 'L0_ffn_gamma2', 'L0_ffn_Wg',
        'L0_ffn_bg', 'L0_ffn_We', 'L0_c', 'L0_wmod', 'L1_attn_Wq', 'L1_attn_bq', 'L1_attn_Wk', 'L1_attn_bk', 'L1_attn_Wv',
        'L1_attn_bv', 'L1_attn_Wo', 'L1_attn_bo', 'L1_attn_Wqs', 'L1_attn_bqs', 'L1_attn_Wks', 'L1_attn_bks', 'L1_attn_Wvs',
        'L1_attn_bvs', 'L1_attn_temp', 'L1_ffn_Wg', 'L1_ffn_bg', 'L1_ffn_W1', 'L1_ffn_b1', 'L1_ffn_W2', 'L1_ffn_b2', 'L1_c',
        'L1_wmod']


def constants():
    c = np.zeros((P, C_END), np.float32)
    c[:, C_ID:C_ID + P] = np.eye(P)
    c[:, C_MQ:C_MQ + P] = -BIG * np.triu(np.ones((P, P)), 1)
    c[:, C_MS:C_MS + P] = -BIG
    c[:, C_MS + P:C_MS + 2 * P] = -BIG * np.tril(np.ones((P, P)), -1)
    p = np.arange(P)
    c[p, C_HM + p // HD] = 1.0
    for a in range(2):
        for e in range(2):
            for d in range(HD):
                c[32 * (2 * a + e) + d, C_SEL + HD * a + d] = 1.0
            c[32 * (2 * a + e) + HD, C_SEL + 2 * HD + a] = 1.0
    c[p % HD, C_REP + p] = 1.0
    for e in range(E1):
        c[:, C_TIE + E1 * e:C_TIE + E1 * e + e] = 1.0
    inv = (1.0 / np.float32(10000.0) ** (np.arange(0, HD, 2, dtype=np.float32) / np.float32(HD))).astype(np.float32)
    ang = np.outer(np.arange(S, dtype=np.float32), inv).astype(np.float32)
    for at, fn in ((C_COS, np.cos), (C_SIN, np.sin)):
        v = fn(ang).astype(np.float32).reshape(TB, P, 1, 4).transpose(1, 0, 2, 3)
        v = np.broadcast_to(v[:, None], (P, 2, TB, 2, 4))
        c[:, at:at + P] = v.reshape(P, P)
    return c


def kernel(**inputs):
    import numpy as _np
    import concourse.bacc as _bacc
    from concourse import mybir as _mybir
    from concourse.bass_utils import run_bass_kernel_spmd as _run

    nc = _bacc.Bacc("TRN2", target_bir_lowering=False, num_devices=1)
    arrays, io = {}, {}
    for name in _INS:
        a = _np.ascontiguousarray(inputs[name])
        if a.ndim == 0:
            a = a.reshape(1)
        arrays[f"in_{name}"] = a
        io[name] = nc.dram_tensor(f"in_{name}", a.shape, _mybir.dt.from_np(a.dtype), kind="ExternalInput").ap()
    arrays["in_consts"] = constants()
    io["consts"] = nc.dram_tensor("in_consts", (P, C_END), F32, kind="ExternalInput").ap()
    out = nc.dram_tensor("out_x", (B, S, D), F32, kind="ExternalOutput").ap()
    build(nc, io, out)
    r = _run(nc, [arrays], core_ids=[0])
    return r.results[0]["out_x"]
```
